# Optimizing a Trainium2 kernel written in Bass

```python
import numpy as np
import jax
import jax.numpy as jnp

def _softmax(x, axis=-1):
    return jax.nn.softmax(x, axis=axis)

def _gelu(x):
    return jax.nn.gelu(x, approximate=True)

def _silu(x):
    return jax.nn.silu(x)

def _sigmoid(x):
    return jax.nn.sigmoid(x)

def _layernorm(x, axis=-1, eps=1e-05):
    m = jnp.mean(x, axis=axis, keepdims=True)
    v = jnp.var(x, axis=axis, keepdims=True)
    return (x - m) / jnp.sqrt(v + eps)

def _scatter_add(tgt, idx, src, axis=0):
    return tgt.at[idx].add(src)

def _segment_sum(src, seg, n):
    return jax.ops.segment_sum(src, seg, n)
kernel_name = 'mk_flamingo_gated_d4_seqx_r8_bd17b5'

def setup_inputs(seed: int=0):
    np.random.seed(seed)
    _w = jnp.asarray

    def _rec_inputs():
        import jax
        import jax.numpy as jnp
        _rk = jax.random.key(seed)
        x = -0.0003929 + 0.9999 * jax.random.normal(jax.random.fold_in(_rk, 1), (32, 128, 128), jnp.float32)
        _lenS = 128 - jax.random.randint(jax.random.fold_in(_rk, 7), (32,), 0, max(1, 128 // 4) + 1, jnp.int32)
        _lenS2 = 77 - jax.random.randint(jax.random.fold_in(_rk, 8), (32,), 0, max(1, 77 // 4) + 1, jnp.int32)
        _ctx_1024P = jax.random.normal(jax.random.fold_in(_rk, 11), (32, 16, 128), jnp.float32)
        _ctx_1024c = jax.random.dirichlet(jax.random.fold_in(_rk, 511), 0.3 * jnp.ones((16,), jnp.float32), (32, 77))
        _ctx_1024t = jnp.einsum('bsk,bkd->bsd', _ctx_1024c, _ctx_1024P)
        _ctx_1024t = _ctx_1024t * jax.lax.rsqrt(jnp.mean(jnp.square(_ctx_1024t)) + 1e-12) * 0.953939
        ctx_1024 = 2.81802e-05 + 1.00001 * (_ctx_1024t + 0.3 * jax.random.normal(jax.random.fold_in(_rk, 611), (32, 77, 128), jnp.float32))
        _validS = jnp.arange(128)[None, :] < _lenS[:, None]
        _validS2 = jnp.arange(77)[None, :] < _lenS2[:, None]
        _causal = jnp.tril(jnp.ones((128, 128), dtype=bool))
        mask_BxSxS2_if1 = jnp.where(jnp.ones((32, 128, 77), dtype=bool), 1, 0).astype(jnp.int32)
        _g = jax.random.normal(jax.random.fold_in(_rk, 9001), (2, 4), jnp.float32)
        _g = jnp.sign(_g) * jnp.maximum(jnp.abs(_g), 1.0) + (_g == 0) * 1.0
        g_xattn = _g[0]
        g_ffn = _g[1]
        return (x, ctx_1024, mask_BxSxS2_if1, g_xattn, g_ffn)
    x, ctx_1024, mask_BxSxS2_if1, g_xattn, g_ffn = _rec_inputs()

    def _L0_xattn_setup():
        import jax, jax.numpy as jnp
        import numpy as np
        D1, D2, D3 = (128, 128, 128)
        key = jax.random.key(seed)
        k1, k2, kw, kb = jax.random.split(key, 4)
        x1 = jax.random.normal(k1, (8, 256, D1), dtype=jnp.float32)
        x2 = jax.random.normal(k2, (8, 256, D2), dtype=jnp.float32)
        bound = 1.0 / np.sqrt(D1 + D2)
        W = jax.random.uniform(kw, (D3, D1 + D2), minval=-bound, maxval=bound, dtype=jnp.float32)
        b = jax.random.uniform(kb, (D3,), minval=-bound, maxval=bound, dtype=jnp.float32)
        return {'x1': x1, 'x2': x2, 'W': W, 'b': b}
    _L0_xattn_all = _L0_xattn_setup()
    _L0_xattn_in = {k: v for k, v in _L0_xattn_all.items() if k in ('W', 'b')}
    del _L0_xattn_all

    def _L0_ffn_setup():
        import jax, jax.numpy as jnp
        import numpy as np
        BLOCK = 32
        W_BITS = 4
        ACT_BITS = 16

        def act_qdq(x):
            qmax = 2.0 ** (ACT_BITS - 1) - 1.0
            scale = jnp.maximum(jnp.max(jnp.abs(x)) / qmax, 1e-12)
            return jnp.clip(jnp.round(x / scale), -qmax - 1.0, qmax) * scale

        def fixed_qdq_u16(x):
            scale = 1.0 / 65536.0
            return jnp.clip(jnp.round(x / scale), 0.0, 65535.0) * scale

        def lpbq_dequant(w):
            O, I = w.shape
            qmax = 2.0 ** (W_BITS - 1) - 1.0
            wb = w.reshape(O, I // BLOCK, BLOCK)
            s = jnp.maximum(jnp.max(jnp.abs(wb), axis=-1, keepdims=True) / qmax, 1e-12)
            wq = jnp.clip(jnp.round(wb / s), -qmax - 1.0, qmax) * s
            return wq.reshape(O, I)
        key = jax.random.key(seed)
        k1, k2, k3, k4 = jax.random.split(key, 4)
        B, S, H, I = (2, 512, 128, 384)
        x = jax.random.normal(k1, (B, S, H), jnp.float32)
        w_gate = jax.random.normal(k2, (I, H), jnp.float32) * 0.02
        w_up = jax.random.normal(k3, (I, H), jnp.float32) * 0.02
        w_down = jax.random.normal(k4, (H, I), jnp.float32) * 0.02
        return {'x': x, 'w_gate': w_gate, 'w_up': w_up, 'w_down': w_down}
    _L0_ffn_all = _L0_ffn_setup()
    _L0_ffn_in = {k: v for k, v in _L0_ffn_all.items() if k in ('w_gate', 'w_up', 'w_down')}
    del _L0_ffn_all

    def _L1_xattn_setup():
        import jax, jax.numpy as jnp
        import numpy as np
        EMBED_DIM = 128
        NUM_HEADS = 16
        HEAD_DIM = EMBED_DIM // NUM_HEADS
        B, T, S = (2, 256, 256)
        key = jax.random.key(seed)
        ks = jax.random.split(key, 5)
        scale_w = 1.0 / np.sqrt(EMBED_DIM)
        return {'q': jax.random.normal(ks[0], (B, T, EMBED_DIM), dtype=jnp.float32), 'k': jax.random.normal(ks[1], (B, S, EMBED_DIM), dtype=jnp.float32), 'v': jax.random.normal(ks[2], (B, S, EMBED_DIM), dtype=jnp.float32), 'in_proj_weight': jax.random.normal(ks[3], (3 * EMBED_DIM, EMBED_DIM), dtype=jnp.float32) * scale_w, 'in_proj_bias': jnp.zeros((3 * EMBED_DIM,), dtype=jnp.float32), 'out_w': jax.random.normal(ks[4], (EMBED_DIM, EMBED_DIM), dtype=jnp.float32) * scale_w, 'out_b': jnp.zeros((EMBED_DIM,), dtype=jnp.float32)}
    _L1_xattn_all = _L1_xattn_setup()
    _L1_xattn_in = {k: v for k, v in _L1_xattn_all.items() if k in ('in_proj_weight', 'in_proj_bias', 'out_w', 'out_b')}
    del _L1_xattn_all

    def _L1_ffn_setup():
        import jax, jax.numpy as jnp
        import numpy as np
        EPS = 1e-12

        def _l2norm(v):
            n = jnp.sqrt(jnp.sum(v * v, axis=-1, keepdims=True))
            return v / jnp.maximum(n, EPS)
        key = jax.random.key(seed)
        ks = jax.random.split(key, 6)
        B, S, D, F, E = (2, 256, 128, 512, 8)
        std = 0.02
        return {'x': jax.random.normal(ks[0], (B, S, D), jnp.float32), 'Wp': jax.random.normal(ks[1], (D, D), jnp.float32) * (1.0 / np.sqrt(D)), 'sim_matrix': jax.random.normal(ks[2], (E, D), jnp.float32) * std, 'temperature': jnp.asarray(1.0, jnp.float32), 'W1': jax.random.normal(ks[3], (E, D, F), jnp.float32) * (1.0 / np.sqrt(D)), 'b1': jnp.zeros((E, F), jnp.float32), 'W2': jax.random.normal(ks[4], (E, F, D), jnp.float32) * (1.0 / np.sqrt(F)), 'b2': jnp.zeros((E, D), jnp.float32)}
    _L1_ffn_all = _L1_ffn_setup()
    _L1_ffn_in = {k: v for k, v in _L1_ffn_all.items() if k in ('Wp', 'sim_matrix', 'temperature', 'W1', 'b1', 'W2', 'b2')}
    del _L1_ffn_all

    def _L2_xattn_setup():
        import jax, jax.numpy as jnp
        import numpy as np
        HEADS = 16
        EPS = 1e-06

        def _rmsnorm(x, gamma):
            inv = jax.lax.rsqrt(jnp.mean(x * x, axis=-1, keepdims=True) + EPS)
            return x * inv * gamma
        key = jax.random.key(seed)
        ks = jax.random.split(key, 7)
        B, L, Lc, D, CTX = (4, 512, 128, 128, 128)
        hd = D // HEADS
        s = 1.0 / np.sqrt(D)
        return {'x': jax.random.normal(ks[0], (B, L, D), jnp.float32), 'ctx': jax.random.normal(ks[1], (B, Lc, CTX), jnp.float32), 'Wq': jax.random.normal(ks[2], (D, D), jnp.float32) * s, 'Wkv': jax.random.normal(ks[3], (CTX, 2 * D), jnp.float32) * s, 'Wproj': jax.random.normal(ks[4], (D, D), jnp.float32) * s, 'q_gamma': jnp.ones((hd,), jnp.float32), 'k_gamma': jnp.ones((hd,), jnp.float32)}
    _L2_xattn_all = _L2_xattn_setup()
    _L2_xattn_in = {k: v for k, v in _L2_xattn_all.items() if k in ('Wq', 'Wkv', 'Wproj', 'q_gamma', 'k_gamma')}
    del _L2_xattn_all

    def _L2_ffn_setup():
        import jax, jax.numpy as jnp
        import numpy as np
        B, S, D_MODEL, D_FF = (4, 256, 128, 512)

        def _quantum_transform(hidden, theta, w_real, w_imag):
            imag = w_imag * jnp.sin(theta + hidden * 0.1)
            quantum_phase = jnp.cos(theta) * w_real + jnp.sin(theta) * w_imag
            return hidden + quantum_phase * imag * 0.1
        key = jax.random.key(seed)
        ks = jax.random.split(key, 8)
        return {'x': jax.random.normal(ks[0], (B, S, D_MODEL), dtype=jnp.float32), 'W1': jax.random.normal(ks[1], (D_MODEL, D_FF), dtype=jnp.float32) * (1.0 / np.sqrt(D_MODEL)), 'b1': jnp.zeros((D_FF,), dtype=jnp.float32), 'quantum_phases': jax.random.normal(ks[2], (D_FF,), dtype=jnp.float32) * (2.0 * np.pi), 'quantum_weights_real': jax.random.normal(ks[3], (D_FF,), dtype=jnp.float32) * 0.1, 'quantum_weights_imag': jax.random.normal(ks[4], (D_FF,), dtype=jnp.float32) * 0.1, 'W2': jax.random.normal(ks[5], (D_FF, D_MODEL), dtype=jnp.float32) * (1.0 / np.sqrt(D_FF)), 'b2': jnp.zeros((D_MODEL,), dtype=jnp.float32)}
    _L2_ffn_all = _L2_ffn_setup()
    _L2_ffn_in = {k: v for k, v in _L2_ffn_all.items() if k in ('W1', 'b1', 'quantum_phases', 'quantum_weights_real', 'quantum_weights_imag', 'W2', 'b2')}
    del _L2_ffn_all

    def _L3_xattn_setup():
        import jax, jax.numpy as jnp
        import numpy as np
        H = 16
        key = jax.random.key(seed)
        ks = jax.random.split(key, 8)
        B, T, D = (4, 256, 128)
        s = 0.02
        return {'query': jax.random.normal(ks[0], (B, T, D), jnp.float32), 'key': jax.random.normal(ks[1], (B, T, D), jnp.float32), 'value': jax.random.normal(ks[2], (B, T, D), jnp.float32), 'mask': jnp.ones((B, T, T), jnp.int32), 'Wq': jax.random.normal(ks[3], (D, D), jnp.float32) * s, 'Wk': jax.random.normal(ks[4], (D, D), jnp.float32) * s, 'Wv': jax.random.normal(ks[5], (D, D), jnp.float32) * s, 'Wo': jax.random.normal(ks[6], (D, D), jnp.float32) * s, 'bo': jnp.zeros((D,), jnp.float32)}
    _L3_xattn_all = _L3_xattn_setup()
    _L3_xattn_in = {k: v for k, v in _L3_xattn_all.items() if k in ('Wq', 'Wk', 'Wv', 'Wo', 'bo')}
    del _L3_xattn_all

    def _L3_ffn_setup():
        import jax, jax.numpy as jnp
        import numpy as np
        E = 16
        F_C = 2.0
        D = 128
        I = 4 * D
        IS = 2 * D
        B, S = (4, 128)
        key = jax.random.key(seed)
        ks = jax.random.split(key, 8)
        w = 0.02
        return {'hidden_states': jax.random.normal(ks[0], (B, S, D), dtype=jnp.float32), 'gate_w': jax.random.normal(ks[1], (E, D), dtype=jnp.float32) * w, 'Wg': jax.random.normal(ks[2], (E, I, D), dtype=jnp.float32) * w, 'Wu': jax.random.normal(ks[3], (E, I, D), dtype=jnp.float32) * w, 'Wd': jax.random.normal(ks[4], (E, D, I), dtype=jnp.float32) * w, 'Sg': jax.random.normal(ks[5], (IS, D), dtype=jnp.float32) * w, 'Su': jax.random.normal(ks[6], (IS, D), dtype=jnp.float32) * w, 'Sd': jax.random.normal(ks[7], (D, IS), dtype=jnp.float32) * w}
    _L3_ffn_all = _L3_ffn_setup()
    _L3_ffn_in = {k: v for k, v in _L3_ffn_all.items() if k in ('gate_w', 'Wg', 'Wu', 'Wd', 'Sg', 'Su', 'Sd')}
    del _L3_ffn_all
    return {'x': x, 'ctx_1024': ctx_1024, 'mask_BxSxS2_if1': mask_BxSxS2_if1, 'g_xattn': g_xattn, 'g_ffn': g_ffn, 'L0_xattn_W': _L0_xattn_in['W'], 'L0_xattn_b': _L0_xattn_in['b'], 'L0_ffn_w_gate': _L0_ffn_in['w_gate'], 'L0_ffn_w_up': _L0_ffn_in['w_up'], 'L0_ffn_w_down': _L0_ffn_in['w_down'], 'L1_xattn_in_proj_weight': _L1_xattn_in['in_proj_weight'], 'L1_xattn_in_proj_bias': _L1_xattn_in['in_proj_bias'], 'L1_xattn_out_w': _L1_xattn_in['out_w'], 'L1_xattn_out_b': _L1_xattn_in['out_b'], 'L1_ffn_Wp': _L1_ffn_in['Wp'], 'L1_ffn_sim_matrix': _L1_ffn_in['sim_matrix'], 'L1_ffn_temperature': _L1_ffn_in['temperature'], 'L1_ffn_W1': _L1_ffn_in['W1'], 'L1_ffn_b1': _L1_ffn_in['b1'], 'L1_ffn_W2': _L1_ffn_in['W2'], 'L1_ffn_b2': _L1_ffn_in['b2'], 'L2_xattn_Wq': _L2_xattn_in['Wq'], 'L2_xattn_Wkv': _L2_xattn_in['Wkv'], 'L2_xattn_Wproj': _L2_xattn_in['Wproj'], 'L2_xattn_q_gamma': _L2_xattn_in['q_gamma'], 'L2_xattn_k_gamma': _L2_xattn_in['k_gamma'], 'L2_ffn_W1': _L2_ffn_in['W1'], 'L2_ffn_b1': _L2_ffn_in['b1'], 'L2_ffn_quantum_phases': _L2_ffn_in['quantum_phases'], 'L2_ffn_quantum_weights_real': _L2_ffn_in['quantum_weights_real'], 'L2_ffn_quantum_weights_imag': _L2_ffn_in['quantum_weights_imag'], 'L2_ffn_W2': _L2_ffn_in['W2'], 'L2_ffn_b2': _L2_ffn_in['b2'], 'L3_xattn_Wq': _L3_xattn_in['Wq'], 'L3_xattn_Wk': _L3_xattn_in['Wk'], 'L3_xattn_Wv': _L3_xattn_in['Wv'], 'L3_xattn_Wo': _L3_xattn_in['Wo'], 'L3_xattn_bo': _L3_xattn_in['bo'], 'L3_ffn_gate_w': _L3_ffn_in['gate_w'], 'L3_ffn_Wg': _L3_ffn_in['Wg'], 'L3_ffn_Wu': _L3_ffn_in['Wu'], 'L3_ffn_Wd': _L3_ffn_in['Wd'], 'L3_ffn_Sg': _L3_ffn_in['Sg'], 'L3_ffn_Su': _L3_ffn_in['Su'], 'L3_ffn_Sd': _L3_ffn_in['Sd']}

def reference(x, ctx_1024, mask_BxSxS2_if1, g_xattn, g_ffn, L0_xattn_W, L0_xattn_b, L0_ffn_w_gate, L0_ffn_w_up, L0_ffn_w_down, L1_xattn_in_proj_weight, L1_xattn_in_proj_bias, L1_xattn_out_w, L1_xattn_out_b, L1_ffn_Wp, L1_ffn_sim_matrix, L1_ffn_temperature, L1_ffn_W1, L1_ffn_b1, L1_ffn_W2, L1_ffn_b2, L2_xattn_Wq, L2_xattn_Wkv, L2_xattn_Wproj, L2_xattn_q_gamma, L2_xattn_k_gamma, L2_ffn_W1, L2_ffn_b1, L2_ffn_quantum_phases, L2_ffn_quantum_weights_real, L2_ffn_quantum_weights_imag, L2_ffn_W2, L2_ffn_b2, L3_xattn_Wq, L3_xattn_Wk, L3_xattn_Wv, L3_xattn_Wo, L3_xattn_bo, L3_ffn_gate_w, L3_ffn_Wg, L3_ffn_Wu, L3_ffn_Wd, L3_ffn_Sg, L3_ffn_Su, L3_ffn_Sd):
    import jax
    import jax.numpy as jnp

    def _L0_xattn_ref(x1, x2, W, b):
        import jax, jax.numpy as jnp
        import numpy as np
        D1, D2, D3 = (128, 128, 128)
        d1 = x1.shape[-1]
        W1 = W[:, :d1]
        W2 = W[:, d1:]
        part1 = jnp.einsum('bld,ed->ble', x1, W1)
        part2 = jnp.einsum('bld,ed->be', x2, W2) / x2.shape[1]
        return part1 + part2[:, None, :] + b

    def _L0_ffn_ref(x, w_gate, w_up, w_down):
        import jax, jax.numpy as jnp
        import numpy as np
        BLOCK = 32
        W_BITS = 4
        ACT_BITS = 16

        def act_qdq(x):
            qmax = 2.0 ** (ACT_BITS - 1) - 1.0
            scale = jnp.maximum(jnp.max(jnp.abs(x)) / qmax, 1e-12)
            return jnp.clip(jnp.round(x / scale), -qmax - 1.0, qmax) * scale

        def fixed_qdq_u16(x):
            scale = 1.0 / 65536.0
            return jnp.clip(jnp.round(x / scale), 0.0, 65535.0) * scale

        def lpbq_dequant(w):
            O, I = w.shape
            qmax = 2.0 ** (W_BITS - 1) - 1.0
            wb = w.reshape(O, I // BLOCK, BLOCK)
            s = jnp.maximum(jnp.max(jnp.abs(wb), axis=-1, keepdims=True) / qmax, 1e-12)
            wq = jnp.clip(jnp.round(wb / s), -qmax - 1.0, qmax) * s
            return wq.reshape(O, I)
        x = act_qdq(x)
        up = act_qdq(x @ lpbq_dequant(w_up).T)
        gate = act_qdq(x @ lpbq_dequant(w_gate).T)
        sig = fixed_qdq_u16(jax.nn.sigmoid(gate))
        gate = act_qdq(gate * sig)
        o = act_qdq(gate * up)
        return o @ lpbq_dequant(w_down).T

    def _L1_xattn_ref(q, k, v, in_proj_weight, in_proj_bias, out_w, out_b):
        import jax, jax.numpy as jnp
        import numpy as np
        EMBED_DIM = 128
        NUM_HEADS = 16
        HEAD_DIM = EMBED_DIM // NUM_HEADS
        B, T, S = (2, 256, 256)
        H, D = (NUM_HEADS, HEAD_DIM)
        w_q, w_k, w_v = jnp.split(in_proj_weight, 3, axis=0)
        b_q, b_k, b_v = jnp.split(in_proj_bias, 3, axis=0)
        qp = q @ w_q.T + b_q
        kp = k @ w_k.T + b_k
        vp = v @ w_v.T + b_v
        bsz, t, _ = qp.shape
        s = kp.shape[1]
        qh = qp.reshape(bsz, t, H, D).transpose(0, 2, 1, 3)
        kh = kp.reshape(bsz, s, H, D).transpose(0, 2, 1, 3)
        vh = vp.reshape(bsz, s, H, D).transpose(0, 2, 1, 3)
        scale = D ** (-0.5)
        attn = jnp.einsum('bhtd,bhsd->bhts', qh, kh) * scale
        attn = jax.nn.softmax(attn, axis=-1)
        ctx = jnp.einsum('bhts,bhsd->bhtd', attn, vh)
        ctx = ctx.transpose(0, 2, 1, 3).reshape(bsz, t, H * D)
        out = ctx @ out_w.T + out_b
        return out

    def _L1_ffn_ref(x, Wp, sim_matrix, temperature, W1, b1, W2, b2):
        import jax, jax.numpy as jnp
        import numpy as np
        EPS = 1e-12

        def _l2norm(v):
            n = jnp.sqrt(jnp.sum(v * v, axis=-1, keepdims=True))
            return v / jnp.maximum(n, EPS)
        E = sim_matrix.shape[0]
        top_k = 2
        proj = jnp.einsum('bsd,ed->bse', x, Wp)
        pn = _l2norm(proj)
        sn = _l2norm(sim_matrix)
        gate_scores = jnp.einsum('bsd,ed->bse', pn, sn) / temperature
        top_v, top_i = jax.lax.top_k(gate_scores, top_k)
        gate_probs = jax.nn.softmax(top_v, axis=-1)
        comb = jnp.sum(jax.nn.one_hot(top_i, E, dtype=x.dtype) * gate_probs[..., None], axis=-2)
        h = jax.nn.gelu(jnp.einsum('bsd,edf->ebsf', x, W1) + b1[:, None, None, :], approximate=False)
        eo = jnp.einsum('ebsf,efd->ebsd', h, W2) + b2[:, None, None, :]
        out = jnp.einsum('ebsd,bse->bsd', eo, comb)
        return out

    def _L2_xattn_ref(x, ctx, Wq, Wkv, Wproj, q_gamma, k_gamma):
        import jax, jax.numpy as jnp
        import numpy as np
        HEADS = 16
        EPS = 1e-06

        def _rmsnorm(x, gamma):
            inv = jax.lax.rsqrt(jnp.mean(x * x, axis=-1, keepdims=True) + EPS)
            return x * inv * gamma
        B, L, D = x.shape
        Lc = ctx.shape[1]
        H = HEADS
        hd = D // H
        q = (x @ Wq).reshape(B, L, H, hd).transpose(0, 2, 1, 3)
        kv = (ctx @ Wkv).reshape(B, Lc, 2, H, hd).transpose(2, 0, 3, 1, 4)
        k, v = (kv[0], kv[1])
        q = _rmsnorm(q, q_gamma)
        k = _rmsnorm(k, k_gamma)
        scale = 1.0 / np.sqrt(hd)
        attn = jnp.einsum('bhld,bhmd->bhlm', q, k) * scale
        attn = jax.nn.softmax(attn, axis=-1)
        out = jnp.einsum('bhlm,bhmd->bhld', attn, v)
        out = out.transpose(0, 2, 1, 3).reshape(B, L, D)
        return out @ Wproj

    def _L2_ffn_ref(x, W1, b1, quantum_phases, quantum_weights_real, quantum_weights_imag, W2, b2):
        import jax, jax.numpy as jnp
        import numpy as np
        B, S, D_MODEL, D_FF = (4, 256, 128, 512)

        def _quantum_transform(hidden, theta, w_real, w_imag):
            imag = w_imag * jnp.sin(theta + hidden * 0.1)
            quantum_phase = jnp.cos(theta) * w_real + jnp.sin(theta) * w_imag
            return hidden + quantum_phase * imag * 0.1
        hidden = jnp.einsum('bsd,df->bsf', x, W1) + b1
        q = _quantum_transform(hidden, quantum_phases, quantum_weights_real, quantum_weights_imag)
        act = jax.nn.relu(q)
        return jnp.einsum('bsf,fd->bsd', act, W2) + b2

    def _L3_xattn_ref(query, key, value, mask, Wq, Wk, Wv, Wo, bo):
        import jax, jax.numpy as jnp
        import numpy as np
        H = 16
        B, Tq, _ = query.shape
        Tk = key.shape[1]
        Dv = Wv.shape[0]
        Q = jnp.einsum('btd,ed->bte', query, Wq).reshape(B, Tq, H, -1).transpose(0, 2, 1, 3)
        K = jnp.einsum('btd,ed->bte', key, Wk).reshape(B, Tk, H, -1).transpose(0, 2, 1, 3)
        V = jnp.einsum('btd,ed->bte', value, Wv).reshape(B, Tk, H, -1).transpose(0, 2, 1, 3)
        d_k = K.shape[-1]
        scores = jnp.einsum('bhqd,bhkd->bhqk', Q, K) / jnp.sqrt(jnp.asarray(d_k, Q.dtype))
        scores = jnp.where(mask[:, None] == 0, jnp.asarray(-1000000000.0, scores.dtype), scores)
        attn = jax.nn.softmax(scores, axis=-1)
        Z = jnp.einsum('bhqk,bhkd->bhqd', attn, V)
        Zc = Z.transpose(0, 2, 1, 3).reshape(B, Tq, Dv)
        return jnp.einsum('btd,ed->bte', Zc, Wo) + bo

    def _L3_ffn_ref(hidden_states, gate_w, Wg, Wu, Wd, Sg, Su, Sd):
        import jax, jax.numpy as jnp
        import numpy as np
        E = 16
        F_C = 2.0
        D = 128
        I = 4 * D
        IS = 2 * D
        B, S = (4, 128)
        b, s, d = hidden_states.shape
        T = b * s
        C = int(T * F_C / E)
        flat_x = hidden_states.reshape(T, d)
        logits = flat_x @ gate_w.T
        scores = jax.nn.softmax(logits, axis=-1).T
        topk_weight, topk_idx = jax.lax.top_k(scores, C)
        xg = flat_x[topk_idx]
        g = jnp.einsum('ecd,eid->eci', xg, Wg)
        u = jnp.einsum('ecd,eid->eci', xg, Wu)
        h = jax.nn.gelu(g, approximate=False) * u
        eo = jnp.einsum('eci,edi->ecd', h, Wd)
        eo = eo * topk_weight[..., None]
        flat_out = jnp.zeros_like(flat_x).at[topk_idx.reshape(-1)].add(eo.reshape(-1, d))
        out = flat_out.reshape(b, s, d)
        sg = hidden_states @ Sg.T
        su = hidden_states @ Su.T
        shared = jax.nn.gelu(sg, approximate=False) * su @ Sd.T
        return out + shared
    x = x + jnp.tanh(g_xattn[0]) * _L0_xattn_ref(_layernorm(x, axis=-1), ctx_1024, L0_xattn_W, L0_xattn_b)
    x = x + jnp.tanh(g_ffn[0]) * _L0_ffn_ref(_layernorm(x, axis=-1), L0_ffn_w_gate, L0_ffn_w_up, L0_ffn_w_down)
    x = x + jnp.tanh(g_xattn[1]) * _L1_xattn_ref(_layernorm(x, axis=-1), ctx_1024, ctx_1024, L1_xattn_in_proj_weight, L1_xattn_in_proj_bias, L1_xattn_out_w, L1_xattn_out_b)
    x = x + jnp.tanh(g_ffn[1]) * _L1_ffn_ref(_layernorm(x, axis=-1), L1_ffn_Wp, L1_ffn_sim_matrix, L1_ffn_temperature, L1_ffn_W1, L1_ffn_b1, L1_ffn_W2, L1_ffn_b2)
    x = x + jnp.tanh(g_xattn[2]) * _L2_xattn_ref(_layernorm(x, axis=-1), ctx_1024, L2_xattn_Wq, L2_xattn_Wkv, L2_xattn_Wproj, L2_xattn_q_gamma, L2_xattn_k_gamma)
    x = x + jnp.tanh(g_ffn[2]) * _L2_ffn_ref(_layernorm(x, axis=-1), L2_ffn_W1, L2_ffn_b1, L2_ffn_quantum_phases, L2_ffn_quantum_weights_real, L2_ffn_quantum_weights_imag, L2_ffn_W2, L2_ffn_b2)
    x = x + jnp.tanh(g_xattn[3]) * _L3_xattn_ref(_layernorm(x, axis=-1), ctx_1024, ctx_1024, mask_BxSxS2_if1, L3_xattn_Wq, L3_xattn_Wk, L3_xattn_Wv, L3_xattn_Wo, L3_xattn_bo)
    x = x + jnp.tanh(g_ffn[3]) * _L3_ffn_ref(_layernorm(x, axis=-1), L3_ffn_gate_w, L3_ffn_Wg, L3_ffn_Wu, L3_ffn_Wd, L3_ffn_Sg, L3_ffn_Su, L3_ffn_Sd)
    return x

_drawn_inputs = setup_inputs


def setup_inputs(seed=0):
    import zlib

    import numpy as np

    out = dict(_drawn_inputs(seed))
    spreads = {'L1_xattn_in_proj_bias': (0.0, 0.1),
     'L1_xattn_out_b': (0.0, 0.1),
     'L1_ffn_b1': (0.0, 0.1),
     'L1_ffn_b2': (0.0, 0.1),
     'L2_xattn_q_gamma': (1.0, 0.2),
     'L2_xattn_k_gamma': (1.0, 0.6),
     'L2_ffn_b1': (0.0, 0.1),
     'L2_ffn_b2': (0.0, 0.1),
     'L3_xattn_bo': (0.0, 0.1)}
    factors = {'g_ffn': 35.544,
     'L2_ffn_quantum_phases': 8.0,
     'L2_ffn_quantum_weights_real': 8.0,
     'L2_ffn_quantum_weights_imag': 8.0,
     'L3_xattn_Wq': 8.0,
     'L3_xattn_Wk': 8.0,
     'L3_xattn_Wv': 3.998,
     'L3_xattn_Wo': 4.063,
     'L3_ffn_gate_w': 8.0,
     'L3_ffn_Wg': 8.0,
     'L3_ffn_Wu': 8.0,
     'L3_ffn_Wd': 8.0,
     'L3_ffn_Sg': 8.0,
     'L3_ffn_Su': 8.0,
     'L3_ffn_Sd': 8.0}
    for name, (base, spread) in spreads.items():
        noise = np.random.default_rng([zlib.crc32(name.encode()), seed]).standard_normal(out[name].shape)
        drawn = base * np.exp(spread * noise) if base else spread * noise
        out[name] = jnp.asarray(drawn.astype(out[name].dtype))
    for name, factor in factors.items():
        out[name] = (out[name] * factor).astype(out[name].dtype)
    return out
```

```python
from contextlib import ExitStack

import concourse.bass as bass
from concourse import mybir

F32 = mybir.dt.float32
BF16 = mybir.dt.bfloat16
I32 = mybir.dt.int32
ALU = mybir.AluOpType
ACT = mybir.ActivationFunctionType
X = mybir.AxisListType.X
RMAX = bass.bass_isa.ReduceOp.max

P = 128
D = 128
NT = 32
KEYS = 77
HEADS = 16
HD = D // HEADS
GROUPS = 4
HG = HEADS // GROUPS
NTOK = NT * P
BLK = 512
NBLK = NTOK // BLK
TB = BLK // P
MAGIC = 12582912.0
NEG = -1e9
S_BANKS = [(0, 6), (6, 6), (12, 4)]
INV_2PI = 0.15915494309189535
TWO_PI = 6.283185


def act(eng, out, in_, func, **kw):
    return eng.activation(out, in_, func, **kw)


class Sems:

    def __init__(self, nc, ctx, stage):
        self.nc, self.stage, self.made = nc, stage, []
        ctx.callback(self.clear)

    def one(self, name):
        self.made.append(self.nc.alloc_semaphore(f"{self.stage}_{name}"))
        return self.made[-1]

    def two(self, name):
        return [self.one(f"{name}{p}") for p in range(2)]

    def clear(self):
        self.nc.clear_and_free_semaphores(self.made)
        self.nc.all_engine_barrier()


class Chain:

    def __init__(self, eng, sem):
        self.eng, self.sem, self.n = eng, sem, 0

    def __call__(self, ins):
        ins.then_inc(self.sem, 1)
        self.n += 1
        self.eng.wait_ge(self.sem, self.n)


def constants(nc, t, d):
    with ExitStack() as ctx:
        s = Sems(nc, ctx, "const")
        ident0, ident1, masks, ones_ready = s.one("ident0"), s.one("ident1"), s.one("masks"), s.one("ones_ready")
        loads, gates = s.one("loads"), s.one("gates")
        pool_steps = s.one("pool_steps")
        block = ctx.enter_context(nc.Block())

        @block.sync
        def _(sp):
            sp.dma_start(t["x"][:], d["x"]).then_inc(loads, 16)
            sp.dma_start(t["ctxT"][:], d["ctxT"]).then_inc(loads, 16)
            sp.dma_start(t["graw"][:, 0:4], d["g_xattn"].partition_broadcast(P)).then_inc(loads, 16)
            sp.dma_start(t["graw"][:, 4:8], d["g_ffn"].partition_broadcast(P)).then_inc(loads, 16)
            sp.wait_ge(loads, 64)

        @block.gpsimd
        def _(pool):
            step = Chain(pool, pool_steps)
            step(pool.memset(t["ident"][:], 0.0))
            step(pool.affine_select(out=t["ident"][:], in_=t["ident"][:], compare_op=ALU.not_equal, fill=1.0,
                                    base=0, pattern=[[-1, P]], channel_multiplier=1))
            step(pool.tensor_copy(t["identb"][:], t["ident"][:]))
            step(pool.memset(t["ones"][:], 1.0))
            step(pool.memset(t["headmask"][:], 1.0))
            step(pool.affine_select(out=t["headmask"][:], in_=t["headmask"][:], compare_op=ALU.is_ge, fill=0.0,
                                    base=0, pattern=[[-HD, HEADS]], channel_multiplier=1))
            step(pool.affine_select(out=t["headmask"][:], in_=t["headmask"][:], compare_op=ALU.is_ge, fill=0.0,
                                    base=HD - 1, pattern=[[HD, HEADS]], channel_multiplier=-1))
            step(pool.tensor_scalar(t["blockones"][:].rearrange("p (h d) -> p h d", d=HD),
                                    t["headmask"][:].unsqueeze(2).broadcast_to([P, HEADS, HD]),
                                    1.0 / HD, None, ALU.mult))
            step(pool.memset(t["onespad"][:], 0.0))
            for i in range(HG):
                step(pool.memset(t["onespad"][:, i, HD * i:HD * i + HD], 1.0))
            step(pool.memset(t["minus_half"][:], -0.5))
            step(pool.memset(t["plus_half"][:], 0.5))
            step(pool.memset(t["eps"][:], 1e-6))
            for b in range(2):
                step(pool.memset(t["Vpad"][b][:], 0.0))

        @block.scalar
        def _(sc):
            sc.wait_ge(loads, 64)
            sc.activation(t["gate"][:], t["graw"][:], ACT.Tanh).then_inc(gates, 1)


def layernorm(nc, t, stage, row_any=None):
    with ExitStack() as ctx:
        s = Sems(nc, ctx, stage)
        steps, centred, squared, var_ready, rstd_ready, scaled, turned, kept = (
            s.one("steps"), s.one("centred"), s.one("squared"), s.one("var_ready"), s.one("rstd_ready"),
            s.two("scaled"), s.two("turned"), s.two("kept"))
        ps = t["ps"]
        small = t["small"]
        mean, var, rstd = small[:, 0:NT], small[:, NT:2 * NT], small[:, 2 * NT:3 * NT]
        x3 = t["x"][:].rearrange("p (n d) -> p n d", d=D)
        xc3 = t["xc"][:].rearrange("p (n d) -> p n d", d=D)
        wide = lambda a: a.unsqueeze(2).broadcast_to([P, NT, D])
        block = ctx.enter_context(nc.Block())

        @block.vector
        def _(v):
            step = Chain(v, steps)
            step(v.tensor_reduce(mean, x3, X, ALU.add))
            step(v.tensor_scalar(mean, mean, 1.0 / D, None, ALU.mult))
            v.tensor_tensor(xc3, x3, wide(mean), ALU.subtract).then_inc(centred, 1)
            v.wait_ge(squared, 1)
            step(v.tensor_reduce(var, t["xnT"][:].rearrange("p (n d) -> p n d", d=D), X, ALU.add))
            v.tensor_scalar(var, var, 1.0 / D, 1e-5, ALU.mult, ALU.add).then_inc(var_ready, 1)
            v.wait_ge(rstd_ready, 1)
            if row_any is not None:
                step(v.tensor_tensor(rstd, rstd, row_any, ALU.mult))
            with v.Fori(0, NBLK // 2) as j:
                for p in range(2):
                    v.wait_ge(turned[p], j)
                    v.tensor_tensor(
                        t["stage"][p][:].rearrange("p (n d) -> p n d", d=D),
                        t["xc"][:, bass.ds((2 * j + p) * BLK, BLK)].rearrange("p (n d) -> p n d", d=D),
                        small[:, bass.ds(2 * NT + (2 * j + p) * TB, TB)].unsqueeze(2).broadcast_to([P, TB, D]),
                        ALU.mult).then_inc(scaled[p], 1)

        @block.gpsimd
        def _(pool):
            pool.wait_ge(var_ready, 1)
            pool.tensor_tensor(rstd, var, t["minus_half"][:, 0:NT], ALU.pow).then_inc(rstd_ready, 1)

        @block.tensor
        def _(pe):
            with pe.Fori(0, NBLK // 2) as j:
                for p in range(2):
                    pe.wait_ge(scaled[p], j + 1)
                    pe.wait_ge(kept[p], j)
                    for i in range(TB):
                        ins = pe.transpose(ps[:, p, i * P:i * P + P], t["stage"][p][:, i * P:i * P + P], t["ident"][:])
                    ins.then_inc(turned[p], 1)

        @block.scalar
        def _(sc):
            sc.wait_ge(centred, 1)
            sc.activation(t["xnT"][:], t["xc"][:], ACT.Square).then_inc(squared, 1)
            sc.wait_ge(rstd_ready, 1)
            with sc.Fori(0, NBLK // 2) as j:
                for p in range(2):
                    sc.wait_ge(turned[p], j + 1)
                    sc.activation(t["xnT"][:, bass.ds((2 * j + p) * BLK, BLK)], ps[:, p, :], ACT.Copy).then_inc(kept[p], 1)


def concat_linear(nc, t, d):
    with ExitStack() as ctx:
        s = Sems(nc, ctx, "l0x")
        loads, sum_ready, mean_ready, linear, residual, feat = (
            s.one("loads"), s.one("sum_ready"), s.two("mean_ready"), s.two("linear"), s.two("residual"), s.two("feat"))
        ps = t["ps"]
        w = t["wstat"]
        block = ctx.enter_context(nc.Block())

        @block.sync
        def _(sp):
            sp.dma_start(w[:, 0:256], d["l0_WT"]).then_inc(loads, 16)
            sp.dma_start(t["row"][:, 0:D], d["l0_b"]).then_inc(loads, 16)

        @block.vector
        def _(v):
            ctx_sum = t["small"][:, 0:NT]
            v.tensor_reduce(ctx_sum, t["ctxT"][:].rearrange("p (n k) -> p n k", k=KEYS), X, ALU.add).then_inc(sum_ready, 1)
            v.wait_ge(sum_ready, 1)
            with v.Fori(0, NT // 2) as j:
                for p in range(2):
                    v.wait_ge(linear[p], j)
                    v.tensor_scalar(t["stage"][p][:, 0:P], t["small"][:, bass.ds(2 * j + p, 1)].broadcast_to([P, P]),
                                    1.0 / KEYS, None, ALU.mult).then_inc(mean_ready[p], 1)
                    v.tensor_copy(t["stage"][p][:, P:2 * P], t["xnT"][:, bass.ds((2 * j + p) * P, P)]).then_inc(feat[p], 1)
                for p in range(2):
                    v.wait_ge(linear[p], j + 1)
                    xb = t["x"][:, bass.ds((2 * j + p) * P, P)]
                    v.scalar_tensor_tensor(xb, ps[:, p, 0:D], t["gate"][:, 0:1], xb, ALU.mult, ALU.add).then_inc(residual[p], 1)

        @block.tensor
        def _(pe):
            pe.wait_ge(loads, 32)
            with pe.Fori(0, NT // 2) as j:
                for p in range(2):
                    pe.wait_ge(residual[p], j)
                    pe.wait_ge(mean_ready[p], j + 1)
                    pe.wait_ge(feat[p], j + 1)
                    pe.matmul(ps[:, p, 0:D], t["stage"][p][:, P:2 * P], w[:, 0:128], start=True, stop=False)
                    pe.matmul(ps[:, p, 0:D], t["stage"][p][:, 0:P], w[:, 128:256], start=False, stop=False)
                    pe.matmul(ps[:, p, 0:D], t["ones"][0:1, 0:P], t["row"][0:1, 0:D], start=False, stop=True).then_inc(linear[p], 1)


def mask_rows(nc, t, d):
    with ExitStack() as ctx:
        s = Sems(nc, ctx, "rows")
        came, read, steps = s.two("came"), s.two("read"), s.one("steps")
        block = ctx.enter_context(nc.Block())
        n = 8

        @block.sync
        def _(sp):
            for c in range(NT // n):
                if c >= 2:
                    sp.wait_ge(read[c % 2], c // 2)
                sp.dma_start(t["maski"][c % 2][:], d["mask"][:, c * n * KEYS:(c + 1) * n * KEYS]).then_inc(came[c % 2], 16)

        @block.vector
        def _(v):
            step = Chain(v, steps)
            for c in range(NT // n):
                v.wait_ge(came[c % 2], 16 * (c // 2 + 1))
                nz = t["maskf"][:, 0:n * KEYS]
                v.tensor_scalar(nz, t["maski"][c % 2][:], 0.0, None, ALU.not_equal).then_inc(read[c % 2], 1)
                v.wait_ge(read[c % 2], c // 2 + 1)
                step(v.tensor_reduce(t["row_any"][:, c * n:c * n + n], nz.rearrange("p (n k) -> p n k", k=KEYS), X, ALU.max))

def rms_qk(nc, t, d, layer):
    KB = 352
    assert KB * 7 == NT * KEYS
    with ExitStack() as ctx:
        s = Sems(nc, ctx, layer + "n")
        loads, made, squared, means, rooted, inverted, normed = (
            s.one("loads"), s.one("made"), s.one("squared"), s.one("means"), s.one("rooted"), s.one("inverted"), s.one("normed"))
        ps, w = t["ps"], t["wstat"]
        sq, root, inv = t["stage"][0], t["stage"][1], t["xc"]
        parts = [(t["xnT"], t["xnT"], w[:, 0:128], t["cols"][:, 0:1], BLK, NBLK, 0),
                 (t["ctxT"], t["kT"], w[:, 128:256], t["cols"][:, 1:2], KB, 7, NBLK)]
        block = ctx.enter_context(nc.Block())

        @block.sync
        def _(sp):
            sp.dma_start(w[:, 0:256], d[f"{layer}_W"][:, 0:256]).then_inc(loads, 16)
            sp.dma_start(t["cols"][:, 0:2], d[f"{layer}_gamma"]).then_inc(loads, 16)

        @block.tensor
        def _(pe):
            pe.wait_ge(loads, 32)
            for src, dst, wt, gamma, n, blocks, before in parts:
                with pe.Fori(0, blocks) as j:
                    pe.wait_ge(normed, before + j)
                    pe.matmul(ps[:, 0, 0:n], wt, src[:, bass.ds(j * n, n)], start=True, stop=True).then_inc(made, 1)
                    pe.wait_ge(squared, before + j + 1)
                    pe.matmul(ps[:, 1, 0:n], t["blockones"][:], sq[:, 0:n], start=True, stop=True).then_inc(means, 1)

        @block.scalar
        def _(sc):
            for src, dst, wt, gamma, n, blocks, before in parts:
                with sc.Fori(0, blocks) as j:
                    sc.wait_ge(made, before + j + 1)
                    sc.activation(sq[:, 0:n], ps[:, 0, 0:n], ACT.Square).then_inc(squared, 1)
                    sc.wait_ge(means, before + j + 1)
                    sc.activation(root[:, 0:n], ps[:, 1, 0:n], ACT.Sqrt, bias=t["eps"][:]).then_inc(rooted, 1)

        @block.vector
        def _(v):
            v.wait_ge(loads, 32)
            for src, dst, wt, gamma, n, blocks, before in parts:
                with v.Fori(0, blocks) as j:
                    v.wait_ge(rooted, before + j + 1)
                    v.wait_ge(normed, before + j)
                    v.reciprocal(inv[:, 0:n], root[:, 0:n]).then_inc(inverted, 1)
                    v.wait_ge(inverted, before + j + 1)
                    v.scalar_tensor_tensor(dst[:, bass.ds(j * n, n)], ps[:, 0, 0:n], gamma, inv[:, 0:n], ALU.mult, ALU.mult).then_inc(normed, 1)


def attention(nc, t, d, layer, gate_at, bias_qk=False, bias_v=False, bias_out=False, ready_qk=False, masked=False):
    with ExitStack() as ctx:
        s = Sems(nc, ctx, layer)
        loads = s.one("loads")
        ctx_staged, qk_made, qk_kept, v_made, v_kept = (
            s.two("ctx_staged"), s.two("qk_made"), s.two("qk_kept"), s.two("v_made"), s.two("v_kept"))
        kblk_ready, scores_ready, max_ready, shifted, exp_ready = (
            s.two("kblk_ready"), s.two("scores_ready"), s.two("max_ready"), s.two("shifted"), s.two("exp_ready"))
        sum_ready, recip_ready, prob_ready = s.two("sum_ready"), s.two("recip_ready"), s.two("prob_ready")
        turned, turned_kept, heads_made, heads_kept, out_made, residual = (
            s.two("turned"), s.two("turned_kept"), s.two("heads_made"), s.two("heads_kept"), s.two("out_made"),
            s.two("residual"))
        if masked:
            mask_came, mask_made, mask_step = s.two("mask_came"), s.two("mask_made"), s.two("mask_step")
        ps = t["ps"]
        w = t["wstat"]
        VB = ps[0:KEYS, 1, 0:D]
        OUT = ps[:, 1, 128:128 + D]
        OT = ps[:, 7, 0:P]
        qk, kblk, prob, pt, vpad, oT, rden = (t[n] for n in ("qk", "kblk", "prob", "pt", "Vpad", "oT", "rden"))
        scale = float(HD) ** -0.5

        def other(j, p):
            return 1 - p, j + p

        block = ctx.enter_context(nc.Block())

        @block.sync
        def _(sp):
            n = 16
            sp.dma_start(w[:, 0:512], d[f"{layer}_W"]).then_inc(loads, n)
            if bias_qk:
                sp.dma_start(t["cols"][:, 0:2], d[f"{layer}_bqk"]).then_inc(loads, n)
            if bias_v:
                sp.dma_start(t["row"][:, 0:D], d[f"{layer}_bv"]).then_inc(loads, n)
            if bias_out:
                sp.dma_start(t["row"][:, D:2 * D], d[f"{layer}_bo"]).then_inc(loads, n)
            if masked:
                with sp.Fori(0, NT // 2) as j:
                    for p in range(2):
                        sp.wait_ge(mask_made[p], j)
                        sp.dma_start(t["maski"][p][:, 0:KEYS], d["mask"][:, bass.ds((2 * j + p) * KEYS, KEYS)]).then_inc(mask_came[p], 16)

        n_loads = 16 * (1 + bias_qk + bias_v + bias_out)

        @block.gpsimd
        def _(pool):
            with pool.Fori(0, NT // 2) as j:
                for p in range(2):
                    pool.wait_ge(v_made[p], j)
                    pool.tensor_copy(t["stage"][p][:, 0:KEYS], t["ctxT"][:, bass.ds((2 * j + p) * KEYS, KEYS)]).then_inc(ctx_staged[p], 1)
                for p in range(2):
                    pool.wait_ge(qk_kept[p], 2 * j + 2)
                    pool.wait_ge(scores_ready[p], j)
                    pool.tensor_tensor(kblk[p][:].rearrange("p (h k) -> p h k", k=KEYS),
                                       qk[p][:, P:P + KEYS].unsqueeze(1).broadcast_to([P, HEADS, KEYS]),
                                       t["headmask"][:].unsqueeze(2).broadcast_to([P, HEADS, KEYS]),
                                       ALU.mult).then_inc(kblk_ready[p], 1)
                for p in range(2):
                    pool.wait_ge(recip_ready[p], j + 1)
                    pool.tensor_tensor(prob[p][:], prob[p][:], rden[p][:].unsqueeze(2).broadcast_to([P, HEADS, KEYS]),
                                       ALU.mult).then_inc(prob_ready[p], 1)

        @block.tensor
        def _(pe):
            pe.wait_ge(loads, n_loads)
            with pe.Fori(0, NT // 2) as j:
                for p in range(2):
                    o, n = other(j, p)
                    if not ready_qk:
                        pe.wait_ge(qk_kept[o], 2 * n)
                        pe.matmul(ps[:, 0, 0:P], w[:, 0:128], t["xnT"][:, bass.ds((2 * j + p) * P, P)], start=True, stop=True)
                        pe.matmul(ps[:, 0, P:P + KEYS], w[:, 128:256], t["ctxT"][:, bass.ds((2 * j + p) * KEYS, KEYS)], start=True, stop=True).then_inc(qk_made[p], 1)
                    pe.wait_ge(ctx_staged[p], j + 1)
                    pe.wait_ge(v_kept[o], n)
                    if p == 0:
                        pe.wait_ge(residual[1], j)
                    ins = pe.matmul(VB, t["stage"][p][:, 0:KEYS], w[:, 256:384], start=True, stop=not bias_v)
                    if bias_v:
                        ins = pe.matmul(VB, t["ones"][0:1, 0:KEYS], t["row"][0:1, 0:D], start=False, stop=True)
                    ins.then_inc(v_made[p], 1)
                for p in range(2):
                    o, n = other(j, p)
                    pe.wait_ge(kblk_ready[p], j + 1)
                    pe.wait_ge(shifted[o], 3 * n)
                    if masked:
                        pe.wait_ge(mask_made[p], j + 1)
                    for i, (h0, nh) in enumerate(S_BANKS):
                        dst = ps[:, 2 + i, 0:nh * KEYS]
                        if masked:
                            pe.matmul(dst.rearrange("p (h k) -> p h k", k=KEYS), t["identb"][:],
                                      t["maskb"][p][:].unsqueeze(1).broadcast_to([P, nh, KEYS]), start=True, stop=False)
                        ins = pe.matmul(dst, qk[p][:, 0:P], kblk[p][:, h0 * KEYS:(h0 + nh) * KEYS], start=not masked, stop=True)
                    ins.then_inc(scores_ready[p], 1)

                def weigh(p, r, o, n):
                    if r == 0:
                        pe.wait_ge(heads_kept[o], n)
                        pe.wait_ge(v_kept[p], j + 1)
                    pe.wait_ge(turned_kept[p], 4 * j + r + 1)
                    for g in range(GROUPS):
                        ins = pe.matmul(ps[32 * g:32 * g + 32, 7, 0:P], vpad[p][:, HG * g + r, :], pt[p][:, r, g, :],
                                        start=(r == 0), stop=(r == HG - 1), tile_position=(0, 32 * g))
                    return ins

                for p in range(2):
                    o, n = other(j, p)
                    pe.wait_ge(prob_ready[p], j + 1)
                    for r in range(HG):
                        if r >= 2:
                            pe.wait_ge(turned_kept[p], 4 * j + r - 1)
                        else:
                            pe.wait_ge(turned_kept[o], 4 * n)
                        for g in range(GROUPS):
                            ins = pe.transpose(ps[0:KEYS, 5 + r % 2, g * P:g * P + P], prob[p][:, HG * g + r, :], t["ident"][:])
                        ins.then_inc(turned[p], 1)
                        if r:
                            weigh(p, r - 1, o, n)
                    weigh(p, HG - 1, o, n).then_inc(heads_made[p], 1)
                for p in range(2):
                    pe.wait_ge(heads_kept[p], j + 1)
                    if p == 0:
                        pe.wait_ge(v_kept[1], j + 1)
                    else:
                        pe.wait_ge(residual[0], j + 1)
                    ins = pe.matmul(OUT, oT[p][:], w[:, 384:512], start=True, stop=not bias_out)
                    if bias_out:
                        ins = pe.matmul(OUT, t["ones"][0:1, 0:P], t["row"][0:1, D:2 * D], start=False, stop=True)
                    ins.then_inc(out_made[p], 1)

        @block.scalar
        def _(sc):
            sc.wait_ge(loads, n_loads)
            with sc.Fori(0, NT // 2) as j:
                for p in range(2):
                    sc.wait_ge(scores_ready[p], j)
                    sc.wait_ge(kblk_ready[p], j)
                    if ready_qk:
                        q_src, k_src = t["xnT"][:, bass.ds((2 * j + p) * P, P)], t["kT"][:, bass.ds((2 * j + p) * KEYS, KEYS)]
                    else:
                        sc.wait_ge(qk_made[p], j + 1)
                        q_src, k_src = ps[:, 0, 0:P], ps[:, 0, P:P + KEYS]
                    bq = dict(bias=t["cols"][:, 0:1]) if bias_qk else {}
                    bk = dict(bias=t["cols"][:, 1:2]) if bias_qk else {}
                    fn = ACT.Identity if bias_qk else ACT.Copy
                    sc.activation(qk[p][:, 0:P], q_src, fn, **bq).then_inc(qk_kept[p], 1)
                    sc.activation(qk[p][:, P:P + KEYS], k_src, fn, **bk).then_inc(qk_kept[p], 1)
                    sc.wait_ge(v_made[p], j + 1)
                    sc.wait_ge(heads_made[p], j)
                    last = sc.activation(bass.AP(tensor=vpad[p], offset=0, ap=[[HEADS * 32, KEYS], [HG * 32, GROUPS], [32 + HD, HG], [1, HD]]),
                                         VB.rearrange("k (g i c) -> k g i c", g=GROUPS, i=HG), ACT.Copy)
                    last.then_inc(v_kept[p], 1)
                for p in range(2):
                    sc.wait_ge(shifted[p], 3 * j + 3)
                    flat = prob[p][:].rearrange("p h k -> p (h k)")
                    sc.activation(flat, flat, ACT.Exp, scale=scale).then_inc(exp_ready[p], 1)
                for p in range(2):
                    sc.wait_ge(heads_made[p], j)
                    for g in range(GROUPS):
                        sc.wait_ge(turned[p], 4 * j + g + 1)
                        sc.activation(pt[p][:, g, :, :].rearrange("k h q -> k (h q)"), ps[0:KEYS, 5 + g % 2, :], ACT.Copy).then_inc(turned_kept[p], 1)

        @block.vector
        def _(v):
            with v.Fori(0, NT // 2) as j:
                if masked:
                    for p in range(2):
                        v.wait_ge(mask_came[p], 16 * (j + 1))
                        v.wait_ge(scores_ready[p], j)
                        v.wait_ge(mask_made[p], j)
                        v.tensor_scalar(t["maskf"][:, p * KEYS:(p + 1) * KEYS], t["maski"][p][:, 0:KEYS], 0.0, None, ALU.is_equal).then_inc(mask_step[p], 1)
                        v.wait_ge(mask_step[p], j + 1)
                        v.tensor_scalar(t["maskb"][p][:], t["maskf"][:, p * KEYS:(p + 1) * KEYS], NEG / scale, None, ALU.mult).then_inc(mask_made[p], 1)
                for p in range(2):
                    v.wait_ge(scores_ready[p], j + 1)
                    for i, (h0, nh) in enumerate(S_BANKS):
                        v.tensor_reduce(t["rowmax"][p][:, h0:h0 + nh], ps[:, 2 + i, 0:nh * KEYS].rearrange("p (h k) -> p h k", k=KEYS), X, ALU.max).then_inc(max_ready[p], 1)
                    v.wait_ge(max_ready[p], 3 * j + 3)
                    v.wait_ge(turned[p], 4 * j)
                    for i, (h0, nh) in enumerate(S_BANKS):
                        v.tensor_tensor(prob[p][:, h0:h0 + nh, :], ps[:, 2 + i, 0:nh * KEYS].rearrange("p (h k) -> p h k", k=KEYS),
                                        t["rowmax"][p][:, h0:h0 + nh].unsqueeze(2).broadcast_to([P, nh, KEYS]), ALU.subtract).then_inc(shifted[p], 1)
                for p in range(2):
                    v.wait_ge(exp_ready[p], j + 1)
                    v.wait_ge(prob_ready[p], j)
                    v.tensor_reduce(t["rowsum"][p][:], prob[p][:], X, ALU.add).then_inc(sum_ready[p], 1)
                    v.wait_ge(sum_ready[p], j + 1)
                    v.reciprocal(rden[p][:], t["rowsum"][p][:]).then_inc(recip_ready[p], 1)
                for p in range(2):
                    v.wait_ge(heads_made[p], j + 1)
                    v.wait_ge(out_made[p], j)
                    v.tensor_copy(oT[p][:], OT).then_inc(heads_kept[p], 1)
                for p in range(2):
                    v.wait_ge(out_made[p], j + 1)
                    xb = t["x"][:, bass.ds((2 * j + p) * P, P)]
                    v.scalar_tensor_tensor(xb, OUT, t["gate"][:, gate_at:gate_at + 1], xb, ALU.mult, ALU.add).then_inc(residual[p], 1)


def quantised_ffn(nc, t, d, gate_at):
    C = 3
    WB = 32
    NW = 3 * C * P // WB
    QCH = 2048
    NQ = C * NTOK // QCH
    with ExitStack() as ctx:
        s = Sems(nc, ctx, "l0f")
        loads, steps, own_max, all_max, wq_ready, w_turned, w_kept, x_ready = (
            s.one("loads"), s.one("steps"), s.one("own_max"), s.one("all_max"), s.one("wq_ready"), s.one("w_turned"),
            s.one("w_kept"), s.one("x_ready"))
        up_made, up_kept, gate_made, gate_kept = s.one("up_made"), s.one("up_kept"), s.one("gate_made"), s.one("gate_kept")
        gate_ready, up_ready, sig_ready, sig_used, sig_step, o_ready = (
            s.one("gate_ready"), s.one("up_ready"), s.two("sig_ready"), s.two("sig_used"), s.two("sig_step"), s.one("o_ready"))
        down_made, down_kept, turned, residual = s.two("down_made"), s.two("down_kept"), s.two("turned"), s.two("residual")
        ps = t["ps"]

        def sb(name, shape):
            return ctx.enter_context(nc.sbuf_tensor("l0f_" + name, shape, F32))

        up, gate = sb("up", [P, C * NTOK]), sb("gate", [P, C * NTOK])
        up3, gate3 = up[:].rearrange("p (c n) -> p c n", c=C), gate[:].rearrange("p (c n) -> p c n", c=C)
        wraw, wT, wscale, winv = sb("wraw", [P, 3 * C * P]), sb("wT", [P, 3 * C * P]), sb("wscale", [P, NW]), sb("winv", [P, NW])
        qs = sb("qs", [P, 32])
        maxes = sb("maxes", [P, 2 * NBLK])
        sig = t["xc"]
        block = ctx.enter_context(nc.Block())

        @block.sync
        def _(sp):
            sp.dma_start(wraw[:], d["l0f_W"]).then_inc(loads, 16)

        @block.vector
        def _(v):
            step = Chain(v, steps)

            def scale_of(k):
                c = qs[:, 4 * k:4 * k + 4]
                v.wait_ge(all_max, k + 1)
                step(v.tensor_scalar(c[:, 2:3], c[:, 1:2], 1.0 / 32767.0, 1e-12, ALU.mult, ALU.max))
                step(v.reciprocal(c[:, 3:4], c[:, 2:3]))
                return c[:, 2:3], c[:, 3:4]

            def quantise(a, k, done):
                scale, inv = scale_of(k)
                step(v.tensor_scalar(a, a, inv, MAGIC, ALU.mult, ALU.add))
                v.tensor_scalar(a, a, MAGIC, scale, ALU.subtract, ALU.mult).then_inc(done, 1)

            v.tensor_reduce(qs[:, 0:1], t["xnT"][:], X, ALU.max, apply_absolute_value=True).then_inc(own_max, 1)
            v.wait_ge(loads, 16)
            w3 = wraw[:].rearrange("p (b i) -> p b i", i=WB)
            sc3 = wscale[:].unsqueeze(2).broadcast_to([P, NW, WB])
            step(v.tensor_reduce(wscale[:], w3, X, ALU.max, apply_absolute_value=True))
            step(v.tensor_scalar(wscale[:], wscale[:], 1.0 / 7.0, 1e-12, ALU.mult, ALU.max))
            step(v.reciprocal(winv[:], wscale[:]))
            step(v.tensor_tensor(w3, w3, winv[:].unsqueeze(2).broadcast_to([P, NW, WB]), ALU.mult))
            step(v.tensor_scalar(wraw[:], wraw[:], MAGIC, MAGIC, ALU.add, ALU.subtract))
            v.tensor_tensor(w3, w3, sc3, ALU.mult).then_inc(wq_ready, 1)
            quantise(t["xnT"][:], 0, x_ready)
            with v.Fori(0, NBLK) as j:
                v.wait_ge(up_kept, j + 1)
                v.tensor_reduce(maxes[:, bass.ds(j, 1)], up3[:, :, bass.ds(j * BLK, BLK)], mybir.AxisListType.XY, ALU.max, apply_absolute_value=True).then_inc(sig_step[0], 1)
                v.wait_ge(gate_kept, j + 1)
                v.tensor_reduce(maxes[:, bass.ds(j + NBLK, 1)], gate3[:, :, bass.ds(j * BLK, BLK)], mybir.AxisListType.XY, ALU.max, apply_absolute_value=True).then_inc(sig_step[0], 1)
            v.wait_ge(sig_step[0], 2 * NBLK)
            v.tensor_reduce(qs[:, 4:5], maxes[:, 0:NBLK], X, ALU.max).then_inc(own_max, 1)
            v.tensor_reduce(qs[:, 8:9], maxes[:, NBLK:2 * NBLK], X, ALU.max).then_inc(own_max, 1)
            quantise(gate[:], 2, gate_ready)
            quantise(up[:], 1, up_ready)
            v.wait_ge(gate_ready, 1)
            for n in range(NQ):
                p = n % 2
                half, part = sig[:, p * QCH:(p + 1) * QCH], gate[:, n * QCH:(n + 1) * QCH]
                v.wait_ge(sig_ready[p], n // 2 + 1)
                step(v.tensor_scalar(half, half, 65536.0, MAGIC, ALU.mult, ALU.add))
                step(v.tensor_scalar(half, half, MAGIC + 65535.0, MAGIC, ALU.min, ALU.subtract))
                v.scalar_tensor_tensor(part, half, 1.0 / 65536.0, part, ALU.mult, ALU.mult).then_inc(sig_used[p], 1)
            v.wait_ge(sig_used[0], NQ // 2)
            v.wait_ge(sig_used[1], NQ // 2)
            v.tensor_reduce(qs[:, 12:13], gate[:], X, ALU.max, apply_absolute_value=True).then_inc(own_max, 1)
            quantise(gate[:], 3, gate_ready)
            v.wait_ge(gate_ready, 2)
            v.wait_ge(up_ready, 1)
            step(v.tensor_tensor(gate[:], gate[:], up[:], ALU.mult))
            v.tensor_reduce(qs[:, 16:17], gate[:], X, ALU.max, apply_absolute_value=True).then_inc(own_max, 1)
            quantise(gate[:], 4, o_ready)
            with v.Fori(0, NBLK // 2) as j:
                for p in range(2):
                    v.wait_ge(turned[p], j + 1)
                    xb = t["x"][:, bass.ds((2 * j + p) * BLK, BLK)]
                    v.scalar_tensor_tensor(xb, ps[:, 2 + p, :], t["gate"][:, gate_at:gate_at + 1], xb, ALU.mult, ALU.add).then_inc(residual[p], 1)

        @block.gpsimd
        def _(pool):
            for k in range(5):
                pool.wait_ge(own_max, {0: 1, 1: 3, 2: 3, 3: 4, 4: 5}[k])
                pool.partition_all_reduce(qs[:, 4 * k + 1:4 * k + 2], qs[:, 4 * k:4 * k + 1], P, RMAX).then_inc(all_max, 1)

        @block.scalar
        def _(sc):
            for b in range(3):
                sc.wait_ge(w_turned, b + 1)
                sc.activation(wT[:, b * C * P:(b + 1) * C * P], ps[:, b, 0:C * P], ACT.Copy).then_inc(w_kept, 1)
            with sc.Fori(0, NBLK) as j:
                sc.wait_ge(up_made, j + 1)
                sc.activation(up3[:, :, bass.ds(j * BLK, BLK)], ps[:, 0:3, :], ACT.Copy).then_inc(up_kept, 1)
                sc.wait_ge(gate_made, j + 1)
                sc.activation(gate3[:, :, bass.ds(j * BLK, BLK)], ps[:, 3:6, :], ACT.Copy).then_inc(gate_kept, 1)
            sc.wait_ge(gate_ready, 1)
            for n in range(NQ):
                p = n % 2
                if n >= 2:
                    sc.wait_ge(sig_used[p], n // 2)
                sc.activation(sig[:, p * QCH:(p + 1) * QCH], gate[:, n * QCH:(n + 1) * QCH], ACT.Sigmoid).then_inc(sig_ready[p], 1)
            with sc.Fori(0, NBLK // 2) as j:
                for p in range(2):
                    sc.wait_ge(down_made[p], j + 1)
                    sc.wait_ge(turned[p], j)
                    sc.activation(t["stage"][p][:], ps[:, p, :], ACT.Copy).then_inc(down_kept[p], 1)

        @block.tensor
        def _(pe):
            pe.wait_ge(wq_ready, 1)
            for b in range(3):
                for i in range(C):
                    ins = pe.transpose(ps[:, b, i * P:(i + 1) * P], wraw[:, (b * C + i) * P:(b * C + i + 1) * P], t["ident"][:])
                ins.then_inc(w_turned, 1)
            pe.wait_ge(w_kept, 3)
            pe.wait_ge(x_ready, 1)
            with pe.Fori(0, NBLK) as j:
                xb = t["xnT"][:, bass.ds(j * BLK, BLK)]
                for which, made, kept in ((0, up_made, up_kept), (1, gate_made, gate_kept)):
                    pe.wait_ge(kept, j)
                    for c in range(C):
                        ins = pe.matmul(ps[:, 3 * which + c, :], wT[:, (which * C + c) * P:(which * C + c + 1) * P], xb, start=True, stop=True)
                    ins.then_inc(made, 1)
            pe.wait_ge(o_ready, 1)
            with pe.Fori(0, NBLK // 2) as j:
                for p in range(2):
                    pe.wait_ge(down_kept[p], j)
                    for c in range(C):
                        ins = pe.matmul(ps[:, p, :], wT[:, (2 * C + c) * P:(2 * C + c + 1) * P], gate3[:, c, bass.ds((2 * j + p) * BLK, BLK)],
                                        start=(c == 0), stop=(c == C - 1))
                    ins.then_inc(down_made[p], 1)
                for p in range(2):
                    pe.wait_ge(down_kept[p], j + 1)
                    pe.wait_ge(residual[p], j)
                    for i in range(TB):
                        ins = pe.transpose(ps[:, 2 + p, i * P:(i + 1) * P], t["stage"][p][:, i * P:(i + 1) * P], t["ident"][:])
                    ins.then_inc(turned[p], 1)


def experts(nc, t, d, stage, E, C, kind, gate_at=None, weight=None, bias1=False, bias2=False):
    nin = 2 if kind == "glu" else 1
    width = (nin + 1) * C * P + (C if bias1 else 0)
    NQ = 2 if E > 1 else 1
    with ExitStack() as ctx:
        s = Sems(nc, ctx, stage)
        came, used = [s.one(f"came{q}") for q in range(NQ)], [s.one(f"used{q}") for q in range(NQ)]
        made, acted, h_step = s.two("made"), s.two("acted"), s.two("h_step")
        h_ready, down_made, residual = s.two("h_ready"), s.two("down_made"), s.two("residual")
        ps = t["ps"]

        def sb(name, shape):
            return ctx.enter_context(nc.sbuf_tensor(f"{stage}_sb_{name}", shape, F32))

        wb = [sb(f"w{q}", [P, width]) for q in range(NQ)]
        b2 = [sb(f"b2{q}", [1, D]) for q in range(NQ)]
        spare = sb("spare", [1, 1])
        h = [sb(f"h{p}", [P, C, BLK]) for p in range(2)]
        ga = [sb(f"ga{p}", [P, BLK]) for p in range(2)]
        sn = [sb(f"sn{p}", [P, BLK]) for p in range(2)] if kind == "sine" else None
        block = ctx.enter_context(nc.Block())
        n_in = 16 * (1 + bias2)

        def chunk_free(eng, p, m, c):
            if c >= 2:
                eng.wait_ge(h_ready[p], m * C + c - 1)
            elif p == 1:
                eng.wait_ge(h_ready[0], m * C + C - 1 + c)
            else:
                eng.wait_ge(h_ready[1], m * C)

        @block.sync
        def _(sp):
            def load(k, q):
                e = bass.ds(k * 2 + q, 1) if E > 1 else slice(0, 1)
                if E > 1:
                    sp.wait_ge(used[q], k)
                sp.dma_start(wb[q][:], d[f"{stage}_W"][e, :, :].rearrange("e p n -> (e p) n")).then_inc(came[q], 16)
                if bias2:
                    sp.dma_start(b2[q][:], d[f"{stage}_b2"][e, :]).then_inc(came[q], 16)
            if E == 1:
                load(0, 0)
            else:
                with sp.Fori(0, E // 2) as k:
                    for q in range(2):
                        load(k, q)

        def loops(eng, each, end=None):
            def inner(k, q):
                e = k * 2 + q if E > 1 else 0
                with eng.Fori(0, NBLK // 2) as j:
                    each(k, q, e, j)
                if end:
                    end(q)
            if E == 1:
                inner(0, 0)
            else:
                with eng.Fori(0, E // 2) as k:
                    for q in range(2):
                        inner(k, q)

        HB = C // 2

        @block.tensor
        def _(pe):
            def each(k, q, e, j):
                pe.wait_ge(came[q], n_in * (k + 1))
                for p in range(2):
                    m = e * (NBLK // 2) + j
                    xb = t["xnT"][:, bass.ds((2 * j + p) * BLK, BLK)]
                    for c in range(C):
                        b = c % 2
                        chunk_free(pe, p, m, c)
                        for i in range(nin):
                            ins = pe.matmul(ps[:, 2 * b + i, :], wb[q][:, (i * C + c) * P:(i * C + c + 1) * P], xb, start=True, stop=True)
                        ins.then_inc(made[b], 1)
                for p in range(2):
                    m = e * (NBLK // 2) + j
                    pe.wait_ge(h_ready[p], (m + 1) * C)
                    pe.wait_ge(residual[p], m)
                    for i in range(TB):
                        dst = ps[:, 4 + p, i * P:(i + 1) * P]
                        for c in range(C):
                            ins = pe.matmul(dst, h[p][:, c, i * P:(i + 1) * P], wb[q][:, (nin * C + c) * P:(nin * C + c + 1) * P],
                                            start=(c == 0), stop=(c == C - 1 and not bias2))
                        if bias2:
                            ins = pe.matmul(dst, t["ones"][0:1, 0:P], b2[q][:], start=False, stop=True)
                    ins.then_inc(down_made[p], 1)
            loops(pe, each)

        @block.scalar
        def _(sc):
            def each(k, q, e, j):
                sc.wait_ge(came[q], n_in * (k + 1))
                for p in range(2):
                    n = (e * NBLK + 2 * j + p) * HB
                    m = e * (NBLK // 2) + j
                    for c in range(C):
                        b = c % 2
                        sc.wait_ge(made[b], n + c // 2 + 1)
                        b1 = wb[q][:, width - C + c:width - C + c + 1] if bias1 else None
                        if kind == "glu":
                            chunk_free(sc, p, m, c)
                            sc.activation(ga[b][:], ps[:, 2 * b, :], ACT.Gelu).then_inc(acted[b], 1)
                        elif kind == "gelu":
                            sc.wait_ge(down_made[p], m)
                            sc.activation(h[p][:, c, :], ps[:, 2 * b, :], ACT.Gelu, bias=b1).then_inc(h_ready[p], 1)
                        else:
                            chunk_free(sc, p, m, c)
                            sc.activation(ga[b][:], ps[:, 2 * b, :], ACT.Identity, scale=0.1 * INV_2PI, bias=t["phase"][:, c:c + 1]).then_inc(acted[b], 1)
                            sc.wait_ge(h_step[b], 3 * (n + c // 2) + 2)
                            sc.activation(sn[b][:], sn[b][:], ACT.Sin, scale=TWO_PI).then_inc(acted[b], 1)
                            sc.wait_ge(h_step[b], 3 * (n + c // 2) + 3)
                            sc.wait_ge(down_made[p], m)
                            sc.activation(h[p][:, c, :], ga[b][:], ACT.Relu, bias=b1).then_inc(h_ready[p], 1)
            loops(sc, each)

        @block.vector
        def _(v):
            def end(q):
                v.memset(spare[:], 0.0).then_inc(used[q], 1)

            def each(k, q, e, j):
                for p in range(2):
                    n = (e * NBLK + 2 * j + p) * HB
                    m = e * (NBLK // 2) + j
                    for c in range(C):
                        b = c % 2
                        if kind == "glu":
                            v.wait_ge(acted[b], n + c // 2 + 1)
                            v.wait_ge(down_made[p], m)
                            v.tensor_tensor(h[p][:, c, :], ga[b][:], ps[:, 2 * b + 1, :], ALU.mult).then_inc(h_ready[p], 1)
                        elif kind == "sine":
                            v.wait_ge(acted[b], 2 * (n + c // 2) + 1)
                            v.tensor_scalar(sn[b][:], ga[b][:], MAGIC, MAGIC, ALU.add, ALU.subtract).then_inc(h_step[b], 1)
                            v.wait_ge(h_step[b], 3 * (n + c // 2) + 1)
                            v.tensor_tensor(sn[b][:], ga[b][:], sn[b][:], ALU.subtract).then_inc(h_step[b], 1)
                            v.wait_ge(acted[b], 2 * (n + c // 2) + 2)
                            v.scalar_tensor_tensor(ga[b][:], sn[b][:], t["amp"][:, c:c + 1], ps[:, 2 * b, :], ALU.mult, ALU.add).then_inc(h_step[b], 1)
                for p in range(2):
                    m = e * (NBLK // 2) + j
                    v.wait_ge(down_made[p], m + 1)
                    v.wait_ge(residual[p], m)
                    if weight is None:
                        xb = t["x"][:, bass.ds((2 * j + p) * BLK, BLK)]
                        v.scalar_tensor_tensor(xb, ps[:, 4 + p, :], t["gate"][:, gate_at:gate_at + 1], xb, ALU.mult, ALU.add).then_inc(residual[p], 1)
                    else:
                        for i in range(TB):
                            at = (2 * j + p) * TB + i
                            xb = t["x"][:, bass.ds(at * P, P)]
                            ins = v.scalar_tensor_tensor(xb, ps[:, 4 + p, i * P:(i + 1) * P], weight[:, bass.ds(e * NT + at, 1)], xb, ALU.mult, ALU.add)
                        ins.then_inc(residual[p], 1)
            loops(v, each, end)


def route_scores(nc, t, d, stage, E, norm):
    with ExitStack() as ctx:
        s = Sems(nc, ctx, stage + "r")
        loads, steps, sq_ready, norm_ready, vec_ready, vec_turned, vec_kept = (
            s.one("loads"), s.one("steps"), s.one("sq_ready"), s.one("norm_ready"), s.one("vec_ready"), s.one("vec_turned"), s.one("vec_kept"))
        projected, kept, squared, made, out = s.two("projected"), s.two("kept"), s.two("squared"), s.two("made"), s.two("out")
        sums_ready, norms_ready = s.one("sums_ready"), s.one("norms_ready")
        ps, w = t["ps"], t["wstat"]
        M = E + norm
        G = w[:, 128:128 + E]
        raw = ctx.enter_context(nc.sbuf_tensor(stage + "_route_raw", [P, NT, M], F32))
        sqs = [ctx.enter_context(nc.sbuf_tensor(f"{stage}_route_sq{p}", [P, BLK], F32)) for p in range(2)]
        vec = ctx.enter_context(nc.sbuf_tensor(stage + "_route_vec", [E, P], F32))
        vsq = ctx.enter_context(nc.sbuf_tensor(stage + "_route_vsq", [E, P], F32))
        vn = ctx.enter_context(nc.sbuf_tensor(stage + "_route_vn", [E, 1], F32))
        temp = ctx.enter_context(nc.sbuf_tensor(stage + "_route_temp", [P, 2], F32))
        norms = t["small"][:, 0:NT]
        block = ctx.enter_context(nc.Block())

        @block.sync
        def _(sp):
            if norm:
                sp.dma_start(w[:, 0:128], d[f"{stage}_proj"]).then_inc(loads, 16)
                sp.dma_start(vec[:], d[f"{stage}_vec"]).then_inc(loads, 16)
                sp.dma_start(temp[:, 0:1], d[f"{stage}_temp"].partition_broadcast(P)).then_inc(loads, 16)
            else:
                sp.dma_start(G, d[f"{stage}_G"]).then_inc(loads, 16)

        n_loads = 48 if norm else 16

        @block.tensor
        def _(pe):
            pe.wait_ge(loads, n_loads)
            if norm:
                pe.wait_ge(vec_ready, 1)
                pe.transpose(ps[:, 6, 0:E], vec[:], t["ident"][0:E, 0:E]).then_inc(vec_turned, 1)
                pe.wait_ge(vec_kept, 1)
            with pe.Fori(0, NBLK // 2) as j:
                if norm:
                    for p in range(2):
                        pe.wait_ge(squared[p], j)
                        pe.wait_ge(kept[p], j)
                        pe.matmul(ps[:, p, :], w[:, 0:128], t["xnT"][:, bass.ds((2 * j + p) * BLK, BLK)], start=True, stop=True).then_inc(projected[p], 1)
                for p in range(2):
                    pe.wait_ge(kept[p], j + 1)
                    if norm:
                        pe.wait_ge(squared[p], j + 1)
                    pe.wait_ge(out[p], j)
                    for i in range(TB):
                        ins = pe.matmul(ps[:, 2 + p, i * M:i * M + E], t["stage"][p][:, i * P:(i + 1) * P], G, start=True, stop=True)
                        if norm:
                            ins = pe.matmul(ps[:, 2 + p, i * M + E:i * M + M], sqs[p][:, i * P:(i + 1) * P], t["ones"][:, 0:1], start=True, stop=True)
                    ins.then_inc(made[p], 1)

        @block.scalar
        def _(sc):
            with sc.Fori(0, NBLK // 2) as j:
                for p in range(2):
                    if norm:
                        sc.wait_ge(projected[p], j + 1)
                        src = ps[:, p, :]
                    else:
                        src = t["xnT"][:, bass.ds((2 * j + p) * BLK, BLK)]
                    sc.wait_ge(made[p], j)
                    sc.activation(t["stage"][p][:], src, ACT.Copy).then_inc(kept[p], 1)
                    if norm:
                        sc.activation(sqs[p][:], src, ACT.Square).then_inc(squared[p], 1)

        @block.gpsimd
        def _(pool):
            if norm:
                pool.wait_ge(sq_ready, 1)
                pool.tensor_tensor(vn[:], vn[:], t["plus_half"][0:E, 0:1], ALU.pow).then_inc(norm_ready, 1)
                pool.wait_ge(sums_ready, 1)
                pool.tensor_tensor(norms, norms, t["plus_half"][:], ALU.pow).then_inc(norms_ready, 1)

        @block.vector
        def _(v):
            step = Chain(v, steps)
            if norm:
                v.wait_ge(loads, n_loads)
                step(v.tensor_tensor(vsq[:], vec[:], vec[:], ALU.mult))
                v.tensor_reduce(vn[:], vsq[:], X, ALU.add).then_inc(sq_ready, 1)
                v.wait_ge(norm_ready, 1)
                step(v.tensor_scalar(vn[:], vn[:], 1e-12, None, ALU.max))
                step(v.reciprocal(vn[:], vn[:]))
                step(v.reciprocal(temp[:, 1:2], temp[:, 0:1]))
                v.tensor_scalar(vec[:], vec[:], vn[:], None, ALU.mult).then_inc(vec_ready, 1)
                v.wait_ge(vec_turned, 1)
                v.tensor_copy(G, ps[:, 6, 0:E]).then_inc(vec_kept, 1)
            with v.Fori(0, NBLK // 2) as j:
                for p in range(2):
                    v.wait_ge(made[p], j + 1)
                    v.tensor_copy(raw[:, bass.ds((2 * j + p) * TB, TB), :], ps[:, 2 + p, 0:TB * M].rearrange("p (i m) -> p i m", m=M)).then_inc(out[p], 1)
            v.wait_ge(out[0], NBLK // 2)
            v.wait_ge(out[1], NBLK // 2)
            if norm:
                v.tensor_copy(norms, raw[:, :, E]).then_inc(sums_ready, 1)
                v.wait_ge(norms_ready, 1)
                step(v.tensor_scalar(norms, norms, 1e-12, None, ALU.max))
                step(v.reciprocal(norms, norms))
                step(v.tensor_scalar(norms, norms, temp[:, 1:2], None, ALU.mult))
                v.tensor_tensor(t["scores"][:, :, 0:E], raw[:, :, 0:E], norms.unsqueeze(2).broadcast_to([P, NT, E]), ALU.mult)
            else:
                v.tensor_copy(t["scores"][:, :, 0:E], raw[:, :, 0:E])


def top_two(nc, t, E, gate_at):
    with ExitStack() as ctx:
        s = Sems(nc, ctx, "top2")
        steps, rank_ready, shifted, exp_ready = s.one("steps"), s.one("rank_ready"), s.one("shifted"), s.one("exp_ready")

        def sb(name, shape):
            return ctx.enter_context(nc.sbuf_tensor("top2_" + name, shape, F32))

        rank, one, two, work, best = (sb(n, [P, NT, E]) for n in ("rank", "one", "two", "work", "best"))
        v1, v2, first, p1, p2 = (sb(n, [P, NT]) for n in ("v1", "v2", "first", "p1", "p2"))
        sc_ = t["scores"][:, :, 0:E]
        wide = lambda a: a[:].unsqueeze(2).broadcast_to([P, NT, E])
        block = ctx.enter_context(nc.Block())

        @block.gpsimd
        def _(pool):
            pool.iota(rank[:], pattern=[[0, NT], [-1, E]], base=E, channel_multiplier=0, allow_small_or_imprecise_dtypes=True).then_inc(rank_ready, 1)

        @block.vector
        def _(v):
            step = Chain(v, steps)

            def pick(a, top, hot):
                step(v.tensor_reduce(top[:], a, X, ALU.max))
                step(v.tensor_tensor(work[:], a, wide(top), ALU.is_equal))
                step(v.tensor_tensor(work[:], work[:], rank[:], ALU.mult))
                step(v.tensor_reduce(first[:], work[:], X, ALU.max))
                step(v.tensor_tensor(hot[:], rank[:], wide(first), ALU.is_equal))

            v.wait_ge(rank_ready, 1)
            pick(sc_, v1, one)
            step(v.scalar_tensor_tensor(best[:], one[:], -1e30, sc_, ALU.mult, ALU.add))
            pick(best[:], v2, two)
            v.tensor_tensor(p2[:], v2[:], v1[:], ALU.subtract).then_inc(shifted, 1)
            v.wait_ge(exp_ready, 1)
            step(v.tensor_scalar(p1[:], p2[:], 1.0, None, ALU.add))
            step(v.reciprocal(p1[:], p1[:]))
            step(v.tensor_scalar(p1[:], p1[:], t["gate"][:, gate_at:gate_at + 1], None, ALU.mult))
            step(v.tensor_tensor(p2[:], p2[:], p1[:], ALU.mult))
            step(v.tensor_tensor(one[:], one[:], wide(p1), ALU.mult))
            step(v.tensor_tensor(two[:], two[:], wide(p2), ALU.mult))
            step(v.tensor_tensor(t["comb"][:, 0:E, :].rearrange("p e n -> p n e"), one[:], two[:], ALU.add))

        @block.scalar
        def _(sc):
            sc.wait_ge(shifted, 1)
            sc.activation(p2[:], p2[:], ACT.Exp).then_inc(exp_ready, 1)


def top_tokens(nc, t, E, K, gate_at):
    BITS = 30
    with ExitStack() as ctx:
        s = Sems(nc, ctx, "topk")
        steps, shifted, exp_ready, loop_steps, counted, summed = (
            s.one("steps"), s.one("shifted"), s.one("exp_ready"), s.one("loop_steps"), s.one("counted"), s.one("summed"))
        tri_steps = s.one("tri_steps")

        def sb(name, shape, dt=F32):
            return ctx.enter_context(nc.sbuf_tensor("topk_" + name, shape, dt))

        tri = sb("tri", [P, P])
        score, work, sel, before = (sb(n, [P, E, NT]) for n in ("score", "work", "sel", "before"))
        reset = sb("reset", [P, E, NT])
        top, total = sb("top", [P, NT]), sb("total", [P, NT])
        thr, cand, inc = (sb(n, [P, E], I32) for n in ("thr", "cand", "inc"))
        bit, biti = sb("bit", [P, 1]), sb("biti", [P, 1], I32)
        count, enough = sb("count", [P, E]), sb("enough", [P, E])
        ps = t["ps"]
        raw = t["scores"][:, :, 0:E]
        by_tile = lambda a: a[:].rearrange("p e n -> p n e")
        over_e = lambda a: a[:].unsqueeze(2).broadcast_to([P, NT, E])
        over_n = lambda a: a.unsqueeze(2).broadcast_to([P, E, NT])
        block = ctx.enter_context(nc.Block())
        LOOP = 7

        @block.gpsimd
        def _(pool):
            step = Chain(pool, tri_steps)
            step(pool.memset(tri[:], 1.0))
            step(pool.affine_select(out=tri[:], in_=tri[:], compare_op=ALU.is_ge, fill=0.0, base=-1, pattern=[[1, P]], channel_multiplier=-1))
            step(pool.memset(reset[:], 1.0))
            step(pool.memset(reset[:, :, 0:1], 0.0))
            step(pool.memset(thr[:], 0))
            step(pool.memset(bit[:], float(2 ** (BITS - 1))))

        @block.scalar
        def _(sc):
            sc.wait_ge(shifted, 1)
            sc.activation(score[:], score[:], ACT.Exp).then_inc(exp_ready, 1)

        @block.tensor
        def _(pe):
            with pe.Fori(0, BITS) as j:
                pe.wait_ge(counted, j + 1)
                pe.matmul(ps[:, 0, 0:E], t["ones"][:], count[:], start=True, stop=True).then_inc(summed, 1)
            pe.wait_ge(counted, BITS + 1)
            pe.matmul(ps[:, 0, 0:E], t["ones"][:], count[:], start=True, stop=True).then_inc(summed, 1)
            flat = work[:].rearrange("p e n -> p (e n)")
            pe.wait_ge(counted, BITS + 2)
            pe.matmul(ps[:, 1, :], tri[:], flat, start=True, stop=True).then_inc(summed, 1)
            pe.matmul(ps[:, 2, :], t["ones"][:], flat, start=True, stop=True).then_inc(summed, 1)

        @block.vector
        def _(v):
            step = Chain(v, steps)
            step(v.tensor_reduce(top[:], raw, X, ALU.max))
            v.tensor_tensor(by_tile(score), raw, over_e(top), ALU.subtract).then_inc(shifted, 1)
            v.wait_ge(exp_ready, 1)
            step(v.tensor_reduce(total[:], by_tile(score), X, ALU.add))
            step(v.reciprocal(total[:], total[:]))
            step(v.tensor_tensor(by_tile(score), by_tile(score), over_e(total), ALU.mult))
            v.wait_ge(tri_steps, 6)
            with v.Fori(0, BITS) as j:
                def did(ins, n):
                    ins.then_inc(loop_steps, 1)
                    v.wait_ge(loop_steps, j * LOOP + n)

                did(v.tensor_copy(biti[:], bit[:]), 1)
                did(v.tensor_tensor(cand[:], thr[:], biti[:].broadcast_to([P, E]), ALU.bitwise_or), 2)
                did(v.tensor_tensor(work[:], score[:], over_n(cand[:].bitcast(F32)), ALU.is_ge), 3)
                v.tensor_reduce(count[:], work[:], X, ALU.add).then_inc(counted, 1)
                v.wait_ge(summed, j + 1)
                did(v.tensor_scalar(enough[:], ps[:, 0, 0:E], float(K), None, ALU.is_ge), 4)
                did(v.tensor_scalar(inc[:], enough[:], bit[:], None, ALU.mult), 5)
                did(v.tensor_tensor(thr[:], thr[:], inc[:], ALU.bitwise_or), 6)
                did(v.tensor_scalar(bit[:], bit[:], 0.5, None, ALU.mult), 7)
            limit = over_n(thr[:].bitcast(F32))
            step(v.tensor_tensor(sel[:], score[:], limit, ALU.is_gt))
            v.tensor_reduce(count[:], sel[:], X, ALU.add).then_inc(counted, 1)
            v.wait_ge(counted, BITS + 1)
            v.tensor_tensor(work[:], score[:], limit, ALU.is_equal).then_inc(counted, 1)
            v.wait_ge(summed, BITS + 1)
            step(v.tensor_scalar(enough[:], ps[:, 0, 0:E], -1.0, float(K), ALU.mult, ALU.add))
            v.wait_ge(summed, BITS + 3)
            flat = lambda a: a[:].rearrange("p e n -> p (e n)")
            step(v.tensor_tensor_scan(flat(before), flat(reset), ps[:, 2, :], 0.0, ALU.mult, ALU.add))
            step(v.tensor_tensor(flat(before), flat(before), ps[:, 2, :], ALU.subtract))
            step(v.tensor_tensor(flat(before), flat(before), ps[:, 1, :], ALU.add))
            step(v.tensor_tensor(before[:], before[:], over_n(enough[:]), ALU.is_lt))
            step(v.tensor_tensor(before[:], before[:], work[:], ALU.mult))
            step(v.tensor_tensor(sel[:], sel[:], before[:], ALU.add))
            step(v.tensor_tensor(sel[:], sel[:], score[:], ALU.mult))
            step(v.tensor_scalar(t["comb"][:, 0:E, :], sel[:], t["gate"][:, gate_at:gate_at + 1], None, ALU.mult))


def sine_constants(nc, t, d, C=4):
    with ExitStack() as ctx:
        s = Sems(nc, ctx, "phase")
        loads, steps, angles, sines = s.one("loads"), s.one("steps"), s.one("angles"), s.one("sines")

        def sb(name, n):
            return ctx.enter_context(nc.sbuf_tensor("phase_" + name, [P, n], F32))

        inp, turns, whole, sc2, tmp = sb("inp", 4 * C), sb("turns", 2 * C), sb("whole", 2 * C), sb("sc2", 2 * C), sb("tmp", C)
        theta, wr, wi, b1 = (inp[:, k * C:(k + 1) * C] for k in range(4))
        block = ctx.enter_context(nc.Block())

        @block.sync
        def _(sp):
            sp.dma_start(inp[:], d["l2f_phase"]).then_inc(loads, 16)

        @block.vector
        def _(v):
            step = Chain(v, steps)
            v.wait_ge(loads, 16)
            step(v.tensor_scalar(turns[:, 0:C], theta, INV_2PI, None, ALU.mult))
            step(v.tensor_scalar(turns[:, C:2 * C], turns[:, 0:C], 0.25, None, ALU.add))
            step(v.tensor_scalar(whole[:], turns[:], MAGIC, MAGIC, ALU.add, ALU.subtract))
            k0 = whole[:, 0:C]
            step(v.scalar_tensor_tensor(tmp[:], k0, -6.28125, theta, ALU.mult, ALU.add))
            step(v.scalar_tensor_tensor(tmp[:], k0, -0.0019350051879882812, tmp[:], ALU.mult, ALU.add))
            step(v.scalar_tensor_tensor(tmp[:], k0, -3.019916050561733e-07, tmp[:], ALU.mult, ALU.add))
            step(v.tensor_scalar(turns[:, 0:C], tmp[:], INV_2PI, None, ALU.mult))
            step(v.tensor_scalar(turns[:, C:2 * C], turns[:, 0:C], 0.25, None, ALU.add))
            step(v.scalar_tensor_tensor(t["phase"][:], b1, 0.1 * INV_2PI, turns[:, 0:C], ALU.mult, ALU.add))
            step(v.tensor_scalar(whole[:], turns[:], MAGIC, MAGIC, ALU.add, ALU.subtract))
            v.tensor_tensor(turns[:], turns[:], whole[:], ALU.subtract).then_inc(angles, 1)
            v.wait_ge(sines, 1)
            step(v.tensor_tensor(tmp[:], sc2[:, 0:C], wi, ALU.mult))
            step(v.tensor_tensor(sc2[:, C:2 * C], sc2[:, C:2 * C], wr, ALU.mult))
            step(v.tensor_tensor(tmp[:], tmp[:], sc2[:, C:2 * C], ALU.add))
            step(v.scalar_tensor_tensor(t["amp"][:], tmp[:], 0.1, wi, ALU.mult, ALU.mult))

        @block.scalar
        def _(sc):
            sc.wait_ge(angles, 1)
            sc.activation(sc2[:], turns[:], ACT.Sin, scale=TWO_PI).then_inc(sines, 1)



def build(nc, d, out, stages=range(8)):
    with ExitStack() as ctx:
        t = {}

        def sb(name, shape, dt=F32):
            t[name] = ctx.enter_context(nc.sbuf_tensor(f"sb_{name}", shape, dt))

        def sb2(name, shape, dt=F32):
            t[name] = [ctx.enter_context(nc.sbuf_tensor(f"sb_{name}{p}", shape, dt)) for p in range(2)]

        sb("x", [P, NT * D])
        sb("xc", [P, NT * D])
        sb("xnT", [P, NTOK])
        sb("ctxT", [P, NT * KEYS])
        sb("graw", [P, 8])
        sb("gate", [P, 8])
        sb("ident", [P, P])
        sb("identb", [P, P], BF16)
        sb("ones", [P, P])
        sb("minus_half", [P, 256])
        sb("plus_half", [P, 32])
        sb("headmask", [P, HEADS])
        sb("blockones", [P, P])
        sb("onespad", [KEYS, HG, 32])
        sb("small", [P, 256])
        sb("eps", [P, 1])
        sb("phase", [P, 4])
        sb("amp", [P, 4])
        sb("row_any", [P, NT])
        sb("wstat", [P, 512])
        sb("cols", [P, 16])
        sb("row", [1, 2 * D])
        sb2("stage", [P, BLK])
        sb2("Vpad", [KEYS, HEADS, 32])
        sb2("maski", [P, 8 * KEYS], I32)
        sb("maskf", [P, 8 * KEYS])
        sb2("maskb", [P, KEYS], BF16)
        t["ps"] = ctx.enter_context(nc.psum_tensor("ps", [P, 8, 512], F32))

        def attention_stage(*a, **k):
            with ExitStack() as own:
                u = dict(t)
                for name, shape in (("qk", [P, P + KEYS]), ("kblk", [P, HEADS * KEYS]), ("prob", [P, HEADS, KEYS]),
                                    ("pt", [KEYS, HG, GROUPS, P]), ("oT", [P, P]), ("rden", [P, HEADS]), ("rowmax", [P, HEADS]),
                                    ("rowsum", [P, HEADS])):
                    u[name] = [own.enter_context(nc.sbuf_tensor(f"{a[0]}_{name}{p}", shape, F32)) for p in range(2)]
                attention(nc, u, d, *a, **k)

        def routed(stage, E, gate_at, select, norm, *a, **kw):
            with ExitStack() as own:
                u = dict(t)
                u["scores"] = own.enter_context(nc.sbuf_tensor(stage + "_route_scores", [P, NT, E], F32))
                u["comb"] = own.enter_context(nc.sbuf_tensor(stage + "_route_comb", [P, E, NT], F32))
                route_scores(nc, u, d, stage, E, norm)
                select(u)
                experts(nc, u, d, stage, E, *a, weight=u["comb"][:].rearrange("p e n -> p (e n)"), **kw)

        constants(nc, t, d)
        if 0 in stages:
            layernorm(nc, t, "ln0")
            concat_linear(nc, t, d)
        if 1 in stages:
            layernorm(nc, t, "ln1")
            quantised_ffn(nc, t, d, 4)
        if 2 in stages:
            layernorm(nc, t, "ln2")
            attention_stage("l1x", 1, bias_qk=True, bias_v=True, bias_out=True)
        if 3 in stages:
            layernorm(nc, t, "ln3")
            routed("l1f", 8, 5, lambda u: top_two(nc, u, 8, 5), True, 4, "gelu", bias1=True, bias2=True)
        if 4 in stages:
            layernorm(nc, t, "ln4")
            with ExitStack() as own:
                t["kT"] = own.enter_context(nc.sbuf_tensor("sb_kT", [P, NT * KEYS], F32))
                rms_qk(nc, t, d, "l2x")
                attention_stage("l2x", 2, ready_qk=True)
        if 5 in stages:
            layernorm(nc, t, "ln5")
            sine_constants(nc, t, d)
            experts(nc, t, d, "l2f", 1, 4, "sine", gate_at=6, bias1=True, bias2=True)
        if 6 in stages:
            mask_rows(nc, t, d)
            layernorm(nc, t, "ln6", row_any=t["row_any"][:])
            attention_stage("l3x", 3, bias_out=True, masked=True)
        if 7 in stages:
            layernorm(nc, t, "ln7")
            routed("l3f", 16, 7, lambda u: top_tokens(nc, u, 16, NTOK * 2 // 16, 7), False, 4, "glu")
            experts(nc, t, d, "l3s", 1, 2, "glu", gate_at=7)
        with ExitStack() as c2:
            stored = c2.enter_context(nc.semaphore("stored"))
            block = c2.enter_context(nc.Block())

            @block.sync
            def _(sp):
                sp.dma_start(out, t["x"][:]).then_inc(stored, 16)
                sp.wait_ge(stored, 16)


def laid_out(i):
    import numpy as np
    a = {k: np.asarray(v) for k, v in i.items()}
    f = {}
    f["x"] = a["x"].transpose(1, 0, 2).reshape(P, NT * D)
    f["ctxT"] = a["ctx_1024"].transpose(2, 0, 1).reshape(D, NT * KEYS)
    f["mask"] = a["mask_BxSxS2_if1"].transpose(1, 0, 2).reshape(P, NT * KEYS)
    f["g_xattn"], f["g_ffn"] = a["g_xattn"], a["g_ffn"]
    f["l0_WT"] = a["L0_xattn_W"].T.reshape(2, D, D).transpose(1, 0, 2).reshape(D, 2 * D)
    f["l0_b"] = a["L0_xattn_b"][None]
    w, b = a["L1_xattn_in_proj_weight"], a["L1_xattn_in_proj_bias"]
    f["l1x_W"] = np.concatenate([w.T, a["L1_xattn_out_w"].T], 1)
    f["l1x_bqk"] = b[:2 * D].reshape(2, D).T
    f["l1x_bv"], f["l1x_bo"] = b[None, 2 * D:], a["L1_xattn_out_b"][None]
    f["l2x_W"] = np.concatenate([a["L2_xattn_Wq"], a["L2_xattn_Wkv"], a["L2_xattn_Wproj"]], 1)
    f["l2x_gamma"] = np.stack([np.tile(a["L2_xattn_q_gamma"], HEADS), np.tile(a["L2_xattn_k_gamma"], HEADS)], 1)
    f["l3x_W"] = np.concatenate([a[f"L3_xattn_W{c}"].T for c in "qkvo"], 1)
    f["l3x_bo"] = a["L3_xattn_bo"][None]
    def rows(w):
        E, F, _ = w.shape
        return w.reshape(E, F // P, P, D).transpose(0, 2, 1, 3).reshape(E, P, F // P * D)

    def column(b):
        E, F = b.shape
        return b.reshape(E, F // P, P).transpose(0, 2, 1)

    up, gate, down = a["L0_ffn_w_up"], a["L0_ffn_w_gate"], a["L0_ffn_w_down"]
    f["l0f_W"] = np.concatenate([rows(up[None])[0], rows(gate[None])[0], down], 1)
    f["l1f_proj"], f["l1f_vec"], f["l1f_temp"] = a["L1_ffn_Wp"].T, a["L1_ffn_sim_matrix"], a["L1_ffn_temperature"].reshape(1)
    f["l1f_W"] = np.concatenate([a["L1_ffn_W1"], rows(a["L1_ffn_W2"]), column(a["L1_ffn_b1"])], 2)
    f["l1f_b2"] = a["L1_ffn_b2"]
    f["l2f_W"] = np.concatenate([a["L2_ffn_W1"][None], rows(a["L2_ffn_W2"][None]), column(a["L2_ffn_b1"][None])], 2)
    f["l2f_b2"] = a["L2_ffn_b2"][None]
    f["l2f_phase"] = np.concatenate([column(a[f"L2_ffn_{n}"][None])[0] for n in ("quantum_phases", "quantum_weights_real", "quantum_weights_imag", "b1")], 1)
    f["l3f_G"] = a["L3_ffn_gate_w"].T
    turn = lambda w: w.transpose(0, 2, 1)
    f["l3f_W"] = np.concatenate([turn(a["L3_ffn_Wg"]), turn(a["L3_ffn_Wu"]), rows(turn(a["L3_ffn_Wd"]))], 2)
    f["l3s_W"] = np.concatenate([turn(a["L3_ffn_Sg"][None]), turn(a["L3_ffn_Su"][None]), rows(turn(a["L3_ffn_Sd"][None]))], 2)
    return {k: np.ascontiguousarray(v) for k, v in f.items()}


def kernel(**inputs):
    import concourse.bacc as bacc
    from concourse.bass_utils import run_bass_kernel_spmd

    nc = bacc.Bacc("TRN2", target_bir_lowering=False, num_devices=1)
    arrays = laid_out(inputs)
    d = {k: nc.dram_tensor(k, v.shape, mybir.dt.from_np(v.dtype), kind="ExternalInput").ap() for k, v in arrays.items()}
    out = nc.dram_tensor("out", (P, NT * D), F32, kind="ExternalOutput").ap()
    build(nc, d, out)
    r = run_bass_kernel_spmd(nc, [arrays], core_ids=[0]).results[0]["out"]
    return r.reshape(P, NT, D).transpose(1, 0, 2)
```

```python
from contextlib import ExitStack

import concourse.bass as bass
from concourse import mybir

F32 = mybir.dt.float32
BF16 = mybir.dt.bfloat16
I32 = mybir.dt.int32
ALU = mybir.AluOpType
ACT = mybir.ActivationFunctionType
X = mybir.AxisListType.X
RMAX = bass.bass_isa.ReduceOp.max

P = 128
D = 128
NT = 32
KEYS = 77
HEADS = 16
HD = D // HEADS
GROUPS = 4
HG = HEADS // GROUPS
NTOK = NT * P
BLK = 512
NBLK = NTOK // BLK
TB = BLK // P
MAGIC = 12582912.0
NEG = -1e9
S_BANKS = [(0, 6), (6, 6), (12, 4)]
INV_2PI = 0.15915494309189535
TWO_PI = 6.283185


def act(eng, out, in_, func, **kw):
    return eng.activation(out, in_, func, **kw)


class Sems:

    def __init__(self, nc, ctx, stage):
        self.nc, self.stage, self.made = nc, stage, []
        ctx.callback(self.clear)

    def one(self, name):
        self.made.append(self.nc.alloc_semaphore(f"{self.stage}_{name}"))
        return self.made[-1]

    def two(self, name):
        return [self.one(f"{name}{p}") for p in range(2)]

    def clear(self):
        self.nc.clear_and_free_semaphores(self.made)
        self.nc.all_engine_barrier()


class Chain:

    def __init__(self, eng, sem):
        self.eng, self.sem, self.n = eng, sem, 0

    def __call__(self, ins):
        ins.then_inc(self.sem, 1)
        self.n += 1
        self.eng.wait_ge(self.sem, self.n)


def constants(nc, t, d):
    with ExitStack() as ctx:
        s = Sems(nc, ctx, "const")
        ident0, ident1, masks, ones_ready = s.one("ident0"), s.one("ident1"), s.one("masks"), s.one("ones_ready")
        loads, gates = s.one("loads"), s.one("gates")
        pool_steps = s.one("pool_steps")
        block = ctx.enter_context(nc.Block())

        @block.sync
        def _(sp):
            sp.dma_start(t["x"][:], d["x"]).then_inc(loads, 16)
            sp.dma_start(t["ctxT"][:], d["ctxT"]).then_inc(loads, 16)
            sp.dma_start(t["graw"][:, 0:4], d["g_xattn"].partition_broadcast(P)).then_inc(loads, 16)
            sp.dma_start(t["graw"][:, 4:8], d["g_ffn"].partition_broadcast(P)).then_inc(loads, 16)
            sp.wait_ge(loads, 64)

        @block.gpsimd
        def _(pool):
            step = Chain(pool, pool_steps)
            step(pool.memset(t["ident"][:], 0.0))
            step(pool.affine_select(out=t["ident"][:], in_=t["ident"][:], compare_op=ALU.not_equal, fill=1.0,
                                    base=0, pattern=[[-1, P]], channel_multiplier=1))
            step(pool.tensor_copy(t["identb"][:], t["ident"][:]))
            step(pool.memset(t["ones"][:], 1.0))
            step(pool.memset(t["headmask"][:], 1.0))
            step(pool.affine_select(out=t["headmask"][:], in_=t["headmask"][:], compare_op=ALU.is_ge, fill=0.0,
                                    base=0, pattern=[[-HD, HEADS]], channel_multiplier=1))
            step(pool.affine_select(out=t["headmask"][:], in_=t["headmask"][:], compare_op=ALU.is_ge, fill=0.0,
                                    base=HD - 1, pattern=[[HD, HEADS]], channel_multiplier=-1))
            step(pool.tensor_scalar(t["blockones"][:].rearrange("p (h d) -> p h d", d=HD),
                                    t["headmask"][:].unsqueeze(2).broadcast_to([P, HEADS, HD]),
                                    1.0 / HD, None, ALU.mult))
            step(pool.memset(t["onespad"][:], 0.0))
            for i in range(HG):
                step(pool.memset(t["onespad"][:, i, HD * i:HD * i + HD], 1.0))
            step(pool.memset(t["minus_half"][:], -0.5))
            step(pool.memset(t["plus_half"][:], 0.5))
            step(pool.memset(t["eps"][:], 1e-6))
            for b in range(2):
                step(pool.memset(t["Vpad"][b][:], 0.0))
            step(pool.memset(t["tri"][:], 1.0))
            step(pool.affine_select(out=t["tri"][:], in_=t["tri"][:], compare_op=ALU.is_ge, fill=0.0, base=-1, pattern=[[1, P]], channel_multiplier=-1))

        @block.scalar
        def _(sc):
            sc.wait_ge(loads, 64)
            sc.activation(t["gate"][:], t["graw"][:], ACT.Tanh).then_inc(gates, 1)


def layernorm(nc, t, stage, row_any=None):
    with ExitStack() as ctx:
        s = Sems(nc, ctx, stage)
        steps, centred, squared, var_ready, rstd_ready, scaled, turned, kept = (
            s.one("steps"), s.one("centred"), s.one("squared"), s.one("var_ready"), s.one("rstd_ready"),
            s.two("scaled"), s.two("turned"), s.two("kept"))
        ps = t["ps"]
        small = t["small"]
        mean, var, rstd = small[:, 0:NT], small[:, NT:2 * NT], small[:, 2 * NT:3 * NT]
        x3 = t["x"][:].rearrange("p (n d) -> p n d", d=D)
        xc3 = t["xc"][:].rearrange("p (n d) -> p n d", d=D)
        wide = lambda a: a.unsqueeze(2).broadcast_to([P, NT, D])
        block = ctx.enter_context(nc.Block())

        @block.vector
        def _(v):
            step = Chain(v, steps)
            step(v.tensor_reduce(mean, x3, X, ALU.add))
            step(v.tensor_scalar(mean, mean, 1.0 / D, None, ALU.mult))
            v.tensor_tensor(xc3, x3, wide(mean), ALU.subtract).then_inc(centred, 1)
            v.wait_ge(squared, 1)
            step(v.tensor_reduce(var, t["xnT"][:].rearrange("p (n d) -> p n d", d=D), X, ALU.add))
            v.tensor_scalar(var, var, 1.0 / D, 1e-5, ALU.mult, ALU.add).then_inc(var_ready, 1)
            v.wait_ge(rstd_ready, 1)
            if row_any is not None:
                step(v.tensor_tensor(rstd, rstd, row_any, ALU.mult))
            with v.Fori(0, NBLK // 2) as j:
                for p in range(2):
                    v.wait_ge(turned[p], j)
                    v.tensor_tensor(
                        t["stage"][p][:].rearrange("p (n d) -> p n d", d=D),
                        t["xc"][:, bass.ds((2 * j + p) * BLK, BLK)].rearrange("p (n d) -> p n d", d=D),
                        small[:, bass.ds(2 * NT + (2 * j + p) * TB, TB)].unsqueeze(2).broadcast_to([P, TB, D]),
                        ALU.mult).then_inc(scaled[p], 1)

        @block.gpsimd
        def _(pool):
            pool.wait_ge(var_ready, 1)
            pool.tensor_tensor(rstd, var, t["minus_half"][:, 0:NT], ALU.pow).then_inc(rstd_ready, 1)

        @block.tensor
        def _(pe):
            with pe.Fori(0, NBLK // 2) as j:
                for p in range(2):
                    pe.wait_ge(scaled[p], j + 1)
                    pe.wait_ge(kept[p], j)
                    for i in range(TB):
                        ins = pe.transpose(ps[:, p, i * P:i * P + P], t["stage"][p][:, i * P:i * P + P], t["ident"][:])
                    ins.then_inc(turned[p], 1)

        @block.scalar
        def _(sc):
            sc.wait_ge(centred, 1)
            sc.activation(t["xnT"][:], t["xc"][:], ACT.Square).then_inc(squared, 1)
            sc.wait_ge(rstd_ready, 1)
            with sc.Fori(0, NBLK // 2) as j:
                for p in range(2):
                    sc.wait_ge(turned[p], j + 1)
                    sc.activation(t["xnT"][:, bass.ds((2 * j + p) * BLK, BLK)], ps[:, p, :], ACT.Copy).then_inc(kept[p], 1)


def concat_linear(nc, t, d):
    with ExitStack() as ctx:
        s = Sems(nc, ctx, "l0x")
        loads, sum_ready, mean_ready, linear, residual, feat = (
            s.one("loads"), s.one("sum_ready"), s.two("mean_ready"), s.two("linear"), s.two("residual"), s.two("feat"))
        ps = t["ps"]
        w = t["wstat"]
        block = ctx.enter_context(nc.Block())

        @block.sync
        def _(sp):
            sp.dma_start(w[:, 0:256], d["l0_WT"]).then_inc(loads, 16)
            sp.dma_start(t["row"][:, 0:D], d["l0_b"]).then_inc(loads, 16)

        @block.vector
        def _(v):
            ctx_sum = t["small"][:, 0:NT]
            v.tensor_reduce(ctx_sum, t["ctxT"][:].rearrange("p (n k) -> p n k", k=KEYS), X, ALU.add).then_inc(sum_ready, 1)
            v.wait_ge(sum_ready, 1)
            with v.Fori(0, NT // 2) as j:
                for p in range(2):
                    v.wait_ge(linear[p], j)
                    v.tensor_scalar(t["stage"][p][:, 0:P], t["small"][:, bass.ds(2 * j + p, 1)].broadcast_to([P, P]),
                                    1.0 / KEYS, None, ALU.mult).then_inc(mean_ready[p], 1)
                    v.tensor_copy(t["stage"][p][:, P:2 * P], t["xnT"][:, bass.ds((2 * j + p) * P, P)]).then_inc(feat[p], 1)
                for p in range(2):
                    v.wait_ge(linear[p], j + 1)
                    xb = t["x"][:, bass.ds((2 * j + p) * P, P)]
                    v.scalar_tensor_tensor(xb, ps[:, p, 0:D], t["gate"][:, 0:1], xb, ALU.mult, ALU.add).then_inc(residual[p], 1)

        @block.tensor
        def _(pe):
            pe.wait_ge(loads, 32)
            with pe.Fori(0, NT // 2) as j:
                for p in range(2):
                    pe.wait_ge(residual[p], j)
                    pe.wait_ge(mean_ready[p], j + 1)
                    pe.wait_ge(feat[p], j + 1)
                    pe.matmul(ps[:, p, 0:D], t["stage"][p][:, P:2 * P], w[:, 0:128], start=True, stop=False)
                    pe.matmul(ps[:, p, 0:D], t["stage"][p][:, 0:P], w[:, 128:256], start=False, stop=False)
                    pe.matmul(ps[:, p, 0:D], t["ones"][0:1, 0:P], t["row"][0:1, 0:D], start=False, stop=True).then_inc(linear[p], 1)


def mask_rows(nc, t, d):
    with ExitStack() as ctx:
        s = Sems(nc, ctx, "rows")
        came, read, steps = s.two("came"), s.two("read"), s.one("steps")
        block = ctx.enter_context(nc.Block())
        n = 8

        @block.sync
        def _(sp):
            for c in range(NT // n):
                if c >= 2:
                    sp.wait_ge(read[c % 2], c // 2)
                sp.dma_start(t["maski"][c % 2][:], d["mask"][:, c * n * KEYS:(c + 1) * n * KEYS]).then_inc(came[c % 2], 16)

        @block.vector
        def _(v):
            step = Chain(v, steps)
            for c in range(NT // n):
                v.wait_ge(came[c % 2], 16 * (c // 2 + 1))
                nz = t["maskf"][:, 0:n * KEYS]
                v.tensor_scalar(nz, t["maski"][c % 2][:], 0.0, None, ALU.not_equal).then_inc(read[c % 2], 1)
                v.wait_ge(read[c % 2], c // 2 + 1)
                step(v.tensor_reduce(t["row_any"][:, c * n:c * n + n], nz.rearrange("p (n k) -> p n k", k=KEYS), X, ALU.max))

def rms_qk(nc, t, d, layer):
    KB = 352
    assert KB * 7 == NT * KEYS
    with ExitStack() as ctx:
        s = Sems(nc, ctx, layer + "n")
        loads, made, squared, means, rooted, inverted, normed = (
            s.one("loads"), s.one("made"), s.one("squared"), s.one("means"), s.one("rooted"), s.one("inverted"), s.one("normed"))
        ps, w = t["ps"], t["wstat"]
        sq, root, inv = t["stage"][0], t["stage"][1], t["xc"]
        parts = [(t["xnT"], t["xnT"], w[:, 0:128], t["cols"][:, 0:1], BLK, NBLK, 0),
                 (t["ctxT"], t["kT"], w[:, 128:256], t["cols"][:, 1:2], KB, 7, NBLK)]
        block = ctx.enter_context(nc.Block())

        @block.sync
        def _(sp):
            sp.dma_start(w[:, 0:256], d[f"{layer}_W"][:, 0:256]).then_inc(loads, 16)
            sp.dma_start(t["cols"][:, 0:2], d[f"{layer}_gamma"]).then_inc(loads, 16)

        @block.tensor
        def _(pe):
            pe.wait_ge(loads, 32)
            for src, dst, wt, gamma, n, blocks, before in parts:
                with pe.Fori(0, blocks) as j:
                    pe.wait_ge(normed, before + j)
                    pe.matmul(ps[:, 0, 0:n], wt, src[:, bass.ds(j * n, n)], start=True, stop=True).then_inc(made, 1)
                    pe.wait_ge(squared, before + j + 1)
                    pe.matmul(ps[:, 1, 0:n], t["blockones"][:], sq[:, 0:n], start=True, stop=True).then_inc(means, 1)

        @block.scalar
        def _(sc):
            for src, dst, wt, gamma, n, blocks, before in parts:
                with sc.Fori(0, blocks) as j:
                    sc.wait_ge(made, before + j + 1)
                    sc.activation(sq[:, 0:n], ps[:, 0, 0:n], ACT.Square).then_inc(squared, 1)
                    sc.wait_ge(means, before + j + 1)
                    sc.activation(root[:, 0:n], ps[:, 1, 0:n], ACT.Sqrt, bias=t["eps"][:]).then_inc(rooted, 1)

        @block.vector
        def _(v):
            v.wait_ge(loads, 32)
            for src, dst, wt, gamma, n, blocks, before in parts:
                with v.Fori(0, blocks) as j:
                    v.wait_ge(rooted, before + j + 1)
                    v.wait_ge(normed, before + j)
                    v.reciprocal(inv[:, 0:n], root[:, 0:n]).then_inc(inverted, 1)
                    v.wait_ge(inverted, before + j + 1)
                    v.scalar_tensor_tensor(dst[:, bass.ds(j * n, n)], ps[:, 0, 0:n], gamma, inv[:, 0:n], ALU.mult, ALU.mult).then_inc(normed, 1)


def attention(nc, t, d, layer, gate_at, bias_qk=False, bias_v=False, bias_out=False, ready_qk=False, masked=False):
    with ExitStack() as ctx:
        s = Sems(nc, ctx, layer)
        loads = s.one("loads")
        ctx_staged, qk_made, qk_kept, v_made, v_kept = (
            s.two("ctx_staged"), s.two("qk_made"), s.two("qk_kept"), s.two("v_made"), s.two("v_kept"))
        kblk_ready, scores_ready, max_ready, shifted, exp_ready = (
            s.two("kblk_ready"), s.two("scores_ready"), s.two("max_ready"), s.two("shifted"), s.two("exp_ready"))
        sum_ready, recip_ready, prob_ready = s.two("sum_ready"), s.two("recip_ready"), s.two("prob_ready")
        turned, turned_kept, heads_made, heads_kept, out_made, residual = (
            s.two("turned"), s.two("turned_kept"), s.two("heads_made"), s.two("heads_kept"), s.two("out_made"),
            s.two("residual"))
        if masked:
            mask_came, mask_made, mask_step = s.two("mask_came"), s.two("mask_made"), s.two("mask_step")
        ps = t["ps"]
        w = t["wstat"]
        VB = ps[0:KEYS, 1, 128:128 + D]
        OUT = ps[:, 1, 0:D]
        OT = ps[:, 7, 0:P]
        qk, kblk, prob, pt, vpad, oT, rden = (t[n] for n in ("qk", "kblk", "prob", "pt", "Vpad", "oT", "rden"))
        scale = float(HD) ** -0.5

        def other(j, p):
            return 1 - p, j + p

        def skip(j, p):
            pass

        def at(n):
            return n // 2, n % 2

        def run(eng, project, score, finish, weigh, output):
            project(0, 0)
            project(0, 1)
            score(0, 0)
            finish(0, 0)
            project(1, 0)
            score(0, 1)
            with eng.Fori(0, NT // 2 - 2) as j:
                for p in range(2):
                    weigh(j, p)
                    finish(j + p, 1 - p)
                    project(j + 1 + p, 1 - p)
                    score(j + 1, p)
                    output(j, p)
            for n in range(NT - 4, NT):
                weigh(*at(n))
                if n + 1 < NT:
                    finish(*at(n + 1))
                if n + 3 < NT:
                    project(*at(n + 3))
                if n + 2 < NT:
                    score(*at(n + 2))
                output(*at(n))

        block = ctx.enter_context(nc.Block())

        @block.sync
        def _(sp):
            n = 16
            sp.dma_start(w[:, 0:512], d[f"{layer}_W"]).then_inc(loads, n)
            if bias_qk:
                sp.dma_start(t["cols"][:, 0:2], d[f"{layer}_bqk"]).then_inc(loads, n)
            if bias_v:
                sp.dma_start(t["row"][:, 0:D], d[f"{layer}_bv"]).then_inc(loads, n)
            if bias_out:
                sp.dma_start(t["row"][:, D:2 * D], d[f"{layer}_bo"]).then_inc(loads, n)
            if masked:
                with sp.Fori(0, NT // 2) as j:
                    for p in range(2):
                        sp.wait_ge(mask_made[p], j)
                        sp.dma_start(t["maski"][p][:, 0:KEYS], d["mask"][:, bass.ds((2 * j + p) * KEYS, KEYS)]).then_inc(mask_came[p], 16)

        n_loads = 16 * (1 + bias_qk + bias_v + bias_out)

        def tile_cols(a, j, p, width):
            return a[:, bass.ds((2 * j + p) * width, width)]

        @block.gpsimd
        def _(pool):
            def project(j, p):
                pool.wait_ge(qk_kept[p], 2 * j + 2)
                pool.wait_ge(scores_ready[p], j)
                pool.tensor_tensor(kblk[p][:].rearrange("p (h k) -> p h k", k=KEYS),
                                   qk[p][:, P:P + KEYS].unsqueeze(1).broadcast_to([P, HEADS, KEYS]),
                                   t["headmask"][:].unsqueeze(2).broadcast_to([P, HEADS, KEYS]),
                                   ALU.mult).then_inc(kblk_ready[p], 1)

            def stage(j, p):
                pool.wait_ge(v_made[p], j)
                pool.tensor_copy(t["stage"][p][:, 0:KEYS], tile_cols(t["ctxT"], j, p, KEYS)).then_inc(ctx_staged[p], 1)

            def finish(j, p):
                pool.wait_ge(recip_ready[p], j + 1)
                by_round = prob[p][:].rearrange("p (g r) k -> p g r k", r=HG)
                recip = rden[p][:].rearrange("p (g r) -> p g r", r=HG)
                for r in range(0, HG, 2):
                    pool.tensor_tensor(by_round[:, :, r:r + 2, :], by_round[:, :, r:r + 2, :],
                                       recip[:, :, r:r + 2].unsqueeze(3).broadcast_to([P, GROUPS, 2, KEYS]),
                                       ALU.mult).then_inc(prob_ready[p], 1)

            def weigh(j, p):
                if not isinstance(j, int) or 2 * j + p + 2 < NT:
                    stage(j + 1, p)

            stage(0, 0)
            stage(0, 1)
            run(pool, project, skip, finish, weigh, skip)

        @block.tensor
        def _(pe):
            pe.wait_ge(loads, n_loads)

            def project(j, p):
                o, n = other(j, p)
                if not ready_qk:
                    pe.wait_ge(qk_kept[o], 2 * n)
                    pe.matmul(ps[:, 0, 0:P], w[:, 0:128], tile_cols(t["xnT"], j, p, P), start=True, stop=True)
                    pe.matmul(ps[:, 0, P:P + KEYS], w[:, 128:256], tile_cols(t["ctxT"], j, p, KEYS), start=True, stop=True).then_inc(qk_made[p], 1)

            def score(j, p):
                o, n = other(j, p)
                pe.wait_ge(kblk_ready[p], j + 1)
                pe.wait_ge(shifted[o], 3 * n)
                if masked:
                    pe.wait_ge(mask_made[p], j + 1)
                for i, (h0, nh) in enumerate(S_BANKS):
                    dst = ps[:, 2 + i, 0:nh * KEYS]
                    if masked:
                        pe.matmul(dst.rearrange("p (h k) -> p h k", k=KEYS), t["identb"][:],
                                  t["maskb"][p][:].unsqueeze(1).broadcast_to([P, nh, KEYS]), start=True, stop=False)
                    ins = pe.matmul(dst, qk[p][:, 0:P], kblk[p][:, h0 * KEYS:(h0 + nh) * KEYS], start=not masked, stop=True)
                ins.then_inc(scores_ready[p], 1)
                pe.wait_ge(ctx_staged[p], j + 1)
                pe.wait_ge(v_kept[o], n)
                if not (isinstance(n, int) and n == 0):
                    pe.wait_ge(residual[o], n - 1)
                ins = pe.matmul(VB, t["stage"][p][:, 0:KEYS], w[:, 256:384], start=True, stop=not bias_v)
                if bias_v:
                    ins = pe.matmul(VB, t["ones"][0:1, 0:KEYS], t["row"][0:1, 0:D], start=False, stop=True)
                ins.then_inc(v_made[p], 1)

            def round_of(j, p, r):
                o, n = other(j, p)
                if r == 0:
                    pe.wait_ge(heads_kept[o], n)
                    pe.wait_ge(v_kept[p], j + 1)
                pe.wait_ge(turned_kept[p], 4 * j + r + 1)
                for g in range(GROUPS):
                    ins = pe.matmul(ps[32 * g:32 * g + 32, 7, 0:P], vpad[p][:, HG * g + r, :], pt[p][:, r, g, :],
                                    start=(r == 0), stop=(r == HG - 1), tile_position=(0, 32 * g))
                return ins

            def weigh(j, p):
                o, n = other(j, p)
                for r in range(HG):
                    if r % 2 == 0:
                        pe.wait_ge(prob_ready[p], 2 * j + 1 + r // 2)
                    if r >= 2:
                        pe.wait_ge(turned_kept[p], 4 * j + r - 1)
                    else:
                        pe.wait_ge(turned_kept[o], 4 * n)
                    for g in range(GROUPS):
                        ins = pe.transpose(ps[0:KEYS, 5 + r % 2, g * P:g * P + P], prob[p][:, HG * g + r, :], t["ident"][:])
                    ins.then_inc(turned[p], 1)
                    if r:
                        round_of(j, p, r - 1)
                round_of(j, p, HG - 1).then_inc(heads_made[p], 1)

            def output(j, p):
                o, n = other(j, p)
                pe.wait_ge(heads_kept[p], j + 1)
                pe.wait_ge(residual[o], n)
                if not isinstance(j, int) or 2 * j + p + 2 < NT:
                    pe.wait_ge(v_kept[p], j + 2)
                ins = pe.matmul(OUT, oT[p][:], w[:, 384:512], start=True, stop=not bias_out)
                if bias_out:
                    ins = pe.matmul(OUT, t["ones"][0:1, 0:P], t["row"][0:1, D:2 * D], start=False, stop=True)
                ins.then_inc(out_made[p], 1)

            run(pe, project, score, skip, weigh, output)

        @block.scalar
        def _(sc):
            sc.wait_ge(loads, n_loads)

            def project(j, p):
                sc.wait_ge(scores_ready[p], j)
                sc.wait_ge(kblk_ready[p], j)
                if ready_qk:
                    q_src, k_src = tile_cols(t["xnT"], j, p, P), tile_cols(t["kT"], j, p, KEYS)
                else:
                    sc.wait_ge(qk_made[p], j + 1)
                    q_src, k_src = ps[:, 0, 0:P], ps[:, 0, P:P + KEYS]
                bq = dict(bias=t["cols"][:, 0:1]) if bias_qk else {}
                bk = dict(bias=t["cols"][:, 1:2]) if bias_qk else {}
                fn = ACT.Identity if bias_qk else ACT.Copy
                sc.activation(qk[p][:, P:P + KEYS], k_src, fn, **bk).then_inc(qk_kept[p], 1)
                sc.activation(qk[p][:, 0:P], q_src, fn, **bq).then_inc(qk_kept[p], 1)

            def score(j, p):
                sc.wait_ge(v_made[p], j + 1)
                sc.wait_ge(heads_made[p], j)
                sc.activation(bass.AP(tensor=vpad[p], offset=0, ap=[[HEADS * 32, KEYS], [HG * 32, GROUPS], [32 + HD, HG], [1, HD]]),
                              VB.rearrange("k (g i c) -> k g i c", g=GROUPS, i=HG), ACT.Copy).then_inc(v_kept[p], 1)

            def finish(j, p):
                sc.wait_ge(shifted[p], 3 * j + 3)
                flat = prob[p][:].rearrange("p h k -> p (h k)")
                sc.activation(flat, flat, ACT.Exp, scale=scale).then_inc(exp_ready[p], 1)

            def weigh(j, p):
                sc.wait_ge(heads_made[p], j)
                for r in range(HG):
                    sc.wait_ge(turned[p], 4 * j + r + 1)
                    sc.activation(pt[p][:, r, :, :].rearrange("k h q -> k (h q)"), ps[0:KEYS, 5 + r % 2, :], ACT.Copy).then_inc(turned_kept[p], 1)

            run(sc, project, score, finish, weigh, skip)

        @block.vector
        def _(v):
            def project(j, p):
                if not masked:
                    return
                v.wait_ge(mask_came[p], 16 * (j + 1))
                v.wait_ge(scores_ready[p], j)
                v.wait_ge(mask_made[p], j)
                v.tensor_scalar(t["maskf"][:, p * KEYS:(p + 1) * KEYS], t["maski"][p][:, 0:KEYS], 0.0, None, ALU.is_equal).then_inc(mask_step[p], 1)
                v.wait_ge(mask_step[p], j + 1)
                v.tensor_scalar(t["maskb"][p][:], t["maskf"][:, p * KEYS:(p + 1) * KEYS], NEG / scale, None, ALU.mult).then_inc(mask_made[p], 1)

            def score(j, p):
                v.wait_ge(scores_ready[p], j + 1)
                for i, (h0, nh) in enumerate(S_BANKS):
                    v.tensor_reduce(t["rowmax"][p][:, h0:h0 + nh], ps[:, 2 + i, 0:nh * KEYS].rearrange("p (h k) -> p h k", k=KEYS), X, ALU.max).then_inc(max_ready[p], 1)
                v.wait_ge(turned[p], 4 * j)
                for i, (h0, nh) in enumerate(S_BANKS):
                    v.wait_ge(max_ready[p], 3 * j + 1 + i)
                    v.tensor_tensor(prob[p][:, h0:h0 + nh, :], ps[:, 2 + i, 0:nh * KEYS].rearrange("p (h k) -> p h k", k=KEYS),
                                    t["rowmax"][p][:, h0:h0 + nh].unsqueeze(2).broadcast_to([P, nh, KEYS]), ALU.subtract).then_inc(shifted[p], 1)

            def finish(j, p):
                v.wait_ge(exp_ready[p], j + 1)
                v.wait_ge(prob_ready[p], 2 * j)
                v.tensor_reduce(t["rowsum"][p][:], prob[p][:], X, ALU.add).then_inc(sum_ready[p], 1)
                v.wait_ge(sum_ready[p], j + 1)
                v.reciprocal(rden[p][:], t["rowsum"][p][:]).then_inc(recip_ready[p], 1)

            def weigh(j, p):
                v.wait_ge(heads_made[p], j + 1)
                v.wait_ge(out_made[p], j)
                v.tensor_copy(oT[p][:], OT).then_inc(heads_kept[p], 1)

            def output(j, p):
                v.wait_ge(out_made[p], j + 1)
                xb = tile_cols(t["x"], j, p, P)
                v.scalar_tensor_tensor(xb, OUT, t["gate"][:, gate_at:gate_at + 1], xb, ALU.mult, ALU.add).then_inc(residual[p], 1)

            run(v, project, score, finish, weigh, output)


def quantised_ffn(nc, t, d, gate_at):
    C = 3
    WB = 32
    NW = 3 * C * P // WB
    QCH = 2048
    NQ = C * NTOK // QCH
    with ExitStack() as ctx:
        s = Sems(nc, ctx, "l0f")
        loads, steps, own_max, all_max, wq_ready, w_turned, w_kept, x_ready = (
            s.one("loads"), s.one("steps"), s.one("own_max"), s.one("all_max"), s.one("wq_ready"), s.one("w_turned"),
            s.one("w_kept"), s.one("x_ready"))
        up_made, up_kept, gate_made, gate_kept = s.one("up_made"), s.one("up_kept"), s.one("gate_made"), s.one("gate_kept")
        gate_ready, up_ready, sig_ready, sig_used, sig_step, o_ready = (
            s.one("gate_ready"), s.one("up_ready"), s.two("sig_ready"), s.two("sig_used"), s.two("sig_step"), s.one("o_ready"))
        down_made, down_kept, turned, residual = s.two("down_made"), s.two("down_kept"), s.two("turned"), s.two("residual")
        ps = t["ps"]

        def sb(name, shape):
            return ctx.enter_context(nc.sbuf_tensor("l0f_" + name, shape, F32))

        up, gate = sb("up", [P, C * NTOK]), sb("gate", [P, C * NTOK])
        up3, gate3 = up[:].rearrange("p (c n) -> p c n", c=C), gate[:].rearrange("p (c n) -> p c n", c=C)
        wraw, wT, wscale, winv = sb("wraw", [P, 3 * C * P]), sb("wT", [P, 3 * C * P]), sb("wscale", [P, NW]), sb("winv", [P, NW])
        qs = sb("qs", [P, 32])
        maxes = sb("maxes", [P, 2 * NBLK])
        sig = t["xc"]
        block = ctx.enter_context(nc.Block())

        @block.sync
        def _(sp):
            sp.dma_start(wraw[:], d["l0f_W"]).then_inc(loads, 16)

        @block.vector
        def _(v):
            step = Chain(v, steps)

            def scale_of(k):
                c = qs[:, 4 * k:4 * k + 4]
                v.wait_ge(all_max, k + 1)
                step(v.tensor_scalar(c[:, 2:3], c[:, 1:2], 1.0 / 32767.0, 1e-12, ALU.mult, ALU.max))
                step(v.reciprocal(c[:, 3:4], c[:, 2:3]))
                return c[:, 2:3], c[:, 3:4]

            def quantise(a, k, done):
                scale, inv = scale_of(k)
                step(v.tensor_scalar(a, a, inv, MAGIC, ALU.mult, ALU.add))
                v.tensor_scalar(a, a, MAGIC, scale, ALU.subtract, ALU.mult).then_inc(done, 1)

            v.tensor_reduce(qs[:, 0:1], t["xnT"][:], X, ALU.max, apply_absolute_value=True).then_inc(own_max, 1)
            v.wait_ge(loads, 16)
            w3 = wraw[:].rearrange("p (b i) -> p b i", i=WB)
            sc3 = wscale[:].unsqueeze(2).broadcast_to([P, NW, WB])
            step(v.tensor_reduce(wscale[:], w3, X, ALU.max, apply_absolute_value=True))
            step(v.tensor_scalar(wscale[:], wscale[:], 1.0 / 7.0, 1e-12, ALU.mult, ALU.max))
            step(v.reciprocal(winv[:], wscale[:]))
            step(v.tensor_tensor(w3, w3, winv[:].unsqueeze(2).broadcast_to([P, NW, WB]), ALU.mult))
            step(v.tensor_scalar(wraw[:], wraw[:], MAGIC, MAGIC, ALU.add, ALU.subtract))
            v.tensor_tensor(w3, w3, sc3, ALU.mult).then_inc(wq_ready, 1)
            quantise(t["xnT"][:], 0, x_ready)
            with v.Fori(0, NBLK) as j:
                v.wait_ge(up_kept, j + 1)
                v.tensor_reduce(maxes[:, bass.ds(j, 1)], up3[:, :, bass.ds(j * BLK, BLK)], mybir.AxisListType.XY, ALU.max, apply_absolute_value=True).then_inc(sig_step[0], 1)
                v.wait_ge(gate_kept, j + 1)
                v.tensor_reduce(maxes[:, bass.ds(j + NBLK, 1)], gate3[:, :, bass.ds(j * BLK, BLK)], mybir.AxisListType.XY, ALU.max, apply_absolute_value=True).then_inc(sig_step[0], 1)
            v.wait_ge(sig_step[0], 2 * NBLK)
            v.tensor_reduce(qs[:, 4:5], maxes[:, 0:NBLK], X, ALU.max).then_inc(own_max, 1)
            v.tensor_reduce(qs[:, 8:9], maxes[:, NBLK:2 * NBLK], X, ALU.max).then_inc(own_max, 1)
            quantise(gate[:], 2, gate_ready)
            quantise(up[:], 1, up_ready)
            v.wait_ge(gate_ready, 1)
            for n in range(NQ):
                p = n % 2
                half, part = sig[:, p * QCH:(p + 1) * QCH], gate[:, n * QCH:(n + 1) * QCH]
                v.wait_ge(sig_ready[p], n // 2 + 1)
                step(v.tensor_scalar(half, half, 65536.0, MAGIC, ALU.mult, ALU.add))
                step(v.tensor_scalar(half, half, MAGIC + 65535.0, MAGIC, ALU.min, ALU.subtract))
                v.scalar_tensor_tensor(part, half, 1.0 / 65536.0, part, ALU.mult, ALU.mult).then_inc(sig_used[p], 1)
            v.wait_ge(sig_used[0], NQ // 2)
            v.wait_ge(sig_used[1], NQ // 2)
            v.tensor_reduce(qs[:, 12:13], gate[:], X, ALU.max, apply_absolute_value=True).then_inc(own_max, 1)
            quantise(gate[:], 3, gate_ready)
            v.wait_ge(gate_ready, 2)
            v.wait_ge(up_ready, 1)
            step(v.tensor_tensor(gate[:], gate[:], up[:], ALU.mult))
            v.tensor_reduce(qs[:, 16:17], gate[:], X, ALU.max, apply_absolute_value=True).then_inc(own_max, 1)
            quantise(gate[:], 4, o_ready)
            with v.Fori(0, NBLK // 2) as j:
                for p in range(2):
                    v.wait_ge(turned[p], j + 1)
                    xb = t["x"][:, bass.ds((2 * j + p) * BLK, BLK)]
                    v.scalar_tensor_tensor(xb, ps[:, 2 + p, :], t["gate"][:, gate_at:gate_at + 1], xb, ALU.mult, ALU.add).then_inc(residual[p], 1)

        @block.gpsimd
        def _(pool):
            for k in range(5):
                pool.wait_ge(own_max, {0: 1, 1: 3, 2: 3, 3: 4, 4: 5}[k])
                pool.partition_all_reduce(qs[:, 4 * k + 1:4 * k + 2], qs[:, 4 * k:4 * k + 1], P, RMAX).then_inc(all_max, 1)

        @block.scalar
        def _(sc):
            for b in range(3):
                sc.wait_ge(w_turned, b + 1)
                sc.activation(wT[:, b * C * P:(b + 1) * C * P], ps[:, b, 0:C * P], ACT.Copy).then_inc(w_kept, 1)
            with sc.Fori(0, NBLK) as j:
                sc.wait_ge(up_made, j + 1)
                sc.activation(up3[:, :, bass.ds(j * BLK, BLK)], ps[:, 0:3, :], ACT.Copy).then_inc(up_kept, 1)
                sc.wait_ge(gate_made, j + 1)
                sc.activation(gate3[:, :, bass.ds(j * BLK, BLK)], ps[:, 3:6, :], ACT.Copy).then_inc(gate_kept, 1)
            sc.wait_ge(gate_ready, 1)
            for n in range(NQ):
                p = n % 2
                if n >= 2:
                    sc.wait_ge(sig_used[p], n // 2)
                sc.activation(sig[:, p * QCH:(p + 1) * QCH], gate[:, n * QCH:(n + 1) * QCH], ACT.Sigmoid).then_inc(sig_ready[p], 1)
            with sc.Fori(0, NBLK // 2) as j:
                for p in range(2):
                    sc.wait_ge(down_made[p], j + 1)
                    sc.wait_ge(turned[p], j)
                    sc.activation(t["stage"][p][:], ps[:, p, :], ACT.Copy).then_inc(down_kept[p], 1)

        @block.tensor
        def _(pe):
            pe.wait_ge(wq_ready, 1)
            for b in range(3):
                for i in range(C):
                    ins = pe.transpose(ps[:, b, i * P:(i + 1) * P], wraw[:, (b * C + i) * P:(b * C + i + 1) * P], t["ident"][:])
                ins.then_inc(w_turned, 1)
            pe.wait_ge(w_kept, 3)
            pe.wait_ge(x_ready, 1)
            with pe.Fori(0, NBLK) as j:
                xb = t["xnT"][:, bass.ds(j * BLK, BLK)]
                for which, made, kept in ((0, up_made, up_kept), (1, gate_made, gate_kept)):
                    pe.wait_ge(kept, j)
                    for c in range(C):
                        ins = pe.matmul(ps[:, 3 * which + c, :], wT[:, (which * C + c) * P:(which * C + c + 1) * P], xb, start=True, stop=True)
                    ins.then_inc(made, 1)
            pe.wait_ge(o_ready, 1)
            with pe.Fori(0, NBLK // 2) as j:
                for p in range(2):
                    pe.wait_ge(down_kept[p], j)
                    for c in range(C):
                        ins = pe.matmul(ps[:, p, :], wT[:, (2 * C + c) * P:(2 * C + c + 1) * P], gate3[:, c, bass.ds((2 * j + p) * BLK, BLK)],
                                        start=(c == 0), stop=(c == C - 1))
                    ins.then_inc(down_made[p], 1)
                for p in range(2):
                    pe.wait_ge(down_kept[p], j + 1)
                    pe.wait_ge(residual[p], j)
                    for i in range(TB):
                        ins = pe.transpose(ps[:, 2 + p, i * P:(i + 1) * P], t["stage"][p][:, i * P:(i + 1) * P], t["ident"][:])
                    ins.then_inc(turned[p], 1)


def experts(nc, t, d, stage, E, C, kind, gate_at=None, weight=None, bias1=False, bias2=False):
    nin = 2 if kind == "glu" else 1
    width = (nin + 1) * C * P + (C if bias1 else 0)
    NQ = 2 if E > 1 else 1
    with ExitStack() as ctx:
        s = Sems(nc, ctx, stage)
        came, used = [s.one(f"came{q}") for q in range(NQ)], [s.one(f"used{q}") for q in range(NQ)]
        made, acted, h_step = s.two("made"), s.two("acted"), s.two("h_step")
        h_ready, down_made, residual = s.two("h_ready"), s.two("down_made"), s.two("residual")
        ps = t["ps"]

        def sb(name, shape):
            return ctx.enter_context(nc.sbuf_tensor(f"{stage}_sb_{name}", shape, F32))

        wb = [sb(f"w{q}", [P, width]) for q in range(NQ)]
        b2 = [sb(f"b2{q}", [1, D]) for q in range(NQ)]
        spare = sb("spare", [1, 1])
        h = [sb(f"h{p}", [P, C, BLK]) for p in range(2)]
        ga = [sb(f"ga{p}", [P, BLK]) for p in range(2)]
        sn = [sb(f"sn{p}", [P, BLK]) for p in range(2)] if kind == "sine" else None
        block = ctx.enter_context(nc.Block())
        n_in = 16 * (1 + bias2)

        def chunk_free(eng, p, m, c):
            if c >= 2:
                eng.wait_ge(h_ready[p], m * C + c - 1)
            elif p == 1:
                eng.wait_ge(h_ready[0], m * C + C - 1 + c)
            else:
                eng.wait_ge(h_ready[1], m * C)

        @block.sync
        def _(sp):
            def load(k, q):
                e = bass.ds(k * 2 + q, 1) if E > 1 else slice(0, 1)
                if E > 1:
                    sp.wait_ge(used[q], k)
                sp.dma_start(wb[q][:], d[f"{stage}_W"][e, :, :].rearrange("e p n -> (e p) n")).then_inc(came[q], 16)
                if bias2:
                    sp.dma_start(b2[q][:], d[f"{stage}_b2"][e, :]).then_inc(came[q], 16)
            if E == 1:
                load(0, 0)
            else:
                with sp.Fori(0, E // 2) as k:
                    for q in range(2):
                        load(k, q)

        def loops(eng, each, end=None):
            def inner(k, q):
                e = k * 2 + q if E > 1 else 0
                with eng.Fori(0, NBLK // 2) as j:
                    each(k, q, e, j)
                if end:
                    end(q)
            if E == 1:
                inner(0, 0)
            else:
                with eng.Fori(0, E // 2) as k:
                    for q in range(2):
                        inner(k, q)

        HB = C // 2

        @block.tensor
        def _(pe):
            def each(k, q, e, j):
                pe.wait_ge(came[q], n_in * (k + 1))
                for p in range(2):
                    m = e * (NBLK // 2) + j
                    xb = t["xnT"][:, bass.ds((2 * j + p) * BLK, BLK)]
                    for c in range(C):
                        b = c % 2
                        chunk_free(pe, p, m, c)
                        for i in range(nin):
                            ins = pe.matmul(ps[:, 2 * b + i, :], wb[q][:, (i * C + c) * P:(i * C + c + 1) * P], xb, start=True, stop=True)
                        ins.then_inc(made[b], 1)
                for p in range(2):
                    m = e * (NBLK // 2) + j
                    pe.wait_ge(h_ready[p], (m + 1) * C)
                    pe.wait_ge(residual[p], m)
                    for i in range(TB):
                        dst = ps[:, 4 + p, i * P:(i + 1) * P]
                        for c in range(C):
                            ins = pe.matmul(dst, h[p][:, c, i * P:(i + 1) * P], wb[q][:, (nin * C + c) * P:(nin * C + c + 1) * P],
                                            start=(c == 0), stop=(c == C - 1 and not bias2))
                        if bias2:
                            ins = pe.matmul(dst, t["ones"][0:1, 0:P], b2[q][:], start=False, stop=True)
                    ins.then_inc(down_made[p], 1)
            loops(pe, each)

        @block.scalar
        def _(sc):
            def each(k, q, e, j):
                sc.wait_ge(came[q], n_in * (k + 1))
                for p in range(2):
                    n = (e * NBLK + 2 * j + p) * HB
                    m = e * (NBLK // 2) + j
                    for c in range(C):
                        b = c % 2
                        sc.wait_ge(made[b], n + c // 2 + 1)
                        b1 = wb[q][:, width - C + c:width - C + c + 1] if bias1 else None
                        if kind == "glu":
                            chunk_free(sc, p, m, c)
                            sc.activation(ga[b][:], ps[:, 2 * b, :], ACT.Gelu).then_inc(acted[b], 1)
                        elif kind == "gelu":
                            sc.wait_ge(down_made[p], m)
                            sc.activation(h[p][:, c, :], ps[:, 2 * b, :], ACT.Gelu, bias=b1).then_inc(h_ready[p], 1)
                        else:
                            chunk_free(sc, p, m, c)
                            sc.activation(ga[b][:], ps[:, 2 * b, :], ACT.Identity, scale=0.1 * INV_2PI, bias=t["phase"][:, c:c + 1]).then_inc(acted[b], 1)
                            sc.wait_ge(h_step[b], 3 * (n + c // 2) + 2)
                            sc.activation(sn[b][:], sn[b][:], ACT.Sin, scale=TWO_PI).then_inc(acted[b], 1)
                            sc.wait_ge(h_step[b], 3 * (n + c // 2) + 3)
                            sc.wait_ge(down_made[p], m)
                            sc.activation(h[p][:, c, :], ga[b][:], ACT.Relu, bias=b1).then_inc(h_ready[p], 1)
            loops(sc, each)

        @block.vector
        def _(v):
            def end(q):
                v.memset(spare[:], 0.0).then_inc(used[q], 1)

            def each(k, q, e, j):
                for p in range(2):
                    n = (e * NBLK + 2 * j + p) * HB
                    m = e * (NBLK // 2) + j
                    for c in range(C):
                        b = c % 2
                        if kind == "glu":
                            v.wait_ge(acted[b], n + c // 2 + 1)
                            v.wait_ge(down_made[p], m)
                            v.tensor_tensor(h[p][:, c, :], ga[b][:], ps[:, 2 * b + 1, :], ALU.mult).then_inc(h_ready[p], 1)
                        elif kind == "sine":
                            v.wait_ge(acted[b], 2 * (n + c // 2) + 1)
                            v.tensor_scalar(sn[b][:], ga[b][:], MAGIC, MAGIC, ALU.add, ALU.subtract).then_inc(h_step[b], 1)
                            v.wait_ge(h_step[b], 3 * (n + c // 2) + 1)
                            v.tensor_tensor(sn[b][:], ga[b][:], sn[b][:], ALU.subtract).then_inc(h_step[b], 1)
                            v.wait_ge(acted[b], 2 * (n + c // 2) + 2)
                            v.scalar_tensor_tensor(ga[b][:], sn[b][:], t["amp"][:, c:c + 1], ps[:, 2 * b, :], ALU.mult, ALU.add).then_inc(h_step[b], 1)
                for p in range(2):
                    m = e * (NBLK // 2) + j
                    v.wait_ge(down_made[p], m + 1)
                    v.wait_ge(residual[p], m)
                    if weight is None:
                        xb = t["x"][:, bass.ds((2 * j + p) * BLK, BLK)]
                        v.scalar_tensor_tensor(xb, ps[:, 4 + p, :], t["gate"][:, gate_at:gate_at + 1], xb, ALU.mult, ALU.add).then_inc(residual[p], 1)
                    else:
                        for i in range(TB):
                            at = (2 * j + p) * TB + i
                            xb = t["x"][:, bass.ds(at * P, P)]
                            ins = v.scalar_tensor_tensor(xb, ps[:, 4 + p, i * P:(i + 1) * P], weight[:, bass.ds(e * NT + at, 1)], xb, ALU.mult, ALU.add)
                        ins.then_inc(residual[p], 1)
            loops(v, each, end)


def route_scores(nc, t, d, stage, E, norm):
    with ExitStack() as ctx:
        s = Sems(nc, ctx, stage + "r")
        loads, steps, sq_ready, norm_ready, vec_ready, vec_turned, vec_kept = (
            s.one("loads"), s.one("steps"), s.one("sq_ready"), s.one("norm_ready"), s.one("vec_ready"), s.one("vec_turned"), s.one("vec_kept"))
        projected, kept, squared, made, out = s.two("projected"), s.two("kept"), s.two("squared"), s.two("made"), s.two("out")
        sums_ready, norms_ready, reset_step = s.one("sums_ready"), s.one("norms_ready"), s.one("reset_step")
        ps, w = t["ps"], t["wstat"]
        M = E + norm
        G = w[:, 128:128 + E]
        raw = ctx.enter_context(nc.sbuf_tensor(stage + "_route_raw", [P, NT, M], F32))
        sqs = [ctx.enter_context(nc.sbuf_tensor(f"{stage}_route_sq{p}", [P, BLK], F32)) for p in range(2)]
        vec = ctx.enter_context(nc.sbuf_tensor(stage + "_route_vec", [E, P], F32))
        vsq = ctx.enter_context(nc.sbuf_tensor(stage + "_route_vsq", [E, P], F32))
        vn = ctx.enter_context(nc.sbuf_tensor(stage + "_route_vn", [E, 1], F32))
        temp = ctx.enter_context(nc.sbuf_tensor(stage + "_route_temp", [P, 2], F32))
        norms = t["small"][:, 0:NT]
        block = ctx.enter_context(nc.Block())

        @block.sync
        def _(sp):
            if norm:
                sp.dma_start(w[:, 0:128], d[f"{stage}_proj"]).then_inc(loads, 16)
                sp.dma_start(vec[:], d[f"{stage}_vec"]).then_inc(loads, 16)
                sp.dma_start(temp[:, 0:1], d[f"{stage}_temp"].partition_broadcast(P)).then_inc(loads, 16)
            else:
                sp.dma_start(G, d[f"{stage}_G"]).then_inc(loads, 16)

        n_loads = 48 if norm else 16

        @block.tensor
        def _(pe):
            pe.wait_ge(loads, n_loads)
            if norm:
                pe.wait_ge(vec_ready, 1)
                pe.transpose(ps[:, 6, 0:E], vec[:], t["ident"][0:E, 0:E]).then_inc(vec_turned, 1)
                pe.wait_ge(vec_kept, 1)
            with pe.Fori(0, NBLK // 2) as j:
                if norm:
                    for p in range(2):
                        pe.wait_ge(squared[p], j)
                        pe.wait_ge(kept[p], j)
                        pe.matmul(ps[:, p, :], w[:, 0:128], t["xnT"][:, bass.ds((2 * j + p) * BLK, BLK)], start=True, stop=True).then_inc(projected[p], 1)
                for p in range(2):
                    pe.wait_ge(kept[p], j + 1)
                    if norm:
                        pe.wait_ge(squared[p], j + 1)
                    pe.wait_ge(out[p], j)
                    for i in range(TB):
                        ins = pe.matmul(ps[:, 2 + p, i * M:i * M + E], t["stage"][p][:, i * P:(i + 1) * P], G, start=True, stop=True)
                        if norm:
                            ins = pe.matmul(ps[:, 2 + p, i * M + E:i * M + M], sqs[p][:, i * P:(i + 1) * P], t["ones"][:, 0:1], start=True, stop=True)
                    ins.then_inc(made[p], 1)

        @block.scalar
        def _(sc):
            with sc.Fori(0, NBLK // 2) as j:
                for p in range(2):
                    if norm:
                        sc.wait_ge(projected[p], j + 1)
                        src = ps[:, p, :]
                    else:
                        src = t["xnT"][:, bass.ds((2 * j + p) * BLK, BLK)]
                    sc.wait_ge(made[p], j)
                    sc.activation(t["stage"][p][:], src, ACT.Copy).then_inc(kept[p], 1)
                    if norm:
                        sc.activation(sqs[p][:], src, ACT.Square).then_inc(squared[p], 1)

        @block.gpsimd
        def _(pool):
            pool.memset(t["reset"][:], 1.0).then_inc(reset_step, 1)
            pool.wait_ge(reset_step, 1)
            pool.memset(t["reset"][:, :, 0:1], 0.0)
            if norm:
                pool.wait_ge(sq_ready, 1)
                pool.tensor_tensor(vn[:], vn[:], t["plus_half"][0:E, 0:1], ALU.pow).then_inc(norm_ready, 1)
                pool.wait_ge(sums_ready, 1)
                pool.tensor_tensor(norms, norms, t["plus_half"][:], ALU.pow).then_inc(norms_ready, 1)

        @block.vector
        def _(v):
            step = Chain(v, steps)
            if norm:
                v.wait_ge(loads, n_loads)
                step(v.tensor_tensor(vsq[:], vec[:], vec[:], ALU.mult))
                v.tensor_reduce(vn[:], vsq[:], X, ALU.add).then_inc(sq_ready, 1)
                v.wait_ge(norm_ready, 1)
                step(v.tensor_scalar(vn[:], vn[:], 1e-12, None, ALU.max))
                step(v.reciprocal(vn[:], vn[:]))
                step(v.reciprocal(temp[:, 1:2], temp[:, 0:1]))
                v.tensor_scalar(vec[:], vec[:], vn[:], None, ALU.mult).then_inc(vec_ready, 1)
                v.wait_ge(vec_turned, 1)
                v.tensor_copy(G, ps[:, 6, 0:E]).then_inc(vec_kept, 1)
            with v.Fori(0, NBLK // 2) as j:
                for p in range(2):
                    v.wait_ge(made[p], j + 1)
                    v.tensor_copy(raw[:, bass.ds((2 * j + p) * TB, TB), :], ps[:, 2 + p, 0:TB * M].rearrange("p (i m) -> p i m", m=M)).then_inc(out[p], 1)
            v.wait_ge(out[0], NBLK // 2)
            v.wait_ge(out[1], NBLK // 2)
            if norm:
                v.tensor_copy(norms, raw[:, :, E]).then_inc(sums_ready, 1)
                v.wait_ge(norms_ready, 1)
                step(v.tensor_scalar(norms, norms, 1e-12, None, ALU.max))
                step(v.reciprocal(norms, norms))
                step(v.tensor_scalar(norms, norms, temp[:, 1:2], None, ALU.mult))
                v.tensor_tensor(t["scores"][:, :, 0:E], raw[:, :, 0:E], norms.unsqueeze(2).broadcast_to([P, NT, E]), ALU.mult)
            else:
                v.tensor_copy(t["scores"][:, :, 0:E], raw[:, :, 0:E])


def top_two(nc, t, E, gate_at):
    with ExitStack() as ctx:
        s = Sems(nc, ctx, "top2")
        steps, rank_ready, shifted, exp_ready = s.one("steps"), s.one("rank_ready"), s.one("shifted"), s.one("exp_ready")

        def sb(name, shape):
            return ctx.enter_context(nc.sbuf_tensor("top2_" + name, shape, F32))

        rank, work, best = (sb(n, [P, NT, E]) for n in ("rank", "work", "best"))
        one, two = t["hots"]
        v1, v2, first, p1, p2 = (sb(n, [P, NT]) for n in ("v1", "v2", "first", "p1", "p2"))
        sc_ = t["scores"][:, :, 0:E]
        wide = lambda a: a[:].unsqueeze(2).broadcast_to([P, NT, E])
        block = ctx.enter_context(nc.Block())

        @block.gpsimd
        def _(pool):
            pool.iota(rank[:], pattern=[[0, NT], [-1, E]], base=E, channel_multiplier=0, allow_small_or_imprecise_dtypes=True).then_inc(rank_ready, 1)

        @block.vector
        def _(v):
            step = Chain(v, steps)

            def pick(a, top, hot):
                step(v.tensor_reduce(top[:], a, X, ALU.max))
                step(v.tensor_tensor(work[:], a, wide(top), ALU.is_equal))
                step(v.tensor_tensor(work[:], work[:], rank[:], ALU.mult))
                step(v.tensor_reduce(first[:], work[:], X, ALU.max))
                step(v.tensor_tensor(hot[:], rank[:], wide(first), ALU.is_equal))

            v.wait_ge(rank_ready, 1)
            pick(sc_, v1, one)
            step(v.scalar_tensor_tensor(best[:], one[:], -1e30, sc_, ALU.mult, ALU.add))
            pick(best[:], v2, two)
            v.tensor_tensor(p2[:], v2[:], v1[:], ALU.subtract).then_inc(shifted, 1)
            v.wait_ge(exp_ready, 1)
            step(v.tensor_scalar(p1[:], p2[:], 1.0, None, ALU.add))
            step(v.reciprocal(p1[:], p1[:]))
            step(v.tensor_scalar(p1[:], p1[:], t["gate"][:, gate_at:gate_at + 1], None, ALU.mult))
            step(v.tensor_tensor(p2[:], p2[:], p1[:], ALU.mult))
            step(v.tensor_tensor(t["sel"][:].rearrange("p e n -> p n e"), one[:], two[:], ALU.add))
            step(v.tensor_tensor(work[:], one[:], wide(p1), ALU.mult))
            step(v.tensor_tensor(best[:], two[:], wide(p2), ALU.mult))
            step(v.tensor_tensor(t["comb"][:, 0:E, :].rearrange("p e n -> p n e"), work[:], best[:], ALU.add))

        @block.scalar
        def _(sc):
            sc.wait_ge(shifted, 1)
            sc.activation(p2[:], p2[:], ACT.Exp).then_inc(exp_ready, 1)


def top_tokens(nc, t, E, K, gate_at):
    BITS = 30
    with ExitStack() as ctx:
        s = Sems(nc, ctx, "topk")
        steps, shifted, exp_ready, loop_steps, counted, summed = (
            s.one("steps"), s.one("shifted"), s.one("exp_ready"), s.one("loop_steps"), s.one("counted"), s.one("summed"))
        start_steps = s.one("start_steps")

        def sb(name, shape, dt=F32):
            return ctx.enter_context(nc.sbuf_tensor("topk_" + name, shape, dt))

        tri, reset, sel = t["tri"], t["reset"], t["sel"]
        score, work, before = (sb(n, [P, E, NT]) for n in ("score", "work", "before"))
        top, total = sb("top", [P, NT]), sb("total", [P, NT])
        thr, cand, inc = (sb(n, [P, E], I32) for n in ("thr", "cand", "inc"))
        bit, biti = sb("bit", [P, 1]), sb("biti", [P, 1], I32)
        count, enough = sb("count", [P, E]), sb("enough", [P, E])
        ps = t["ps"]
        raw = t["scores"][:, :, 0:E]
        by_tile = lambda a: a[:].rearrange("p e n -> p n e")
        over_e = lambda a: a[:].unsqueeze(2).broadcast_to([P, NT, E])
        over_n = lambda a: a.unsqueeze(2).broadcast_to([P, E, NT])
        block = ctx.enter_context(nc.Block())
        LOOP = 7

        @block.gpsimd
        def _(pool):
            step = Chain(pool, start_steps)
            step(pool.memset(thr[:], 0))
            step(pool.memset(bit[:], float(2 ** (BITS - 1))))

        @block.scalar
        def _(sc):
            sc.wait_ge(shifted, 1)
            sc.activation(score[:], score[:], ACT.Exp).then_inc(exp_ready, 1)

        @block.tensor
        def _(pe):
            with pe.Fori(0, BITS) as j:
                pe.wait_ge(counted, j + 1)
                pe.matmul(ps[:, 0, 0:E], t["ones"][:], count[:], start=True, stop=True).then_inc(summed, 1)
            pe.wait_ge(counted, BITS + 1)
            pe.matmul(ps[:, 0, 0:E], t["ones"][:], count[:], start=True, stop=True).then_inc(summed, 1)
            flat = work[:].rearrange("p e n -> p (e n)")
            pe.wait_ge(counted, BITS + 2)
            pe.matmul(ps[:, 1, :], tri[:], flat, start=True, stop=True).then_inc(summed, 1)
            pe.matmul(ps[:, 2, :], t["ones"][:], flat, start=True, stop=True).then_inc(summed, 1)

        @block.vector
        def _(v):
            step = Chain(v, steps)
            step(v.tensor_reduce(top[:], raw, X, ALU.max))
            v.tensor_tensor(by_tile(score), raw, over_e(top), ALU.subtract).then_inc(shifted, 1)
            v.wait_ge(exp_ready, 1)
            step(v.tensor_reduce(total[:], by_tile(score), X, ALU.add))
            step(v.reciprocal(total[:], total[:]))
            step(v.tensor_tensor(by_tile(score), by_tile(score), over_e(total), ALU.mult))
            v.wait_ge(start_steps, 2)
            with v.Fori(0, BITS) as j:
                def did(ins, n):
                    ins.then_inc(loop_steps, 1)
                    v.wait_ge(loop_steps, j * LOOP + n)

                did(v.tensor_copy(biti[:], bit[:]), 1)
                did(v.tensor_tensor(cand[:], thr[:], biti[:].broadcast_to([P, E]), ALU.bitwise_or), 2)
                did(v.tensor_tensor(work[:], score[:], over_n(cand[:].bitcast(F32)), ALU.is_ge), 3)
                v.tensor_reduce(count[:], work[:], X, ALU.add).then_inc(counted, 1)
                v.wait_ge(summed, j + 1)
                did(v.tensor_scalar(enough[:], ps[:, 0, 0:E], float(K), None, ALU.is_ge), 4)
                did(v.tensor_scalar(inc[:], enough[:], bit[:], None, ALU.mult), 5)
                did(v.tensor_tensor(thr[:], thr[:], inc[:], ALU.bitwise_or), 6)
                did(v.tensor_scalar(bit[:], bit[:], 0.5, None, ALU.mult), 7)
            limit = over_n(thr[:].bitcast(F32))
            step(v.tensor_tensor(sel[:], score[:], limit, ALU.is_gt))
            v.tensor_reduce(count[:], sel[:], X, ALU.add).then_inc(counted, 1)
            v.wait_ge(counted, BITS + 1)
            v.tensor_tensor(work[:], score[:], limit, ALU.is_equal).then_inc(counted, 1)
            v.wait_ge(summed, BITS + 1)
            step(v.tensor_scalar(enough[:], ps[:, 0, 0:E], -1.0, float(K), ALU.mult, ALU.add))
            v.wait_ge(summed, BITS + 3)
            flat = lambda a: a[:].rearrange("p e n -> p (e n)")
            step(v.tensor_tensor_scan(flat(before), flat(reset), ps[:, 2, :], 0.0, ALU.mult, ALU.add))
            step(v.tensor_tensor(flat(before), flat(before), ps[:, 2, :], ALU.subtract))
            step(v.tensor_tensor(flat(before), flat(before), ps[:, 1, :], ALU.add))
            step(v.tensor_tensor(before[:], before[:], over_n(enough[:]), ALU.is_lt))
            step(v.tensor_tensor(before[:], before[:], work[:], ALU.mult))
            step(v.tensor_tensor(sel[:], sel[:], before[:], ALU.add))
            step(v.tensor_tensor(score[:], sel[:], score[:], ALU.mult))
            step(v.tensor_scalar(t["comb"][:, 0:E, :], score[:], t["gate"][:, gate_at:gate_at + 1], None, ALU.mult))


def token_rows(nc, u, stage, E):
    with ExitStack() as ctx:
        s = Sems(nc, ctx, stage + "rows")
        cleared, rows_ready, stored = s.one("cleared"), s.one("rows_ready"), s.one("stored")
        rows = ctx.enter_context(nc.sbuf_tensor(stage + "_rows_sb", [P, NT, D + E], F32))
        zero = ctx.enter_context(nc.sbuf_tensor(stage + "_zero", [P, D + E], F32))
        rstd = u["small"][:, 2 * NT:3 * NT]
        block = ctx.enter_context(nc.Block())

        @block.gpsimd
        def _(pool):
            pool.memset(zero[:], 0.0).then_inc(cleared, 1)

        @block.scalar
        def _(sc):
            sc.activation(rows[:, :, D:D + E], u["comb"][:].rearrange("p e n -> p n e"), ACT.Copy).then_inc(rows_ready, 1)

        @block.vector
        def _(v):
            v.tensor_tensor(rows[:, :, 0:D], u["xc"][:].rearrange("p (n d) -> p n d", d=D),
                            rstd.unsqueeze(2).broadcast_to([P, NT, D]), ALU.mult).then_inc(rows_ready, 1)

        @block.sync
        def _(sp):
            by_tile = lambda a: a.rearrange("(n p) f -> p n f", p=P)
            sp.wait_ge(cleared, 1)
            sp.dma_start(by_tile(u["sum_rows"]), zero[:, 0:D].unsqueeze(1).broadcast_to([P, NT + TB, D])).then_inc(stored, 16)
            sp.dma_start(by_tile(u["rows"][NTOK:NTOK + BLK, :]), zero[:].unsqueeze(1).broadcast_to([P, TB, D + E])).then_inc(stored, 16)
            sp.wait_ge(rows_ready, 2)
            sp.dma_start(by_tile(u["rows"][0:NTOK, :]), rows[:]).then_inc(stored, 16)
            sp.wait_ge(stored, 48)


def slot_lists(nc, u, stage, E, NG, two_choices):
    NHI = NG * TB if two_choices else TB
    CH = NT
    NC = 2 if two_choices else E
    with ExitStack() as ctx:
        s = Sems(nc, ctx, stage + "slots")
        steps, sums, iotas, lo_ready, hi_ready, hot_used, listed, hot_step, taken = (
            s.one("steps"), s.one("sums"), s.one("iotas"), s.two("lo_ready"), s.two("hi_ready"), s.two("hot_used"),
            s.two("listed"), s.two("hot_step"), s.two("taken"))

        def sb(name, shape, dt=F32):
            return ctx.enter_context(nc.sbuf_tensor(f"{stage}_slots_{name}", shape, dt))

        rank = sb("rank", [P, E, NT])
        lo, hi, tile = sb("lo", [P, NC * CH]), sb("hi", [P, NC * CH]), sb("tile", [P, CH])
        iota_lo, iota_hi, iota_e, iota_g = sb("iota_lo", [P, P]), sb("iota_hi", [P, NHI]), sb("iota_e", [P, E]), sb("iota_g", [P, NG])
        token, spare_row = sb("token", [P, 1]), sb("spare_row", [P, NG * TB])
        lo_hot = [sb(f"lo_hot{p}", [P, CH, P], BF16) for p in range(2)]
        hi_hot = [sb(f"hi_hot{p}", [P, CH, NHI]) for p in range(2)]
        hi_num = [sb(f"hi_num{p}", [P, CH, 2, NHI], BF16) for p in range(2)]
        nums = sb("nums", [P, NG * TB, 2])
        slot, none = sb("slot", [P, NG * TB]), sb("none", [P, NG * TB])
        if two_choices:
            groups, first, ones_e = sb("groups", [P, E]), sb("first", [P, E]), sb("ones_e", [P, E])
            begun = sb("begun", [P, NG, E + 1])
            picked = sb("picked", [P, NT, E])
            eid = sb("eid", [P, NG])
        ps = u["ps"]
        sel = u["sel"]
        flat = lambda a: a[:].rearrange("p e n -> p (e n)")
        W = E * NT
        block = ctx.enter_context(nc.Block())
        wide = dict(channel_multiplier=0, allow_small_or_imprecise_dtypes=True)

        @block.gpsimd
        def _(pool):
            step = Chain(pool, iotas)
            step(pool.iota(iota_lo[:], pattern=[[1, P]], base=0, **wide))
            step(pool.iota(iota_hi[:], pattern=[[1, NHI]], base=0, **wide))
            step(pool.iota(iota_e[:], pattern=[[1, E]], base=0, **wide))
            step(pool.iota(iota_g[:], pattern=[[1, NG]], base=0, **wide))
            step(pool.iota(tile[:], pattern=[[1, CH]], base=0, **wide))
            step(pool.iota(token[:], pattern=[[0, 1]], base=1, channel_multiplier=1, allow_small_or_imprecise_dtypes=True))
            step(pool.iota(spare_row[:], pattern=[[0, NG], [P, TB]], base=NTOK + 1, channel_multiplier=1, allow_small_or_imprecise_dtypes=True))

        @block.tensor
        def _(pe):
            pe.matmul(ps[:, 1, 0:W], u["tri"][:], flat(sel), start=True, stop=True).then_inc(sums, 1)
            pe.matmul(ps[:, 2, 0:W], u["ones"][:], flat(sel), start=True, stop=True).then_inc(sums, 1)

            def product(j, p, first, last):
                pe.wait_ge(lo_ready[p], j + 1)
                pe.wait_ge(hi_ready[p], 2 * j + 2)
                if not two_choices:
                    pe.wait_ge(taken[p], j)
                bank = 4 if two_choices else 4 + p
                for i in range(CH):
                    ins = pe.matmul(ps[:, bank, 0:2 * NHI], lo_hot[p][:, i, :], hi_num[p][:, i, :, :].rearrange("p k h -> p (k h)"),
                                    start=(first and i == 0), stop=(last and i == CH - 1))
                ins.then_inc(listed[p], 1)

            if two_choices:
                product(0, 0, True, False)
                product(0, 1, False, True)
            else:
                with pe.Fori(0, NC // 2) as j:
                    for p in range(2):
                        product(j, p, True, True)

        @block.vector
        def _(v):
            step = Chain(v, steps)
            v.wait_ge(sums, 2)
            step(v.tensor_tensor_scan(flat(rank), flat(u["reset"]), ps[:, 2, 0:W], 0.0, ALU.mult, ALU.add))
            if two_choices:
                v.wait_ge(iotas, 7)
                step(v.tensor_scalar(groups[:], rank[:, :, NT - 1], 1.0 / BLK, (BLK - 1.0) / BLK - 0.5 + 0.5 / BLK, ALU.mult, ALU.add))
                step(v.tensor_scalar(groups[:], groups[:], MAGIC, MAGIC, ALU.add, ALU.subtract))
                step(v.memset(ones_e[:], 1.0))
                step(v.tensor_tensor_scan(first[:], ones_e[:], groups[:], 0.0, ALU.mult, ALU.add))
                step(v.tensor_tensor(first[:], first[:], groups[:], ALU.subtract))
                step(v.memset(begun[:], 0.0))
                step(v.tensor_tensor(begun[:, :, 0:E], iota_g[:].unsqueeze(2).broadcast_to([P, NG, E]),
                                     first[:].unsqueeze(1).broadcast_to([P, NG, E]), ALU.is_ge))
                step(v.tensor_tensor(u["of_expert"][:], begun[:, :, 0:E], begun[:, :, 1:E + 1], ALU.subtract))
                step(v.tensor_tensor(begun[:, :, 0:E], u["of_expert"][:], iota_e[:].unsqueeze(1).broadcast_to([P, NG, E]), ALU.mult))
                step(v.tensor_reduce(eid[:], begun[:, :, 0:E], X, ALU.add))
                step(v.tensor_scalar(eid[:], eid[:], float(P), token[:], ALU.mult, ALU.add))
                step(v.tensor_scalar(u["w_rows"][:], eid[:], -1.0, None, ALU.add))
            step(v.tensor_tensor(flat(rank), flat(rank), ps[:, 2, 0:W], ALU.subtract))
            step(v.tensor_tensor(flat(rank), flat(rank), ps[:, 1, 0:W], ALU.add))
            if two_choices:
                step(v.scalar_tensor_tensor(rank[:], first[:].unsqueeze(2).broadcast_to([P, E, NT]), float(BLK), rank[:], ALU.mult, ALU.add))
                for c, hot in enumerate(u["hots"]):
                    step(v.tensor_tensor(picked[:], hot[:], rank[:].rearrange("p e n -> p n e"), ALU.mult))
                    step(v.tensor_reduce(lo[:, c * NT:(c + 1) * NT], picked[:], X, ALU.add))
            else:
                v.wait_ge(iotas, 7)
                step(v.tensor_tensor(u["of_expert"][:], iota_g[:].unsqueeze(2).broadcast_to([P, NG, E]),
                                     iota_e[:].unsqueeze(1).broadcast_to([P, NG, E]), ALU.is_equal))
                step(v.tensor_copy(lo[:], flat(rank)))
            step(v.tensor_scalar(hi[:], lo[:], 1.0 / P, -0.5 + 0.5 / P, ALU.mult, ALU.add))
            step(v.tensor_scalar(hi[:], hi[:], MAGIC, MAGIC, ALU.add, ALU.subtract))
            step(v.scalar_tensor_tensor(lo[:], hi[:], -float(P), lo[:], ALU.mult, ALU.add))
            if not two_choices:
                step(v.scalar_tensor_tensor(hi[:], hi[:], 1.0, flat(sel), ALU.add, ALU.mult))
                step(v.tensor_scalar(hi[:], hi[:], -1.0, None, ALU.add))

            def chunk(j, p):
                at = bass.ds((2 * j + p) * CH, CH)
                v.wait_ge(listed[p], j)
                v.tensor_tensor(lo_hot[p][:], iota_lo[:].unsqueeze(1).broadcast_to([P, CH, P]),
                                lo[:, at].unsqueeze(2).broadcast_to([P, CH, P]), ALU.is_equal).then_inc(lo_ready[p], 1)
                v.tensor_tensor(hi_hot[p][:], iota_hi[:].unsqueeze(1).broadcast_to([P, CH, NHI]),
                                hi[:, at].unsqueeze(2).broadcast_to([P, CH, NHI]), ALU.is_equal).then_inc(hot_step[p], 1)
                v.wait_ge(hot_step[p], j + 1)
                v.tensor_scalar(hi_num[p][:, :, 0, :], hi_hot[p][:], token[:], None, ALU.mult).then_inc(hi_ready[p], 1)
                v.tensor_tensor(hi_num[p][:, :, 1, :], hi_hot[p][:], tile[:].unsqueeze(2).broadcast_to([P, CH, NHI]), ALU.mult).then_inc(hi_ready[p], 1)

            def take(j, p):
                v.wait_ge(listed[p], j + 1)
                at = bass.ds((2 * j + p) * NHI, NHI) if not two_choices else slice(0, NHI)
                bank = 4 if two_choices else 4 + p
                v.tensor_copy(nums[:, at, :].rearrange("p h k -> p k h"), ps[:, bank, 0:2 * NHI].rearrange("p (k h) -> p k h", k=2)).then_inc(taken[p], 1)

            if two_choices:
                chunk(0, 0)
                chunk(0, 1)
                take(0, 1)
                v.wait_ge(taken[1], 1)
            else:
                chunk(0, 0)
                with v.Fori(0, NC // 2 - 1) as j:
                    chunk(j, 1)
                    take(j, 0)
                    chunk(j + 1, 0)
                    take(j, 1)
                chunk(NC // 2 - 1, 1)
                take(NC // 2 - 1, 0)
                take(NC // 2 - 1, 1)
                v.wait_ge(taken[0], NC // 2)
                v.wait_ge(taken[1], NC // 2)
            step(v.scalar_tensor_tensor(slot[:], nums[:, :, 1], float(P), nums[:, :, 0], ALU.mult, ALU.add))
            step(v.scalar_tensor_tensor(none[:], slot[:], 0.0, spare_row[:], ALU.is_equal, ALU.mult))
            step(v.scalar_tensor_tensor(slot[:], slot[:], -1.0, none[:], ALU.add, ALU.add))
            step(v.tensor_copy(u["slots"][:], slot[:]))


def gathered_experts(nc, u, d, stage, E, NG, C, kind, bias1=False, bias2=False):
    nin = 2 if kind == "glu" else 1
    width = (nin + 1) * C * P + (C if bias1 else 0) + (D if bias2 else 0)
    HB = C // 2
    RW = D + E
    chosen = "w_rows" in u
    with ExitStack() as ctx:
        s = Sems(nc, ctx, stage)
        w_came, x_came, x_turned, x_kept, weighed, w_step = (
            s.two("w_came"), s.two("x_came"), s.two("x_turned"), s.two("x_kept"), s.two("weighed"), s.two("w_step"))
        gi_ready, si_ready, wi_ready, spare_step = s.two("gi_ready"), s.two("si_ready"), s.two("wi_ready"), s.one("spare_step")
        made, acted, h_ready, down_made, y_ready, added = (
            s.two("made"), s.two("acted"), s.two("h_ready"), s.two("down_made"), s.two("y_ready"), s.two("added"))
        back = [s.one(f"back{q}") for q in range(4)]
        ps = u["ps"]

        def sb2(name, shape, dt=F32):
            return [ctx.enter_context(nc.sbuf_tensor(f"{stage}_g_{name}{p}", shape, dt)) for p in range(2)]

        wb, xg, xgT, h, ga = sb2("w", [P, width]), sb2("xg", [P, TB, RW]), sb2("xgT", [P, BLK]), sb2("h", [P, C, BLK]), sb2("ga", [P, BLK])
        wmul, wsel, y = sb2("wmul", [P, TB, E]), sb2("wsel", [P, TB]), sb2("y", [P, TB, D])
        gi, si, wi, spare = sb2("gi", [P, TB], I32), sb2("si", [P, TB], I32), sb2("wi", [P, 1], I32), sb2("spare", [P, 1])
        block = ctx.enter_context(nc.Block())

        def at(g):
            return g // 2, g % 2

        def run(eng, turn, up, down, start=None):
            turn(0, 0)
            with eng.Fori(0, (NG - 1) // 2) as j:
                for p in range(2):
                    up(j, p)
                    turn(j + p, 1 - p)
                    down(j, p)
            for g in range((NG - 1) // 2 * 2, NG):
                up(*at(g))
                if g + 1 < NG:
                    turn(*at(g + 1))
                down(*at(g))

        def chunk_free(eng, j, p, c):
            if c >= 2:
                eng.wait_ge(h_ready[p], j * C + c - 1)
            elif p == 1:
                eng.wait_ge(h_ready[0], j * C + C - 1 + c)
            else:
                eng.wait_ge(h_ready[1], j * C)

        def group(j, p):
            return bass.ds(2 * j + p, 1)

        @block.gpsimd
        def _(pool):
            def load_rows(j, p):
                pool.wait_ge(x_turned[p], j)
                pool.wait_ge(weighed[p], j)
                pool.tensor_copy(gi[p][:], u["slots"][:, bass.ds((2 * j + p) * TB, TB)]).then_inc(gi_ready[p], 1)
                pool.wait_ge(gi_ready[p], j + 1)
                pool.tensor_tensor(spare[0][:], spare[1][:], spare[1][:], ALU.add)
                for i in range(TB):
                    pool.indirect_dma_start(out=xg[p][:, i, :], out_offset=None, in_=u["rows"],
                                            in_offset=bass.IndirectOffsetOnAxis(ap=gi[p][:, i:i + 1], axis=0)).then_inc(x_came[p], 16)

            def load_weights(j, p):
                if chosen:
                    pool.wait_ge(down_made[p], j)
                    pool.tensor_copy(wi[p][:], u["w_rows"][:, group(j, p)]).then_inc(wi_ready[p], 1)
                    pool.wait_ge(wi_ready[p], j + 1)
                    pool.tensor_tensor(spare[0][:], spare[1][:], spare[1][:], ALU.add)
                    pool.indirect_dma_start(out=wb[p][:], out_offset=None, in_=d[f"{stage}_W"],
                                            in_offset=bass.IndirectOffsetOnAxis(ap=wi[p][:, 0:1], axis=0)).then_inc(w_came[p], 16)

            def add_rows(j, p):
                pool.wait_ge(y_ready[p], j + 1)
                pool.wait_ge(added[p], 16 * TB * j)
                pool.wait_ge(added[1 - p], 16 * TB * (j + p))
                pool.tensor_copy(si[p][:], u["slots"][:, bass.ds((2 * j + p) * TB, TB)]).then_inc(si_ready[p], 1)
                pool.wait_ge(si_ready[p], j + 1)
                pool.tensor_tensor(spare[0][:], spare[1][:], spare[1][:], ALU.add)
                for i in range(TB):
                    pool.indirect_dma_start(out=u["sum_rows"], out_offset=bass.IndirectOffsetOnAxis(ap=si[p][:, i:i + 1], axis=0),
                                            in_=y[p][:, i, :], in_offset=None, compute_op=ALU.add).then_inc(added[p], 16)

            pool.memset(spare[1][:], 0.0).then_inc(spare_step, 1)
            pool.wait_ge(spare_step, 1)
            for p in range(2):
                load_rows(0, p)
                load_weights(0, p)
            with pool.Fori(0, NG // 2 - 1) as j:
                for p in range(2):
                    load_rows(j + 1, p)
                    add_rows(j, p)
                    load_weights(j + 1, p)
            for g in range(NG // 2 * 2 - 2, NG):
                if g + 2 < NG:
                    load_rows(*at(g + 2))
                add_rows(*at(g))
                if g + 2 < NG:
                    load_weights(*at(g + 2))

        @block.sync
        def _(sp):
            if not chosen:
                with sp.Fori(0, NG // 2) as j:
                    for p in range(2):
                        sp.wait_ge(down_made[p], j)
                        sp.dma_start(wb[p][:], d[f"{stage}_W"][group(j, p), :, :].rearrange("e p n -> (e p) n")).then_inc(w_came[p], 16)
            sp.wait_ge(added[0], 16 * TB * ((NG + 1) // 2))
            sp.wait_ge(added[1], 16 * TB * (NG // 2))
            sums = u["sum_rows"][0:NTOK, :].rearrange("(n p) f -> p n f", p=P)
            for q in range(4):
                tiles = slice(q * NT // 4, (q + 1) * NT // 4)
                sp.dma_start(u["xc"][:].rearrange("p (n d) -> p n d", d=D)[:, tiles, :], sums[:, tiles, :]).then_inc(back[q], 16)

        @block.tensor
        def _(pe):
            def turn(j, p):
                pe.wait_ge(x_came[p], 16 * TB * (j + 1))
                pe.wait_ge(x_kept[p], j)
                for i in range(TB):
                    ins = pe.transpose(ps[:, 6 + p, i * P:(i + 1) * P], xg[p][:, i, 0:D], u["ident"][:])
                ins.then_inc(x_turned[p], 1)

            def up(j, p):
                pe.wait_ge(x_kept[p], j + 1)
                pe.wait_ge(w_came[p], 16 * (j + 1))
                for c in range(C):
                    b = c % 2
                    chunk_free(pe, j, p, c)
                    for i in range(nin):
                        ins = pe.matmul(ps[:, 2 * b + i, :], wb[p][:, (i * C + c) * P:(i * C + c + 1) * P], xgT[p][:], start=True, stop=True)
                    ins.then_inc(made[b], 1)

            def down(j, p):
                pe.wait_ge(h_ready[p], (j + 1) * C)
                pe.wait_ge(y_ready[p], j)
                for i in range(TB):
                    dst = ps[:, 4 + p, i * P:(i + 1) * P]
                    for c in range(C):
                        ins = pe.matmul(dst, h[p][:, c, i * P:(i + 1) * P], wb[p][:, (nin * C + c) * P:(nin * C + c + 1) * P],
                                        start=(c == 0), stop=(c == C - 1 and not bias2))
                    if bias2:
                        ins = pe.matmul(dst, u["ones"][0:1, 0:P], wb[p][0:1, width - D:width], start=False, stop=True)
                ins.then_inc(down_made[p], 1)

            run(pe, turn, up, down)

        @block.scalar
        def _(sc):
            def turn(j, p):
                sc.wait_ge(x_turned[p], j + 1)
                sc.activation(xgT[p][:], ps[:, 6 + p, :], ACT.Copy).then_inc(x_kept[p], 1)

            def up(j, p):
                n = (2 * j + p) * HB
                sc.wait_ge(w_came[p], 16 * (j + 1))
                for c in range(C):
                    b = c % 2
                    sc.wait_ge(made[b], n + c // 2 + 1)
                    if kind == "glu":
                        chunk_free(sc, j, p, c)
                        sc.activation(ga[b][:], ps[:, 2 * b, :], ACT.Gelu).then_inc(acted[b], 1)
                    else:
                        at_b1 = (nin + 1) * C * P + c
                        sc.wait_ge(down_made[p], j)
                        sc.activation(h[p][:, c, :], ps[:, 2 * b, :], ACT.Gelu, bias=wb[p][:, at_b1:at_b1 + 1]).then_inc(h_ready[p], 1)

            run(sc, turn, up, lambda j, p: None)

        @block.vector
        def _(v):
            def turn(j, p):
                v.wait_ge(x_came[p], 16 * TB * (j + 1))
                v.wait_ge(w_step[p], j)
                v.tensor_tensor(wmul[p][:], xg[p][:, :, D:D + E], u["of_expert"][:, group(j, p), :].broadcast_to([P, TB, E]), ALU.mult).then_inc(w_step[p], 1)
                v.wait_ge(w_step[p], j + 1)
                v.wait_ge(y_ready[p], j)
                v.tensor_reduce(wsel[p][:], wmul[p][:], X, ALU.add).then_inc(weighed[p], 1)

            def up(j, p):
                n = (2 * j + p) * HB
                if kind == "glu":
                    for c in range(C):
                        b = c % 2
                        v.wait_ge(acted[b], n + c // 2 + 1)
                        v.wait_ge(down_made[p], j)
                        v.tensor_tensor(h[p][:, c, :], ga[b][:], ps[:, 2 * b + 1, :], ALU.mult).then_inc(h_ready[p], 1)

            def down(j, p):
                v.wait_ge(down_made[p], j + 1)
                v.wait_ge(weighed[p], j + 1)
                v.wait_ge(added[p], 16 * TB * j)
                v.tensor_tensor(y[p][:], ps[:, 4 + p, :].rearrange("p (i d) -> p i d", d=D),
                                wsel[p][:].unsqueeze(2).broadcast_to([P, TB, D]), ALU.mult).then_inc(y_ready[p], 1)

            run(v, turn, up, down)
            for q in range(4):
                cols = slice(q * NT * D // 4, (q + 1) * NT * D // 4)
                v.wait_ge(back[q], 16)
                v.tensor_tensor(u["x"][:, cols], u["x"][:, cols], u["xc"][:, cols], ALU.add)


def sine_constants(nc, t, d, C=4):
    with ExitStack() as ctx:
        s = Sems(nc, ctx, "phase")
        loads, steps, angles, sines = s.one("loads"), s.one("steps"), s.one("angles"), s.one("sines")

        def sb(name, n):
            return ctx.enter_context(nc.sbuf_tensor("phase_" + name, [P, n], F32))

        inp, turns, whole, sc2, tmp = sb("inp", 4 * C), sb("turns", 2 * C), sb("whole", 2 * C), sb("sc2", 2 * C), sb("tmp", C)
        theta, wr, wi, b1 = (inp[:, k * C:(k + 1) * C] for k in range(4))
        block = ctx.enter_context(nc.Block())

        @block.sync
        def _(sp):
            sp.dma_start(inp[:], d["l2f_phase"]).then_inc(loads, 16)

        @block.vector
        def _(v):
            step = Chain(v, steps)
            v.wait_ge(loads, 16)
            step(v.tensor_scalar(turns[:, 0:C], theta, INV_2PI, None, ALU.mult))
            step(v.tensor_scalar(turns[:, C:2 * C], turns[:, 0:C], 0.25, None, ALU.add))
            step(v.tensor_scalar(whole[:], turns[:], MAGIC, MAGIC, ALU.add, ALU.subtract))
            k0 = whole[:, 0:C]
            step(v.scalar_tensor_tensor(tmp[:], k0, -6.28125, theta, ALU.mult, ALU.add))
            step(v.scalar_tensor_tensor(tmp[:], k0, -0.0019350051879882812, tmp[:], ALU.mult, ALU.add))
            step(v.scalar_tensor_tensor(tmp[:], k0, -3.019916050561733e-07, tmp[:], ALU.mult, ALU.add))
            step(v.tensor_scalar(turns[:, 0:C], tmp[:], INV_2PI, None, ALU.mult))
            step(v.tensor_scalar(turns[:, C:2 * C], turns[:, 0:C], 0.25, None, ALU.add))
            step(v.scalar_tensor_tensor(t["phase"][:], b1, 0.1 * INV_2PI, turns[:, 0:C], ALU.mult, ALU.add))
            step(v.tensor_scalar(whole[:], turns[:], MAGIC, MAGIC, ALU.add, ALU.subtract))
            v.tensor_tensor(turns[:], turns[:], whole[:], ALU.subtract).then_inc(angles, 1)
            v.wait_ge(sines, 1)
            step(v.tensor_tensor(tmp[:], sc2[:, 0:C], wi, ALU.mult))
            step(v.tensor_tensor(sc2[:, C:2 * C], sc2[:, C:2 * C], wr, ALU.mult))
            step(v.tensor_tensor(tmp[:], tmp[:], sc2[:, C:2 * C], ALU.add))
            step(v.scalar_tensor_tensor(t["amp"][:], tmp[:], 0.1, wi, ALU.mult, ALU.mult))

        @block.scalar
        def _(sc):
            sc.wait_ge(angles, 1)
            sc.activation(sc2[:], turns[:], ACT.Sin, scale=TWO_PI).then_inc(sines, 1)



def build(nc, d, out, stages=range(8)):
    with ExitStack() as ctx:
        t = {}

        def sb(name, shape, dt=F32):
            t[name] = ctx.enter_context(nc.sbuf_tensor(f"sb_{name}", shape, dt))

        def sb2(name, shape, dt=F32):
            t[name] = [ctx.enter_context(nc.sbuf_tensor(f"sb_{name}{p}", shape, dt)) for p in range(2)]

        sb("x", [P, NT * D])
        sb("xc", [P, NT * D])
        sb("xnT", [P, NTOK])
        sb("ctxT", [P, NT * KEYS])
        sb("graw", [P, 8])
        sb("gate", [P, 8])
        sb("ident", [P, P])
        sb("identb", [P, P], BF16)
        sb("ones", [P, P])
        sb("minus_half", [P, 256])
        sb("tri", [P, P])
        sb("plus_half", [P, 32])
        sb("headmask", [P, HEADS])
        sb("blockones", [P, P])
        sb("onespad", [KEYS, HG, 32])
        sb("small", [P, 256])
        sb("eps", [P, 1])
        sb("phase", [P, 4])
        sb("amp", [P, 4])
        sb("row_any", [P, NT])
        sb("wstat", [P, 512])
        sb("cols", [P, 16])
        sb("row", [1, 2 * D])
        sb2("stage", [P, BLK])
        sb2("Vpad", [KEYS, HEADS, 32])
        sb2("maski", [P, 8 * KEYS], I32)
        sb("maskf", [P, 8 * KEYS])
        sb2("maskb", [P, KEYS], BF16)
        t["ps"] = ctx.enter_context(nc.psum_tensor("ps", [P, 8, 512], F32))

        def attention_stage(*a, **k):
            with ExitStack() as own:
                u = dict(t)
                for name, shape in (("qk", [P, P + KEYS]), ("kblk", [P, HEADS * KEYS]), ("prob", [P, HEADS, KEYS]),
                                    ("pt", [KEYS, HG, GROUPS, P]), ("oT", [P, P]), ("rden", [P, HEADS]), ("rowmax", [P, HEADS]),
                                    ("rowsum", [P, HEADS])):
                    u[name] = [own.enter_context(nc.sbuf_tensor(f"{a[0]}_{name}{p}", shape, F32)) for p in range(2)]
                attention(nc, u, d, *a, **k)

        def routed(stage, E, NG, gate_at, select, norm, *a, two_choices=False, **kw):
            with ExitStack() as own:
                u = dict(t)

                def sb(name, shape, dt=F32):
                    return own.enter_context(nc.sbuf_tensor(f"{stage}_route_{name}", shape, dt))

                u["scores"], u["comb"], u["sel"], u["reset"] = sb("scores", [P, NT, E]), sb("comb", [P, E, NT]), sb("sel", [P, E, NT]), sb("reset", [P, E, NT])
                u["slots"], u["of_expert"] = sb("slots", [P, NG * TB], I32), sb("of_expert", [P, NG, E])
                if two_choices:
                    u["hots"] = [sb("one", [P, NT, E]), sb("two", [P, NT, E])]
                    u["w_rows"] = sb("w_rows", [P, NG], I32)
                u["rows"] = nc.dram_tensor(stage + "_rows", (NTOK + BLK, D + E), F32).ap()
                u["sum_rows"] = nc.dram_tensor(stage + "_sum_rows", (NTOK + BLK, D), F32).ap()
                route_scores(nc, u, d, stage, E, norm)
                select(u)
                token_rows(nc, u, stage, E)
                slot_lists(nc, u, stage, E, NG, two_choices)
                gathered_experts(nc, u, d, stage, E, NG, *a, **kw)

        constants(nc, t, d)
        if 0 in stages:
            layernorm(nc, t, "ln0")
            concat_linear(nc, t, d)
        if 1 in stages:
            layernorm(nc, t, "ln1")
            quantised_ffn(nc, t, d, 4)
        if 2 in stages:
            layernorm(nc, t, "ln2")
            attention_stage("l1x", 1, bias_qk=True, bias_v=True, bias_out=True)
        if 3 in stages:
            layernorm(nc, t, "ln3")
            routed("l1f", 8, (2 * NTOK + 8 * (BLK - 1)) // BLK, 5, lambda u: top_two(nc, u, 8, 5), True, 4, "gelu", two_choices=True, bias1=True, bias2=True)
        if 4 in stages:
            layernorm(nc, t, "ln4")
            with ExitStack() as own:
                t["kT"] = own.enter_context(nc.sbuf_tensor("sb_kT", [P, NT * KEYS], F32))
                rms_qk(nc, t, d, "l2x")
                attention_stage("l2x", 2, ready_qk=True)
        if 5 in stages:
            layernorm(nc, t, "ln5")
            sine_constants(nc, t, d)
            experts(nc, t, d, "l2f", 1, 4, "sine", gate_at=6, bias1=True, bias2=True)
        if 6 in stages:
            mask_rows(nc, t, d)
            layernorm(nc, t, "ln6", row_any=t["row_any"][:])
            attention_stage("l3x", 3, bias_out=True, masked=True)
        if 7 in stages:
            layernorm(nc, t, "ln7")
            routed("l3f", 16, 16, 7, lambda u: top_tokens(nc, u, 16, BLK, 7), False, 4, "glu")
            experts(nc, t, d, "l3s", 1, 2, "glu", gate_at=7)
        with ExitStack() as c2:
            stored = c2.enter_context(nc.semaphore("stored"))
            block = c2.enter_context(nc.Block())

            @block.sync
            def _(sp):
                sp.dma_start(out, t["x"][:]).then_inc(stored, 16)
                sp.wait_ge(stored, 16)


def laid_out(i):
    import numpy as np
    a = {k: np.asarray(v) for k, v in i.items()}
    f = {}
    f["x"] = a["x"].transpose(1, 0, 2).reshape(P, NT * D)
    f["ctxT"] = a["ctx_1024"].transpose(2, 0, 1).reshape(D, NT * KEYS)
    f["mask"] = a["mask_BxSxS2_if1"].transpose(1, 0, 2).reshape(P, NT * KEYS)
    f["g_xattn"], f["g_ffn"] = a["g_xattn"], a["g_ffn"]
    f["l0_WT"] = a["L0_xattn_W"].T.reshape(2, D, D).transpose(1, 0, 2).reshape(D, 2 * D)
    f["l0_b"] = a["L0_xattn_b"][None]
    w, b = a["L1_xattn_in_proj_weight"], a["L1_xattn_in_proj_bias"]
    f["l1x_W"] = np.concatenate([w.T, a["L1_xattn_out_w"].T], 1)
    f["l1x_bqk"] = b[:2 * D].reshape(2, D).T
    f["l1x_bv"], f["l1x_bo"] = b[None, 2 * D:], a["L1_xattn_out_b"][None]
    f["l2x_W"] = np.concatenate([a["L2_xattn_Wq"], a["L2_xattn_Wkv"], a["L2_xattn_Wproj"]], 1)
    f["l2x_gamma"] = np.stack([np.tile(a["L2_xattn_q_gamma"], HEADS), np.tile(a["L2_xattn_k_gamma"], HEADS)], 1)
    f["l3x_W"] = np.concatenate([a[f"L3_xattn_W{c}"].T for c in "qkvo"], 1)
    f["l3x_bo"] = a["L3_xattn_bo"][None]
    def rows(w):
        E, F, _ = w.shape
        return w.reshape(E, F // P, P, D).transpose(0, 2, 1, 3).reshape(E, P, F // P * D)

    def column(b):
        E, F = b.shape
        return b.reshape(E, F // P, P).transpose(0, 2, 1)

    up, gate, down = a["L0_ffn_w_up"], a["L0_ffn_w_gate"], a["L0_ffn_w_down"]
    f["l0f_W"] = np.concatenate([rows(up[None])[0], rows(gate[None])[0], down], 1)
    f["l1f_proj"], f["l1f_vec"], f["l1f_temp"] = a["L1_ffn_Wp"].T, a["L1_ffn_sim_matrix"], a["L1_ffn_temperature"].reshape(1)
    b2 = np.broadcast_to(a["L1_ffn_b2"][:, None], (8, P, D))
    f["l1f_W"] = np.concatenate([a["L1_ffn_W1"], rows(a["L1_ffn_W2"]), column(a["L1_ffn_b1"]), b2], 2).reshape(8 * P, -1)
    f["l2f_W"] = np.concatenate([a["L2_ffn_W1"][None], rows(a["L2_ffn_W2"][None]), column(a["L2_ffn_b1"][None])], 2)
    f["l2f_b2"] = a["L2_ffn_b2"][None]
    f["l2f_phase"] = np.concatenate([column(a[f"L2_ffn_{n}"][None])[0] for n in ("quantum_phases", "quantum_weights_real", "quantum_weights_imag", "b1")], 1)
    f["l3f_G"] = a["L3_ffn_gate_w"].T
    turn = lambda w: w.transpose(0, 2, 1)
    f["l3f_W"] = np.concatenate([turn(a["L3_ffn_Wg"]), turn(a["L3_ffn_Wu"]), rows(turn(a["L3_ffn_Wd"]))], 2)
    f["l3s_W"] = np.concatenate([turn(a["L3_ffn_Sg"][None]), turn(a["L3_ffn_Su"][None]), rows(turn(a["L3_ffn_Sd"][None]))], 2)
    return {k: np.ascontiguousarray(v) for k, v in f.items()}


def kernel(**inputs):
    import concourse.bacc as bacc
    from concourse.bass_utils import run_bass_kernel_spmd

    nc = bacc.Bacc("TRN2", target_bir_lowering=False, num_devices=1)
    arrays = laid_out(inputs)
    d = {k: nc.dram_tensor(k, v.shape, mybir.dt.from_np(v.dtype), kind="ExternalInput").ap() for k, v in arrays.items()}
    out = nc.dram_tensor("out", (P, NT * D), F32, kind="ExternalOutput").ap()
    build(nc, d, out)
    r = run_bass_kernel_spmd(nc, [arrays], core_ids=[0]).results[0]["out"]
    return r.reshape(P, NT, D).transpose(1, 0, 2)
```

```python
from contextlib import ExitStack

import concourse.bass as bass
from concourse import mybir

F32 = mybir.dt.float32
BF16 = mybir.dt.bfloat16
I32 = mybir.dt.int32
ALU = mybir.AluOpType
ACT = mybir.ActivationFunctionType
X = mybir.AxisListType.X
RMAX = bass.bass_isa.ReduceOp.max

P = 128
D = 128
NT = 32
KEYS = 77
HEADS = 16
HD = D // HEADS
GROUPS = 4
HG = HEADS // GROUPS
NTOK = NT * P
BLK = 512
NBLK = NTOK // BLK
TB = BLK // P
MAGIC = 12582912.0
NEG = -1e9
S_BANKS = [(0, 6), (6, 6), (12, 4)]
INV_2PI = 0.15915494309189535
TWO_PI = 6.283185


def act(eng, out, in_, func, **kw):
    return eng.activation(out, in_, func, **kw)


class Sems:

    def __init__(self, nc, ctx, stage):
        self.nc, self.stage, self.made = nc, stage, []
        ctx.callback(self.clear)

    def one(self, name):
        self.made.append(self.nc.alloc_semaphore(f"{self.stage}_{name}"))
        return self.made[-1]

    def two(self, name):
        return [self.one(f"{name}{p}") for p in range(2)]

    def clear(self):
        self.nc.clear_and_free_semaphores(self.made)
        self.nc.all_engine_barrier()


class Chain:

    def __init__(self, eng, sem):
        self.eng, self.sem, self.n = eng, sem, 0

    def __call__(self, ins):
        ins.then_inc(self.sem, 1)
        self.n += 1
        self.eng.wait_ge(self.sem, self.n)


def constants(nc, t, d):
    with ExitStack() as ctx:
        s = Sems(nc, ctx, "const")
        ident0, ident1, masks, ones_ready = s.one("ident0"), s.one("ident1"), s.one("masks"), s.one("ones_ready")
        loads, gates = s.one("loads"), s.one("gates")
        pool_steps = s.one("pool_steps")
        block = ctx.enter_context(nc.Block())

        @block.sync
        def _(sp):
            sp.dma_start(t["x"][:], d["x"]).then_inc(loads, 16)
            sp.dma_start(t["ctxT"][:], d["ctxT"]).then_inc(loads, 16)
            sp.dma_start(t["graw"][:, 0:4], d["g_xattn"].partition_broadcast(P)).then_inc(loads, 16)
            sp.dma_start(t["graw"][:, 4:8], d["g_ffn"].partition_broadcast(P)).then_inc(loads, 16)
            sp.wait_ge(loads, 64)

        @block.gpsimd
        def _(pool):
            step = Chain(pool, pool_steps)
            step(pool.memset(t["ident"][:], 0.0))
            step(pool.affine_select(out=t["ident"][:], in_=t["ident"][:], compare_op=ALU.not_equal, fill=1.0,
                                    base=0, pattern=[[-1, P]], channel_multiplier=1))
            step(pool.tensor_copy(t["identb"][:], t["ident"][:]))
            step(pool.memset(t["ones"][:], 1.0))
            step(pool.memset(t["headmask"][:], 1.0))
            step(pool.affine_select(out=t["headmask"][:], in_=t["headmask"][:], compare_op=ALU.is_ge, fill=0.0,
                                    base=0, pattern=[[-HD, HEADS]], channel_multiplier=1))
            step(pool.affine_select(out=t["headmask"][:], in_=t["headmask"][:], compare_op=ALU.is_ge, fill=0.0,
                                    base=HD - 1, pattern=[[HD, HEADS]], channel_multiplier=-1))
            step(pool.tensor_scalar(t["blockones"][:].rearrange("p (h d) -> p h d", d=HD),
                                    t["headmask"][:].unsqueeze(2).broadcast_to([P, HEADS, HD]),
                                    1.0 / HD, None, ALU.mult))
            step(pool.memset(t["onespad"][:], 0.0))
            for i in range(HG):
                step(pool.memset(t["onespad"][:, i, HD * i:HD * i + HD], 1.0))
            step(pool.memset(t["eps_ln"][:], 1e-5))
            step(pool.memset(t["plus_half"][:], 0.5))
            step(pool.memset(t["eps"][:], 1e-6))
            for b in range(2):
                step(pool.memset(t["Vpad"][b][:], 0.0))
            step(pool.memset(t["tri"][:], 1.0))
            step(pool.affine_select(out=t["tri"][:], in_=t["tri"][:], compare_op=ALU.is_ge, fill=0.0, base=-1, pattern=[[1, P]], channel_multiplier=-1))

        @block.scalar
        def _(sc):
            sc.wait_ge(loads, 64)
            sc.activation(t["gate"][:], t["graw"][:], ACT.Tanh).then_inc(gates, 1)


def layernorm(nc, t, stage, row_any=None):
    Q, QT = 4, NT // 4
    with ExitStack() as ctx:
        s = Sems(nc, ctx, stage)
        steps, mean_ready, centred, squared, var_ready, rooted, scaled, turned, kept = (
            s.one("steps"), s.one("mean_ready"), s.one("centred"), s.one("squared"), s.one("var_ready"), s.one("rooted"),
            s.two("scaled"), s.two("turned"), s.two("kept"))
        ps = t["ps"]
        small = t["small"]
        mean, var, rstd = (small[:, i * NT:(i + 1) * NT] for i in range(3))
        by_tile = lambda a: a[:].rearrange("p (n d) -> p n d", d=D)
        x3, xc3, sq3 = by_tile(t["x"]), by_tile(t["xc"]), by_tile(t["xnT"])
        tiles = lambda c: slice(c * QT, (c + 1) * QT)
        wide = lambda a: a.unsqueeze(2).broadcast_to([P, a.shape[1], D])
        BQ = NBLK // Q
        block = ctx.enter_context(nc.Block())

        @block.vector
        def _(v):
            step = Chain(v, steps)
            for at in range(Q + 2):
                if at < Q:
                    c = tiles(at)
                    step(v.tensor_reduce(mean[:, c], x3[:, c, :], X, ALU.add))
                    v.tensor_scalar(mean[:, c], mean[:, c], 1.0 / D, None, ALU.mult).then_inc(mean_ready, 1)
                if 1 <= at <= Q:
                    c = tiles(at - 1)
                    v.wait_ge(squared, at)
                    v.tensor_reduce(var[:, c], sq3[:, c, :], X, ALU.add).then_inc(var_ready, 1)
                if at >= 2:
                    c = tiles(at - 2)
                    v.wait_ge(rooted, at - 1)
                    step(v.reciprocal(rstd[:, c], rstd[:, c]))
                    if row_any is not None:
                        step(v.tensor_tensor(rstd[:, c], rstd[:, c], row_any[:, c], ALU.mult))
                    for b in range((at - 2) * BQ, (at - 1) * BQ):
                        p = b % 2
                        if b >= 2:
                            v.wait_ge(turned[p], b // 2)
                        v.tensor_tensor(by_tile(t["stage"][p]), xc3[:, b * TB:(b + 1) * TB, :], wide(rstd[:, b * TB:(b + 1) * TB]),
                                        ALU.mult).then_inc(scaled[p], 1)

        @block.gpsimd
        def _(pool):
            for at in range(Q):
                c = tiles(at)
                pool.wait_ge(mean_ready, at + 1)
                pool.tensor_tensor(xc3[:, c, :], x3[:, c, :], wide(mean[:, c]), ALU.subtract).then_inc(centred, 1)

        @block.tensor
        def _(pe):
            for b in range(NBLK):
                p = b % 2
                pe.wait_ge(scaled[p], b // 2 + 1)
                if b >= 2:
                    pe.wait_ge(kept[p], b // 2)
                for i in range(TB):
                    ins = pe.transpose(ps[:, p, i * P:i * P + P], t["stage"][p][:, i * P:i * P + P], t["ident"][:])
                ins.then_inc(turned[p], 1)

        @block.scalar
        def _(sc):
            for at in range(Q + 2):
                if at < Q:
                    c = tiles(at)
                    sc.wait_ge(centred, at + 1)
                    sc.activation(sq3[:, c, :], xc3[:, c, :], ACT.Square).then_inc(squared, 1)
                if 1 <= at <= Q:
                    c = tiles(at - 1)
                    sc.wait_ge(var_ready, at)
                    sc.activation(rstd[:, c], var[:, c], ACT.Sqrt, scale=1.0 / D, bias=t["eps_ln"][:]).then_inc(rooted, 1)
                if at >= 2:
                    for b in range((at - 2) * BQ, (at - 1) * BQ):
                        p = b % 2
                        sc.wait_ge(turned[p], b // 2 + 1)
                        sc.activation(t["xnT"][:, b * BLK:(b + 1) * BLK], ps[:, p, :], ACT.Copy).then_inc(kept[p], 1)


def concat_linear(nc, t, d):
    with ExitStack() as ctx:
        s = Sems(nc, ctx, "l0x")
        loads, sum_ready, mean_ready, linear, residual, staged = (
            s.one("loads"), s.one("sum_ready"), s.two("mean_ready"), s.two("linear"), s.two("residual"), s.two("staged"))
        ps = t["ps"]
        w = t["wstat"]
        means = [ctx.enter_context(nc.sbuf_tensor(f"l0x_means{p}", [P, TB, P], F32)) for p in range(2)]
        block = ctx.enter_context(nc.Block())

        @block.sync
        def _(sp):
            sp.dma_start(w[:, 0:256], d["l0_WT"]).then_inc(loads, 16)
            sp.dma_start(t["row"][:, 0:D], d["l0_b"]).then_inc(loads, 16)

        @block.scalar
        def _(sc):
            with sc.Fori(0, NBLK // 2) as j:
                for p in range(2):
                    sc.wait_ge(linear[p], j)
                    sc.activation(t["stage"][p][:], t["xnT"][:, bass.ds((2 * j + p) * BLK, BLK)], ACT.Copy).then_inc(staged[p], 1)

        @block.vector
        def _(v):
            ctx_sum = t["small"][:, 0:NT]
            v.tensor_reduce(ctx_sum, t["ctxT"][:].rearrange("p (n k) -> p n k", k=KEYS), X, ALU.add).then_inc(sum_ready, 1)
            v.wait_ge(sum_ready, 1)

            def mean(j, p):
                v.wait_ge(linear[p], j)
                v.tensor_scalar(means[p][:], t["small"][:, bass.ds((2 * j + p) * TB, TB)].unsqueeze(2).broadcast_to([P, TB, P]),
                                1.0 / KEYS, None, ALU.mult).then_inc(mean_ready[p], 1)

            def add(j, p):
                v.wait_ge(linear[p], j + 1)
                xb = t["x"][:, bass.ds((2 * j + p) * BLK, BLK)]
                v.scalar_tensor_tensor(xb, ps[:, p, :], t["gate"][:, 0:1], xb, ALU.mult, ALU.add).then_inc(residual[p], 1)

            mean(0, 0)
            mean(0, 1)
            with v.Fori(0, NBLK // 2 - 1) as j:
                for p in range(2):
                    add(j, p)
                    mean(j + 1, p)
            for p in range(2):
                add(NBLK // 2 - 1, p)

        @block.tensor
        def _(pe):
            pe.wait_ge(loads, 32)
            with pe.Fori(0, NBLK // 2) as j:
                for p in range(2):
                    pe.wait_ge(residual[p], j)
                    pe.wait_ge(mean_ready[p], j + 1)
                    pe.wait_ge(staged[p], j + 1)
                    for i in range(TB):
                        dst = ps[:, p, i * P:(i + 1) * P]
                        pe.matmul(dst, t["stage"][p][:, i * P:(i + 1) * P], w[:, 0:128], start=True, stop=False)
                        pe.matmul(dst, means[p][:, i, :], w[:, 128:256], start=False, stop=False)
                        ins = pe.matmul(dst, t["ones"][0:1, 0:P], t["row"][0:1, 0:D], start=False, stop=True)
                    ins.then_inc(linear[p], 1)


def mask_rows(nc, t, d):
    with ExitStack() as ctx:
        s = Sems(nc, ctx, "rows")
        came, read, steps = s.two("came"), s.two("read"), s.one("steps")
        block = ctx.enter_context(nc.Block())
        n = 8

        @block.sync
        def _(sp):
            for c in range(NT // n):
                if c >= 2:
                    sp.wait_ge(read[c % 2], c // 2)
                sp.dma_start(t["maski"][c % 2][:], d["mask"][:, c * n * KEYS:(c + 1) * n * KEYS]).then_inc(came[c % 2], 16)

        @block.vector
        def _(v):
            step = Chain(v, steps)
            for c in range(NT // n):
                v.wait_ge(came[c % 2], 16 * (c // 2 + 1))
                nz = t["maskf"][:, 0:n * KEYS]
                v.tensor_scalar(nz, t["maski"][c % 2][:], 0.0, None, ALU.not_equal).then_inc(read[c % 2], 1)
                v.wait_ge(read[c % 2], c // 2 + 1)
                step(v.tensor_reduce(t["row_any"][:, c * n:c * n + n], nz.rearrange("p (n k) -> p n k", k=KEYS), X, ALU.max))

def rms_qk(nc, t, d, layer):
    KB = 352
    assert KB * 7 == NT * KEYS
    PACK = P // HEADS
    with ExitStack() as ctx:
        s = Sems(nc, ctx, layer + "n")
        loads, consts, made, kept, squared, summed, rooted, inverted, spread, normed = (
            s.one("loads"), s.one("consts"), s.two("made"), s.two("kept"), s.two("squared"), s.two("summed"), s.one("rooted"),
            s.one("inverted"), s.two("spread"), s.two("normed"))
        ps, w = t["ps"], t["wstat"]
        raw_sq = t["stage"]
        to_heads = ctx.enter_context(nc.sbuf_tensor("rms_to_heads", [P, 2 * P - HEADS], F32))
        to_features = ctx.enter_context(nc.sbuf_tensor("rms_to_features", [P, PACK, P], F32))
        root = [t["xc"][:, i * BLK:(i + 1) * BLK] for i in range(2)]
        inv = [t["xc"][:, (2 + i) * BLK:(3 + i) * BLK] for i in range(2)]
        q_part = [(0, b, t["xnT"], t["xnT"], w[:, 0:128], t["cols"][:, 0:1], BLK) for b in range(NBLK)]
        k_part = [(1, b, t["ctxT"], t["kT"], w[:, 128:256], t["cols"][:, 1:2], KB) for b in range(7)]
        blocks = q_part + k_part
        N = len(blocks)
        last = (NBLK - 1, N - 1)
        block = ctx.enter_context(nc.Block())

        @block.sync
        def _(sp):
            sp.dma_start(w[:, 0:256], d[f"{layer}_W"][:, 0:256]).then_inc(loads, 16)
            sp.dma_start(t["cols"][:, 0:2], d[f"{layer}_gamma"]).then_inc(loads, 16)

        @block.gpsimd
        def _(pool):
            step = Chain(pool, consts)
            step(pool.memset(to_heads[:], 0.0))
            step(pool.tensor_scalar(to_heads[:, P - HEADS:P], t["headmask"][:], 1.0 / HD, None, ALU.mult))
            step(pool.memset(to_features[:], 0.0))
            step(pool.affine_select(out=to_features[:].rearrange("p b (h d) -> p b h d", d=HD), in_=to_features[:].rearrange("p b (h d) -> p b h d", d=HD),
                                    compare_op=ALU.not_equal, fill=1.0, base=0, pattern=[[-HEADS, PACK], [-1, HEADS], [0, HD]], channel_multiplier=1))

        @block.tensor
        def _(pe):
            pe.wait_ge(loads, 32)
            pe.wait_ge(consts, 4)
            for i in range(N + 1):
                if i < N:
                    part, b, src, dst, wt, gamma, n = blocks[i]
                    p = i % 2
                    if i >= 2:
                        pe.wait_ge(kept[p], i // 2)
                        pe.wait_ge(squared[p], i // 2)
                    pe.matmul(ps[:, p, 0:n], wt, src[:, b * n:(b + 1) * n], start=True, stop=True).then_inc(made[p], 1)
                if i >= 1:
                    part, b, src, dst, wt, gamma, n = blocks[i - 1]
                    p = (i - 1) % 2
                    pe.wait_ge(squared[p], (i - 1) // 2 + 1)
                    first = P - HEADS - HEADS * b
                    pe.matmul(ps[:, 2 + part, 0:n], to_heads[:, first:first + P], raw_sq[p][:, 0:n],
                              start=(b == 0), stop=(i - 1 in last)).then_inc(summed[p], 1)
            for i, (part, b, src, dst, wt, gamma, n) in enumerate(blocks):
                p = i % 2
                if b == 0:
                    pe.wait_ge(inverted, part + 1)
                if i >= 2:
                    pe.wait_ge(normed[p], i // 2)
                pe.matmul(ps[:, 4 + p, 0:n], to_features[:, b, :], inv[part][:, 0:n], start=True, stop=True).then_inc(spread[p], 1)

        @block.scalar
        def _(sc):
            for i, (part, b, src, dst, wt, gamma, n) in enumerate(blocks):
                p = i % 2
                sc.wait_ge(made[p], i // 2 + 1)
                if i >= 2:
                    sc.wait_ge(summed[p], i // 2)
                sc.activation(raw_sq[p][:, 0:n], ps[:, p, 0:n], ACT.Square).then_inc(squared[p], 1)
                sc.activation(dst[:, b * n:(b + 1) * n], ps[:, p, 0:n], ACT.Copy).then_inc(kept[p], 1)
            for part, i in enumerate(last):
                n = blocks[i][-1]
                sc.wait_ge(summed[i % 2], i // 2 + 1)
                sc.activation(root[part][:, 0:n], ps[:, 2 + part, 0:n], ACT.Sqrt, bias=t["eps"][:]).then_inc(rooted, 1)

        @block.vector
        def _(v):
            v.wait_ge(loads, 32)
            for part, i in enumerate(last):
                n = blocks[i][-1]
                v.wait_ge(rooted, part + 1)
                v.reciprocal(inv[part][:, 0:n], root[part][:, 0:n]).then_inc(inverted, 1)
            for i, (part, b, src, dst, wt, gamma, n) in enumerate(blocks):
                p = i % 2
                v.wait_ge(spread[p], i // 2 + 1)
                cols = dst[:, b * n:(b + 1) * n]
                v.wait_ge(kept[p], i // 2 + 1)
                v.scalar_tensor_tensor(cols, cols, gamma, ps[:, 4 + p, 0:n], ALU.mult, ALU.mult).then_inc(normed[p], 1)


def attention(nc, t, d, layer, gate_at, bias_qk=False, bias_v=False, bias_out=False, ready_qk=False, masked=False):
    with ExitStack() as ctx:
        s = Sems(nc, ctx, layer)
        loads = s.one("loads")
        ctx_staged, qk_made, qk_kept, v_made, v_kept = (
            s.two("ctx_staged"), s.two("qk_made"), s.two("qk_kept"), s.two("v_made"), s.two("v_kept"))
        kblk_ready, scores_ready, max_ready, shifted, exp_ready = (
            s.two("kblk_ready"), s.two("scores_ready"), s.two("max_ready"), s.two("shifted"), s.two("exp_ready"))
        sum_ready, recip_ready, prob_ready = s.two("sum_ready"), s.two("recip_ready"), s.two("prob_ready")
        turned, turned_kept, heads_made, heads_kept, out_made, residual = (
            s.two("turned"), s.two("turned_kept"), s.two("heads_made"), s.two("heads_kept"), s.two("out_made"),
            s.two("residual"))
        if masked:
            mask_came, mask_made, mask_step = s.two("mask_came"), s.two("mask_made"), s.two("mask_step")
        ps = t["ps"]
        w = t["wstat"]
        VB = ps[0:KEYS, 0, 256:256 + D]
        OUT = ps[:, 1, 0:D]
        OT = ps[:, 7, 0:P]
        qk, kblk, prob, pt, vpad, oT, rden = (t[n] for n in ("qk", "kblk", "prob", "pt", "Vpad", "oT", "rden"))
        scale = float(HD) ** -0.5

        def other(j, p):
            return 1 - p, j + p

        def half(a, i):
            return a[:].rearrange("p (g r) k -> p g r k", r=HG)[:, :, 2 * i:2 * i + 2, :]

        def half_row(a, i):
            return a[:].rearrange("p (g r) -> p g r", r=HG)[:, :, 2 * i:2 * i + 2]

        def skip(j, p):
            pass

        def follows(j, p):
            return None if isinstance(j, int) and 2 * j + p + 1 == NT else (j + p, 1 - p)

        def at(n):
            return n // 2, n % 2

        def run(eng, project, value, score, finish, weigh, output):
            project(0, 0)
            project(0, 1)
            value(0, 0)
            score(0, 0)
            finish(0, 0)
            project(1, 0)
            score(0, 1)
            with eng.Fori(0, NT // 2 - 2) as j:
                for p in range(2):
                    weigh(j, p)
                    finish(j + p, 1 - p)
                    project(j + 1 + p, 1 - p)
                    score(j + 1, p)
                    output(j, p)
            for n in range(NT - 4, NT):
                weigh(*at(n))
                if n + 1 < NT:
                    finish(*at(n + 1))
                if n + 3 < NT:
                    project(*at(n + 3))
                if n + 2 < NT:
                    score(*at(n + 2))
                output(*at(n))

        block = ctx.enter_context(nc.Block())

        @block.sync
        def _(sp):
            n = 16
            sp.dma_start(w[:, 0:512], d[f"{layer}_W"]).then_inc(loads, n)
            if bias_qk:
                sp.dma_start(t["cols"][:, 0:2], d[f"{layer}_bqk"]).then_inc(loads, n)
            if bias_v:
                sp.dma_start(t["row"][:, 0:D], d[f"{layer}_bv"]).then_inc(loads, n)
            if bias_out:
                sp.dma_start(t["row"][:, D:2 * D], d[f"{layer}_bo"]).then_inc(loads, n)
            if masked:
                with sp.Fori(0, NT // 2) as j:
                    for p in range(2):
                        sp.wait_ge(mask_made[p], j)
                        sp.dma_start(t["maski"][p][:, 0:KEYS], d["mask"][:, bass.ds((2 * j + p) * KEYS, KEYS)]).then_inc(mask_came[p], 16)

        n_loads = 16 * (1 + bias_qk + bias_v + bias_out)

        def tile_cols(a, j, p, width):
            return a[:, bass.ds((2 * j + p) * width, width)]

        @block.gpsimd
        def _(pool):
            def project(j, p):
                pool.wait_ge(qk_kept[p], 2 * j + 2)
                pool.wait_ge(scores_ready[p], j)
                pool.tensor_tensor(kblk[p][:].rearrange("p (h k) -> p h k", k=KEYS),
                                   qk[p][:, P:P + KEYS].unsqueeze(1).broadcast_to([P, HEADS, KEYS]),
                                   t["headmask"][:].unsqueeze(2).broadcast_to([P, HEADS, KEYS]),
                                   ALU.mult).then_inc(kblk_ready[p], 1)

            def stage(j, p):
                pool.wait_ge(v_made[p], j)
                pool.tensor_copy(t["stage"][p][:, 0:KEYS], tile_cols(t["ctxT"], j, p, KEYS)).then_inc(ctx_staged[p], 1)

            def finish(j, p):
                for i in range(2):
                    pool.wait_ge(recip_ready[p], 2 * j + 1 + i)
                    pool.tensor_tensor(half(prob[p], i), half(prob[p], i), half_row(rden[p], i).unsqueeze(3).broadcast_to([P, GROUPS, 2, KEYS]),
                                       ALU.mult).then_inc(prob_ready[p], 1)

            def weigh(j, p):
                if not isinstance(j, int) or 2 * j + p + 2 < NT:
                    stage(j + 1, p)

            stage(0, 0)
            stage(0, 1)
            run(pool, project, skip, skip, finish, weigh, skip)

        @block.tensor
        def _(pe):
            pe.wait_ge(loads, n_loads)

            def project(j, p):
                o, n = other(j, p)
                if not ready_qk:
                    pe.wait_ge(qk_kept[o], 2 * n)
                    if not isinstance(j, int) or j > 0:
                        pe.wait_ge(v_kept[p], j)
                    pe.matmul(ps[:, 0, 0:P], w[:, 0:128], tile_cols(t["xnT"], j, p, P), start=True, stop=True)
                    pe.matmul(ps[:, 0, P:P + KEYS], w[:, 128:256], tile_cols(t["ctxT"], j, p, KEYS), start=True, stop=True).then_inc(qk_made[p], 1)

            def score(j, p):
                o, n = other(j, p)
                pe.wait_ge(kblk_ready[p], j + 1)
                pe.wait_ge(shifted[o], 3 * n)
                if masked:
                    pe.wait_ge(mask_made[p], j + 1)
                for i, (h0, nh) in enumerate(S_BANKS):
                    dst = ps[:, 2 + i, 0:nh * KEYS]
                    if masked:
                        pe.matmul(dst.rearrange("p (h k) -> p h k", k=KEYS), t["identb"][:],
                                  t["maskb"][p][:].unsqueeze(1).broadcast_to([P, nh, KEYS]), start=True, stop=False)
                    ins = pe.matmul(dst, qk[p][:, 0:P], kblk[p][:, h0 * KEYS:(h0 + nh) * KEYS], start=not masked, stop=True)
                ins.then_inc(scores_ready[p], 1)

            def value(j, p):
                o, n = other(j, p)
                pe.wait_ge(ctx_staged[p], j + 1)
                pe.wait_ge(v_kept[o], n)
                if not ready_qk:
                    m = follows(j, p)
                    if m:
                        pe.wait_ge(qk_kept[m[1]], 2 * m[0] + 2)
                ins = pe.matmul(VB, t["stage"][p][:, 0:KEYS], w[:, 256:384], start=True, stop=not bias_v)
                if bias_v:
                    ins = pe.matmul(VB, t["ones"][0:1, 0:KEYS], t["row"][0:1, 0:D], start=False, stop=True)
                ins.then_inc(v_made[p], 1)

            def round_of(j, p, r):
                o, n = other(j, p)
                if r == 0:
                    pe.wait_ge(heads_kept[o], n)
                    pe.wait_ge(v_kept[p], j + 1)
                pe.wait_ge(turned_kept[p], 4 * j + r + 1)
                for g in range(GROUPS):
                    ins = pe.matmul(ps[32 * g:32 * g + 32, 7, 0:P], vpad[p][:, HG * g + r, :], pt[p][:, r, g, :],
                                    start=(r == 0), stop=(r == HG - 1), tile_position=(0, 32 * g))
                return ins

            def weigh(j, p):
                o, n = other(j, p)
                for r in range(HG):
                    if r % 2 == 0:
                        pe.wait_ge(prob_ready[p], 2 * j + 1 + r // 2)
                    if r >= 2:
                        pe.wait_ge(turned_kept[p], 4 * j + r - 1)
                    else:
                        pe.wait_ge(turned_kept[o], 4 * n)
                    for g in range(GROUPS):
                        ins = pe.transpose(ps[0:KEYS, 5 + r % 2, g * P:g * P + P], prob[p][:, HG * g + r, :], t["ident"][:])
                    ins.then_inc(turned[p], 1)
                    if r == 1 and follows(j, p):
                        value(*follows(j, p))
                    if r:
                        round_of(j, p, r - 1)
                round_of(j, p, HG - 1).then_inc(heads_made[p], 1)

            def output(j, p):
                o, n = other(j, p)
                pe.wait_ge(heads_kept[p], j + 1)
                pe.wait_ge(residual[o], n)
                ins = pe.matmul(OUT, oT[p][:], w[:, 384:512], start=True, stop=not bias_out)
                if bias_out:
                    ins = pe.matmul(OUT, t["ones"][0:1, 0:P], t["row"][0:1, D:2 * D], start=False, stop=True)
                ins.then_inc(out_made[p], 1)

            run(pe, project, value, score, skip, weigh, output)

        @block.scalar
        def _(sc):
            sc.wait_ge(loads, n_loads)

            def project(j, p):
                sc.wait_ge(scores_ready[p], j)
                sc.wait_ge(kblk_ready[p], j)
                if ready_qk:
                    q_src, k_src = tile_cols(t["xnT"], j, p, P), tile_cols(t["kT"], j, p, KEYS)
                else:
                    sc.wait_ge(qk_made[p], j + 1)
                    q_src, k_src = ps[:, 0, 0:P], ps[:, 0, P:P + KEYS]
                bq = dict(bias=t["cols"][:, 0:1]) if bias_qk else {}
                bk = dict(bias=t["cols"][:, 1:2]) if bias_qk else {}
                fn = ACT.Identity if bias_qk else ACT.Copy
                sc.activation(qk[p][:, P:P + KEYS], k_src, fn, **bk).then_inc(qk_kept[p], 1)
                sc.activation(qk[p][:, 0:P], q_src, fn, **bq).then_inc(qk_kept[p], 1)

            def value(j, p):
                sc.wait_ge(v_made[p], j + 1)
                sc.wait_ge(heads_made[p], j)
                sc.activation(bass.AP(tensor=vpad[p], offset=0, ap=[[HEADS * 32, KEYS], [HG * 32, GROUPS], [32 + HD, HG], [1, HD]]),
                              VB.rearrange("k (g i c) -> k g i c", g=GROUPS, i=HG), ACT.Copy).then_inc(v_kept[p], 1)

            def finish(j, p):
                sc.wait_ge(shifted[p], 3 * j + 3)
                for i in range(2):
                    sc.activation(half(prob[p], i), half(prob[p], i), ACT.Exp, scale=scale).then_inc(exp_ready[p], 1)

            def weigh(j, p):
                sc.wait_ge(heads_made[p], j)
                for r in range(HG):
                    sc.wait_ge(turned[p], 4 * j + r + 1)
                    sc.activation(pt[p][:, r, :, :].rearrange("k h q -> k (h q)"), ps[0:KEYS, 5 + r % 2, :], ACT.Copy).then_inc(turned_kept[p], 1)
                    if r == 1 and follows(j, p):
                        value(*follows(j, p))

            run(sc, project, value, skip, finish, weigh, skip)

        @block.vector
        def _(v):
            def project(j, p):
                if not masked:
                    return
                v.wait_ge(mask_came[p], 16 * (j + 1))
                v.wait_ge(scores_ready[p], j)
                v.wait_ge(mask_made[p], j)
                v.tensor_scalar(t["maskf"][:, p * KEYS:(p + 1) * KEYS], t["maski"][p][:, 0:KEYS], 0.0, None, ALU.is_equal).then_inc(mask_step[p], 1)
                v.wait_ge(mask_step[p], j + 1)
                v.tensor_scalar(t["maskb"][p][:], t["maskf"][:, p * KEYS:(p + 1) * KEYS], NEG / scale, None, ALU.mult).then_inc(mask_made[p], 1)

            def score(j, p):
                v.wait_ge(scores_ready[p], j + 1)
                for i, (h0, nh) in enumerate(S_BANKS):
                    v.tensor_reduce(t["rowmax"][p][:, h0:h0 + nh], ps[:, 2 + i, 0:nh * KEYS].rearrange("p (h k) -> p h k", k=KEYS), X, ALU.max).then_inc(max_ready[p], 1)
                v.wait_ge(turned[p], 4 * j)
                for i, (h0, nh) in enumerate(S_BANKS):
                    v.wait_ge(max_ready[p], 3 * j + 1 + i)
                    v.tensor_tensor(prob[p][:, h0:h0 + nh, :], ps[:, 2 + i, 0:nh * KEYS].rearrange("p (h k) -> p h k", k=KEYS),
                                    t["rowmax"][p][:, h0:h0 + nh].unsqueeze(2).broadcast_to([P, nh, KEYS]), ALU.subtract).then_inc(shifted[p], 1)

            def finish(j, p):
                v.wait_ge(prob_ready[p], 2 * j)
                for i in range(2):
                    v.wait_ge(exp_ready[p], 2 * j + 1 + i)
                    v.tensor_reduce(half_row(t["rowsum"][p], i), half(prob[p], i), X, ALU.add).then_inc(sum_ready[p], 1)
                    v.wait_ge(sum_ready[p], 2 * j + 1 + i)
                    v.reciprocal(half_row(rden[p], i), half_row(t["rowsum"][p], i)).then_inc(recip_ready[p], 1)

            def weigh(j, p):
                v.wait_ge(heads_made[p], j + 1)
                v.wait_ge(out_made[p], j)
                v.tensor_copy(oT[p][:], OT).then_inc(heads_kept[p], 1)

            def output(j, p):
                v.wait_ge(out_made[p], j + 1)
                xb = tile_cols(t["x"], j, p, P)
                v.scalar_tensor_tensor(xb, OUT, t["gate"][:, gate_at:gate_at + 1], xb, ALU.mult, ALU.add).then_inc(residual[p], 1)

            run(v, project, skip, score, finish, weigh, output)


def quantised_ffn(nc, t, d, gate_at):
    C = 3
    WB = 32
    NW = 3 * C * P // WB
    QCH = 2048
    NQ = C * NTOK // QCH
    POOL_COLS = NTOK
    with ExitStack() as ctx:
        s = Sems(nc, ctx, "l0f")
        loads, steps, own_max, all_max, wq_ready, w_turned, w_kept, x_ready = (
            s.one("loads"), s.one("steps"), s.one("own_max"), s.one("all_max"), s.one("wq_ready"), s.one("w_turned"),
            s.one("w_kept"), s.one("x_ready"))
        up_made, up_kept, gate_made, gate_kept = s.one("up_made"), s.one("up_kept"), s.one("gate_made"), s.one("gate_kept")
        gate_ready, up_ready, sig_ready, sig_used, sig_step, o_ready = (
            s.one("gate_ready"), s.one("up_ready"), s.two("sig_ready"), s.two("sig_used"), s.two("sig_step"), s.two("o_ready"))
        scales, up_rounded, product, sig_raw, o_step, magic_ready = (
            s.one("scales"), s.one("up_rounded"), s.one("product"), s.two("sig_raw"), s.two("o_step"), s.one("magic_ready"))
        down_made, down_kept, turned, residual = s.two("down_made"), s.two("down_kept"), s.two("turned"), s.two("residual")
        ps = t["ps"]

        def sb(name, shape):
            return ctx.enter_context(nc.sbuf_tensor("l0f_" + name, shape, F32))

        up, gate = sb("up", [P, C * NTOK]), sb("gate", [P, C * NTOK])
        up3, gate3 = up[:].rearrange("p (c n) -> p c n", c=C), gate[:].rearrange("p (c n) -> p c n", c=C)
        wraw, wT, wscale, winv = sb("wraw", [P, 3 * C * P]), sb("wT", [P, 3 * C * P]), sb("wscale", [P, NW]), sb("winv", [P, NW])
        qs = sb("qs", [P, 32])
        maxes = sb("maxes", [P, 2 * NBLK])
        magic = sb("magic", [P, 1])
        sig = t["xc"]
        block = ctx.enter_context(nc.Block())

        @block.sync
        def _(sp):
            sp.dma_start(wraw[:], d["l0f_W"]).then_inc(loads, 16)

        @block.vector
        def _(v):
            step = Chain(v, steps)

            def scale_of(k):
                c = qs[:, 4 * k:4 * k + 4]
                v.wait_ge(all_max, k + 1)
                step(v.tensor_scalar(c[:, 2:3], c[:, 1:2], 1.0 / 32767.0, 1e-12, ALU.mult, ALU.max))
                v.reciprocal(c[:, 3:4], c[:, 2:3]).then_inc(scales, 1)
                v.wait_ge(scales, k + 1)
                return c[:, 2:3], c[:, 3:4]

            def quantise(a, k, done):
                scale, inv = scale_of(k)
                step(v.tensor_scalar(a, a, inv, MAGIC, ALU.mult, ALU.add))
                v.tensor_scalar(a, a, MAGIC, scale, ALU.subtract, ALU.mult).then_inc(done, 1)

            v.tensor_reduce(qs[:, 0:1], t["xnT"][:], X, ALU.max, apply_absolute_value=True).then_inc(own_max, 1)
            v.wait_ge(loads, 16)
            w3 = wraw[:].rearrange("p (b i) -> p b i", i=WB)
            sc3 = wscale[:].unsqueeze(2).broadcast_to([P, NW, WB])
            step(v.tensor_reduce(wscale[:], w3, X, ALU.max, apply_absolute_value=True))
            step(v.tensor_scalar(wscale[:], wscale[:], 1.0 / 7.0, 1e-12, ALU.mult, ALU.max))
            step(v.reciprocal(winv[:], wscale[:]))
            step(v.tensor_tensor(w3, w3, winv[:].unsqueeze(2).broadcast_to([P, NW, WB]), ALU.mult))
            step(v.tensor_scalar(wraw[:], wraw[:], MAGIC, MAGIC, ALU.add, ALU.subtract))
            v.tensor_tensor(w3, w3, sc3, ALU.mult).then_inc(wq_ready, 1)
            quantise(t["xnT"][:], 0, x_ready)
            with v.Fori(0, NBLK) as j:
                v.wait_ge(up_kept, j + 1)
                v.tensor_reduce(maxes[:, bass.ds(j, 1)], up3[:, :, bass.ds(j * BLK, BLK)], mybir.AxisListType.XY, ALU.max, apply_absolute_value=True).then_inc(sig_step[0], 1)
                v.wait_ge(gate_kept, j + 1)
                v.tensor_reduce(maxes[:, bass.ds(j + NBLK, 1)], gate3[:, :, bass.ds(j * BLK, BLK)], mybir.AxisListType.XY, ALU.max, apply_absolute_value=True).then_inc(sig_step[0], 1)
            v.wait_ge(sig_step[0], 2 * NBLK)
            v.tensor_reduce(qs[:, 4:5], maxes[:, 0:NBLK], X, ALU.max).then_inc(own_max, 1)
            v.tensor_reduce(qs[:, 8:9], maxes[:, NBLK:2 * NBLK], X, ALU.max).then_inc(own_max, 1)
            up_scale, _ = scale_of(1)
            quantise(gate[:], 2, gate_ready)
            for c in range(C):
                v.wait_ge(up_rounded, c + 1)
                part = up[:, c * NTOK:(c + 1) * NTOK]
                v.tensor_scalar(part, part, MAGIC, up_scale, ALU.subtract, ALU.mult).then_inc(up_ready, 1)
            v.wait_ge(gate_ready, 1)
            for n in range(NQ):
                p = n % 2
                half, part = sig[:, p * QCH:(p + 1) * QCH], gate[:, n * QCH:(n + 1) * QCH]
                v.wait_ge(sig_ready[p], n // 2 + 1)
                step(v.tensor_scalar(half, half, MAGIC + 65535.0, MAGIC, ALU.min, ALU.subtract))
                v.scalar_tensor_tensor(part, half, 1.0 / 65536.0, part, ALU.mult, ALU.mult).then_inc(sig_used[p], 1)
            v.wait_ge(sig_used[0], NQ // 2)
            v.wait_ge(sig_used[1], NQ // 2)
            v.tensor_reduce(qs[:, 12:13], gate[:], X, ALU.max, apply_absolute_value=True).then_inc(own_max, 1)
            quantise(gate[:], 3, gate_ready)
            v.wait_ge(gate_ready, 2)
            v.wait_ge(up_ready, C)
            own = C * NTOK - POOL_COLS
            v.tensor_tensor(gate[:, 0:own], gate[:, 0:own], up[:, 0:own], ALU.mult).then_inc(product, 1)
            v.wait_ge(product, 2)
            v.tensor_reduce(qs[:, 16:17], gate[:], X, ALU.max, apply_absolute_value=True).then_inc(own_max, 1)
            scale, inv = scale_of(4)

            def quantise_block(j, p):
                cols = gate3[:, :, bass.ds((2 * j + p) * BLK, BLK)]
                v.tensor_scalar(cols, cols, inv, MAGIC, ALU.mult, ALU.add).then_inc(o_step[p], 1)
                v.wait_ge(o_step[p], j + 1)
                v.tensor_scalar(cols, cols, MAGIC, scale, ALU.subtract, ALU.mult).then_inc(o_ready[p], 1)

            def add(j, p):
                v.wait_ge(turned[p], j + 1)
                xb = t["x"][:, bass.ds((2 * j + p) * BLK, BLK)]
                v.scalar_tensor_tensor(xb, ps[:, 2 + p, :], t["gate"][:, gate_at:gate_at + 1], xb, ALU.mult, ALU.add).then_inc(residual[p], 1)

            for p in range(2):
                quantise_block(0, p)
            with v.Fori(0, NBLK // 2 - 1) as j:
                for p in range(2):
                    quantise_block(j + 1, p)
                for p in range(2):
                    add(j, p)
            for p in range(2):
                add(NBLK // 2 - 1, p)

        @block.gpsimd
        def _(pool):
            pool.memset(magic[:], MAGIC).then_inc(magic_ready, 1)
            for k in range(5):
                pool.wait_ge(own_max, {0: 1, 1: 3, 2: 3, 3: 4, 4: 5}[k])
                pool.partition_all_reduce(qs[:, 4 * k + 1:4 * k + 2], qs[:, 4 * k:4 * k + 1], P, RMAX).then_inc(all_max, 1)
                if k == 3:
                    pool.wait_ge(gate_ready, 2)
                    pool.wait_ge(up_ready, C)
                    part = slice(C * NTOK - POOL_COLS, C * NTOK)
                    pool.tensor_tensor(gate[:, part], gate[:, part], up[:, part], ALU.mult).then_inc(product, 1)

        @block.scalar
        def _(sc):
            for b in range(3):
                sc.wait_ge(w_turned, b + 1)
                sc.activation(wT[:, b * C * P:(b + 1) * C * P], ps[:, b, 0:C * P], ACT.Copy).then_inc(w_kept, 1)
            with sc.Fori(0, NBLK) as j:
                sc.wait_ge(up_made, j + 1)
                sc.activation(up3[:, :, bass.ds(j * BLK, BLK)], ps[:, 0:3, :], ACT.Copy).then_inc(up_kept, 1)
                sc.wait_ge(gate_made, j + 1)
                sc.activation(gate3[:, :, bass.ds(j * BLK, BLK)], ps[:, 3:6, :], ACT.Copy).then_inc(gate_kept, 1)
            sc.wait_ge(magic_ready, 1)
            sc.wait_ge(scales, 2)
            for c in range(C):
                part = up[:, c * NTOK:(c + 1) * NTOK]
                sc.activation(part, part, ACT.Identity, scale=qs[:, 7:8], bias=magic[:]).then_inc(up_rounded, 1)
            sc.wait_ge(gate_ready, 1)
            for n in range(NQ):
                p = n % 2
                if n >= 2:
                    sc.wait_ge(sig_used[p], n // 2)
                sc.activation(sig[:, p * QCH:(p + 1) * QCH], gate[:, n * QCH:(n + 1) * QCH], ACT.Sigmoid).then_inc(sig_raw[p], 1)
                sc.wait_ge(sig_raw[p], n // 2 + 1)
                sc.activation(sig[:, p * QCH:(p + 1) * QCH], sig[:, p * QCH:(p + 1) * QCH], ACT.Identity, scale=65536.0, bias=magic[:]).then_inc(sig_ready[p], 1)
            with sc.Fori(0, NBLK // 2) as j:
                for p in range(2):
                    sc.wait_ge(down_made[p], j + 1)
                    sc.wait_ge(turned[p], j)
                    sc.activation(t["stage"][p][:], ps[:, p, :], ACT.Copy).then_inc(down_kept[p], 1)

        @block.tensor
        def _(pe):
            pe.wait_ge(wq_ready, 1)
            for b in range(3):
                for i in range(C):
                    ins = pe.transpose(ps[:, b, i * P:(i + 1) * P], wraw[:, (b * C + i) * P:(b * C + i + 1) * P], t["ident"][:])
                ins.then_inc(w_turned, 1)
            pe.wait_ge(w_kept, 3)
            pe.wait_ge(x_ready, 1)
            with pe.Fori(0, NBLK) as j:
                xb = t["xnT"][:, bass.ds(j * BLK, BLK)]
                for which, made, kept in ((0, up_made, up_kept), (1, gate_made, gate_kept)):
                    pe.wait_ge(kept, j)
                    for c in range(C):
                        ins = pe.matmul(ps[:, 3 * which + c, :], wT[:, (which * C + c) * P:(which * C + c + 1) * P], xb, start=True, stop=True)
                    ins.then_inc(made, 1)
            with pe.Fori(0, NBLK // 2) as j:
                for p in range(2):
                    pe.wait_ge(o_ready[p], j + 1)
                    pe.wait_ge(down_kept[p], j)
                    for c in range(C):
                        ins = pe.matmul(ps[:, p, :], wT[:, (2 * C + c) * P:(2 * C + c + 1) * P], gate3[:, c, bass.ds((2 * j + p) * BLK, BLK)],
                                        start=(c == 0), stop=(c == C - 1))
                    ins.then_inc(down_made[p], 1)
                for p in range(2):
                    pe.wait_ge(down_kept[p], j + 1)
                    pe.wait_ge(residual[p], j)
                    for i in range(TB):
                        ins = pe.transpose(ps[:, 2 + p, i * P:(i + 1) * P], t["stage"][p][:, i * P:(i + 1) * P], t["ident"][:])
                    ins.then_inc(turned[p], 1)


def dense_ffn(nc, t, d, stage, C, kind, gate_at):
    sine = kind == "sine"
    nin = 1 if sine else 2
    width = (nin + 1) * C * P + (C if sine else 0)
    with ExitStack() as ctx:
        s = Sems(nc, ctx, stage)
        loads = s.one("loads")

        def each(name):
            return [s.one(f"{name}{c}") for c in range(C)]

        made, acted, rounded, angled, sined, combined = (each(n) for n in ("made", "acted", "rounded", "angled", "sined", "combined"))
        done = each("done") if sine else combined
        down_made, residual = s.two("down_made"), s.two("residual")
        ps = t["ps"]

        def sb(name, shape):
            return ctx.enter_context(nc.sbuf_tensor(f"{stage}_sb_{name}", shape, F32))

        w, b2 = sb("w", [P, width]), sb("b2", [1, D])
        h = [sb(f"h{p}", [P, C, BLK]) for p in range(2)]
        ga = [sb(f"ga{c}", [P, BLK]) for c in range(C)]
        sn = [sb(f"sn{c}", [P, BLK]) for c in range(C)]
        block = ctx.enter_context(nc.Block())
        PAIRS = NBLK // 2

        def bank(c, i=0):
            return ps[:, nin * c + i, :]

        def skip(j, p, c):
            pass

        def run(eng, first, second, third, after):
            def pair(j, last):
                for p in range(2):
                    for c in range(C):
                        for ahead, step in ((2, first), (1, second), (0, third)):
                            k = p * C + c + ahead
                            if k < 2 * C:
                                step(j, k // C, k % C)
                            elif not last:
                                step(j + 1, 0, k % C)
                    after(j, p)
            first(0, 0, 0)
            first(0, 0, 1)
            second(0, 0, 0)
            pair(0, False)
            with eng.Fori(1, PAIRS - 1) as j:
                pair(j, False)
            pair(PAIRS - 1, True)

        @block.sync
        def _(sp):
            sp.dma_start(w[:], d[f"{stage}_W"][0, :, :]).then_inc(loads, 16)
            if sine:
                sp.dma_start(b2[:], d[f"{stage}_b2"]).then_inc(loads, 16)

        n_loads = 16 * (1 + sine)

        @block.tensor
        def _(pe):
            pe.wait_ge(loads, n_loads)

            def up(j, p):
                xb = t["xnT"][:, bass.ds((2 * j + p) * BLK, BLK)]
                for c in range(C):
                    if not isinstance(j, int) or j + p > 0:
                        pe.wait_ge(combined[c], 2 * j + p)
                    for i in range(nin):
                        ins = pe.matmul(bank(c, i), w[:, (i * C + c) * P:(i * C + c + 1) * P], xb, start=True, stop=True)
                    ins.then_inc(made[c], 1)

            def down(j, p):
                for c in range(C):
                    pe.wait_ge(done[c], 2 * j + p + 1)
                pe.wait_ge(residual[p], j)
                for i in range(TB):
                    dst = ps[:, 4 + p, i * P:(i + 1) * P]
                    for c in range(C):
                        ins = pe.matmul(dst, h[p][:, c, i * P:(i + 1) * P], w[:, (nin * C + c) * P:(nin * C + c + 1) * P],
                                        start=(c == 0), stop=(c == C - 1 and not sine))
                    if sine:
                        ins = pe.matmul(dst, t["ones"][0:1, 0:P], b2[:], start=False, stop=True)
                ins.then_inc(down_made[p], 1)

            up(0, 0)
            with pe.Fori(0, PAIRS - 1) as j:
                for p in range(2):
                    up(j + p, 1 - p)
                    down(j, p)
            up(PAIRS - 1, 1)
            down(PAIRS - 1, 0)
            down(PAIRS - 1, 1)

        @block.scalar
        def _(sc):
            sc.wait_ge(loads, n_loads)

            def begin(j, p, c):
                sc.wait_ge(made[c], 2 * j + p + 1)
                sc.wait_ge(done[c], 2 * j + p)
                if sine:
                    sc.activation(ga[c][:], bank(c), ACT.Identity, scale=0.1 * INV_2PI, bias=t["phase"][:, c:c + 1]).then_inc(acted[c], 1)
                else:
                    sc.activation(ga[c][:], bank(c), ACT.Gelu).then_inc(acted[c], 1)

            def take_sine(j, p, c):
                sc.wait_ge(angled[c], 2 * j + p + 1)
                sc.activation(sn[c][:], sn[c][:], ACT.Sin, scale=TWO_PI).then_inc(sined[c], 1)

            def relu(j, p, c):
                sc.wait_ge(combined[c], 2 * j + p + 1)
                sc.wait_ge(down_made[p], j)
                b1 = w[:, width - C + c:width - C + c + 1]
                sc.activation(h[p][:, c, :], ga[c][:], ACT.Relu, bias=b1).then_inc(done[c], 1)

            run(sc, begin, take_sine if sine else skip, relu if sine else skip, lambda j, p: None)

        @block.vector
        def _(v):
            def angle(j, p, c):
                v.wait_ge(acted[c], 2 * j + p + 1)
                v.wait_ge(combined[c], 2 * j + p)
                v.tensor_scalar(sn[c][:], ga[c][:], MAGIC, MAGIC, ALU.add, ALU.subtract).then_inc(rounded[c], 1)
                v.wait_ge(rounded[c], 2 * j + p + 1)
                v.tensor_tensor(sn[c][:], ga[c][:], sn[c][:], ALU.subtract).then_inc(angled[c], 1)

            def combine(j, p, c):
                if sine:
                    v.wait_ge(sined[c], 2 * j + p + 1)
                    v.scalar_tensor_tensor(ga[c][:], sn[c][:], t["amp"][:, c:c + 1], bank(c), ALU.mult, ALU.add).then_inc(combined[c], 1)
                else:
                    v.wait_ge(acted[c], 2 * j + p + 1)
                    v.wait_ge(down_made[p], j)
                    v.tensor_tensor(h[p][:, c, :], ga[c][:], bank(c, 1), ALU.mult).then_inc(combined[c], 1)

            def add(j, p):
                v.wait_ge(down_made[p], j + 1)
                xb = t["x"][:, bass.ds((2 * j + p) * BLK, BLK)]
                v.scalar_tensor_tensor(xb, ps[:, 4 + p, :], t["gate"][:, gate_at:gate_at + 1], xb, ALU.mult, ALU.add).then_inc(residual[p], 1)

            def add_before(j, p):
                if p == 1:
                    add(j, 0)
                elif not isinstance(j, int) or j > 0:
                    add(j - 1, 1)

            run(v, angle if sine else skip, combine, skip, add_before)
            add(PAIRS - 1, 1)


def route_scores(nc, t, d, stage, E, norm):
    with ExitStack() as ctx:
        s = Sems(nc, ctx, stage + "r")
        loads, steps, sq_ready, norm_ready, vec_ready, vec_turned, vec_kept = (
            s.one("loads"), s.one("steps"), s.one("sq_ready"), s.one("norm_ready"), s.one("vec_ready"), s.one("vec_turned"), s.one("vec_kept"))
        projected, kept, squared, made, out = s.two("projected"), s.two("kept"), s.two("squared"), s.two("made"), s.two("out")
        sums_ready, norms_ready, reset_step = s.one("sums_ready"), s.one("norms_ready"), s.one("reset_step")
        ps, w = t["ps"], t["wstat"]
        M = E + norm
        G = w[:, 128:128 + E]
        raw = ctx.enter_context(nc.sbuf_tensor(stage + "_route_raw", [P, NT, M], F32))
        sqs = [ctx.enter_context(nc.sbuf_tensor(f"{stage}_route_sq{p}", [P, BLK], F32)) for p in range(2)]
        vec = ctx.enter_context(nc.sbuf_tensor(stage + "_route_vec", [E, P], F32))
        vsq = ctx.enter_context(nc.sbuf_tensor(stage + "_route_vsq", [E, P], F32))
        vn = ctx.enter_context(nc.sbuf_tensor(stage + "_route_vn", [E, 1], F32))
        temp = ctx.enter_context(nc.sbuf_tensor(stage + "_route_temp", [P, 2], F32))
        norms = t["small"][:, 0:NT]
        block = ctx.enter_context(nc.Block())

        @block.sync
        def _(sp):
            if norm:
                sp.dma_start(w[:, 0:128], d[f"{stage}_proj"]).then_inc(loads, 16)
                sp.dma_start(vec[:], d[f"{stage}_vec"]).then_inc(loads, 16)
                sp.dma_start(temp[:, 0:1], d[f"{stage}_temp"].partition_broadcast(P)).then_inc(loads, 16)
            else:
                sp.dma_start(G, d[f"{stage}_G"]).then_inc(loads, 16)

        n_loads = 48 if norm else 16

        @block.tensor
        def _(pe):
            pe.wait_ge(loads, n_loads)
            if norm:
                pe.wait_ge(vec_ready, 1)
                pe.transpose(ps[:, 6, 0:E], vec[:], t["ident"][0:E, 0:E]).then_inc(vec_turned, 1)
                pe.wait_ge(vec_kept, 1)
            with pe.Fori(0, NBLK // 2) as j:
                if norm:
                    for p in range(2):
                        pe.wait_ge(squared[p], j)
                        pe.wait_ge(kept[p], j)
                        pe.matmul(ps[:, p, :], w[:, 0:128], t["xnT"][:, bass.ds((2 * j + p) * BLK, BLK)], start=True, stop=True).then_inc(projected[p], 1)
                for p in range(2):
                    pe.wait_ge(kept[p], j + 1)
                    if norm:
                        pe.wait_ge(squared[p], j + 1)
                    pe.wait_ge(out[p], j)
                    for i in range(TB):
                        ins = pe.matmul(ps[:, 2 + p, i * M:i * M + E], t["stage"][p][:, i * P:(i + 1) * P], G, start=True, stop=True)
                        if norm:
                            ins = pe.matmul(ps[:, 2 + p, i * M + E:i * M + M], sqs[p][:, i * P:(i + 1) * P], t["ones"][:, 0:1], start=True, stop=True)
                    ins.then_inc(made[p], 1)

        @block.scalar
        def _(sc):
            with sc.Fori(0, NBLK // 2) as j:
                for p in range(2):
                    if norm:
                        sc.wait_ge(projected[p], j + 1)
                        src = ps[:, p, :]
                    else:
                        src = t["xnT"][:, bass.ds((2 * j + p) * BLK, BLK)]
                    sc.wait_ge(made[p], j)
                    sc.activation(t["stage"][p][:], src, ACT.Copy).then_inc(kept[p], 1)
                    if norm:
                        sc.activation(sqs[p][:], src, ACT.Square).then_inc(squared[p], 1)

        @block.gpsimd
        def _(pool):
            pool.memset(t["reset"][:], 1.0).then_inc(reset_step, 1)
            pool.wait_ge(reset_step, 1)
            pool.memset(t["reset"][:, :, 0:1], 0.0)
            if norm:
                pool.wait_ge(sq_ready, 1)
                pool.tensor_tensor(vn[:], vn[:], t["plus_half"][0:E, 0:1], ALU.pow).then_inc(norm_ready, 1)
                pool.wait_ge(sums_ready, 1)
                pool.tensor_tensor(norms, norms, t["plus_half"][:], ALU.pow).then_inc(norms_ready, 1)

        @block.vector
        def _(v):
            step = Chain(v, steps)
            if norm:
                v.wait_ge(loads, n_loads)
                step(v.tensor_tensor(vsq[:], vec[:], vec[:], ALU.mult))
                v.tensor_reduce(vn[:], vsq[:], X, ALU.add).then_inc(sq_ready, 1)
                v.wait_ge(norm_ready, 1)
                step(v.tensor_scalar(vn[:], vn[:], 1e-12, None, ALU.max))
                step(v.reciprocal(vn[:], vn[:]))
                step(v.reciprocal(temp[:, 1:2], temp[:, 0:1]))
                v.tensor_scalar(vec[:], vec[:], vn[:], None, ALU.mult).then_inc(vec_ready, 1)
                v.wait_ge(vec_turned, 1)
                v.tensor_copy(G, ps[:, 6, 0:E]).then_inc(vec_kept, 1)
            with v.Fori(0, NBLK // 2) as j:
                for p in range(2):
                    v.wait_ge(made[p], j + 1)
                    v.tensor_copy(raw[:, bass.ds((2 * j + p) * TB, TB), :], ps[:, 2 + p, 0:TB * M].rearrange("p (i m) -> p i m", m=M)).then_inc(out[p], 1)
            v.wait_ge(out[0], NBLK // 2)
            v.wait_ge(out[1], NBLK // 2)
            if norm:
                v.tensor_copy(norms, raw[:, :, E]).then_inc(sums_ready, 1)
                v.wait_ge(norms_ready, 1)
                step(v.tensor_scalar(norms, norms, 1e-12, None, ALU.max))
                step(v.reciprocal(norms, norms))
                step(v.tensor_scalar(norms, norms, temp[:, 1:2], None, ALU.mult))
                v.tensor_tensor(t["scores"][:, :, 0:E], raw[:, :, 0:E], norms.unsqueeze(2).broadcast_to([P, NT, E]), ALU.mult)
            else:
                v.tensor_copy(t["scores"][:, :, 0:E], raw[:, :, 0:E])


def top_two(nc, t, E, gate_at):
    with ExitStack() as ctx:
        s = Sems(nc, ctx, "top2")
        steps, rank_ready, shifted, exp_ready = s.one("steps"), s.one("rank_ready"), s.one("shifted"), s.one("exp_ready")

        def sb(name, shape):
            return ctx.enter_context(nc.sbuf_tensor("top2_" + name, shape, F32))

        rank, work, best = (sb(n, [P, NT, E]) for n in ("rank", "work", "best"))
        one, two = t["hots"]
        v1, v2, first, p1, p2 = (sb(n, [P, NT]) for n in ("v1", "v2", "first", "p1", "p2"))
        sc_ = t["scores"][:, :, 0:E]
        wide = lambda a: a[:].unsqueeze(2).broadcast_to([P, NT, E])
        block = ctx.enter_context(nc.Block())

        @block.gpsimd
        def _(pool):
            pool.iota(rank[:], pattern=[[0, NT], [-1, E]], base=E, channel_multiplier=0, allow_small_or_imprecise_dtypes=True).then_inc(rank_ready, 1)

        @block.vector
        def _(v):
            step = Chain(v, steps)

            def pick(a, top, hot):
                step(v.tensor_reduce(top[:], a, X, ALU.max))
                step(v.tensor_tensor(work[:], a, wide(top), ALU.is_equal))
                step(v.tensor_tensor(work[:], work[:], rank[:], ALU.mult))
                step(v.tensor_reduce(first[:], work[:], X, ALU.max))
                step(v.tensor_tensor(hot[:], rank[:], wide(first), ALU.is_equal))

            v.wait_ge(rank_ready, 1)
            pick(sc_, v1, one)
            step(v.scalar_tensor_tensor(best[:], one[:], -1e30, sc_, ALU.mult, ALU.add))
            pick(best[:], v2, two)
            v.tensor_tensor(p2[:], v2[:], v1[:], ALU.subtract).then_inc(shifted, 1)
            v.wait_ge(exp_ready, 1)
            step(v.tensor_scalar(p1[:], p2[:], 1.0, None, ALU.add))
            step(v.reciprocal(p1[:], p1[:]))
            step(v.tensor_scalar(p1[:], p1[:], t["gate"][:, gate_at:gate_at + 1], None, ALU.mult))
            step(v.tensor_tensor(p2[:], p2[:], p1[:], ALU.mult))
            step(v.tensor_tensor(t["sel"][:].rearrange("p e n -> p n e"), one[:], two[:], ALU.add))
            step(v.tensor_tensor(work[:], one[:], wide(p1), ALU.mult))
            step(v.tensor_tensor(best[:], two[:], wide(p2), ALU.mult))
            step(v.tensor_tensor(t["comb"][:, 0:E, :].rearrange("p e n -> p n e"), work[:], best[:], ALU.add))

        @block.scalar
        def _(sc):
            sc.wait_ge(shifted, 1)
            sc.activation(p2[:], p2[:], ACT.Exp).then_inc(exp_ready, 1)


def top_tokens(nc, t, E, K, gate_at):
    BITS = 30
    STEPS = BITS // 2
    UNROLL = 3
    SEG = NT * E // P
    assert P // E == HD
    with ExitStack() as ctx:
        s = Sems(nc, ctx, "topk")
        steps, shifted, exp_ready, loop_steps, counted, summed = (
            s.one("steps"), s.one("shifted"), s.one("exp_ready"), s.one("loop_steps"), s.one("counted"), s.one("summed"))
        start_steps, probs_ready, seg_turned, found, stored, loaded = (
            s.one("start_steps"), s.one("probs_ready"), s.one("seg_turned"), s.one("found"), s.one("stored"), s.one("loaded"))

        def sb(name, shape, dt=F32):
            return ctx.enter_context(nc.sbuf_tensor("topk_" + name, shape, dt))

        tri, reset, sel = t["tri"], t["reset"], t["sel"]
        score, work, before = (sb(n, [P, E, NT]) for n in ("score", "work", "before"))
        top, total = sb("top", [P, NT]), sb("total", [P, NT])
        seg_score = sb("seg_score", [P, SEG, P])
        thr, inc = sb("thr", [P, 1], I32), sb("inc", [P, 1], I32)
        cand, nexti = sb("cand", [P, 3], I32), sb("nexti", [P, 3], I32)
        bits, nextbits, seg_count, reached = sb("bits", [P, 3]), sb("nextbits", [P, 3]), sb("seg_count", [P, 3]), sb("reached", [P, 4])
        junk = [sb(f"junk{k}", [P, SEG * P]) for k in range(3)]
        limits = sb("limits", [P, P], I32)
        limits_dram = nc.dram_tensor("topk_limits_bounce", (P,), I32).ap()
        count, enough = sb("count", [P, E]), sb("enough", [P, E])
        ps = t["ps"]
        raw = t["scores"][:, :, 0:E]
        by_tile = lambda a: a[:].rearrange("p e n -> p n e")
        over_e = lambda a: a[:].unsqueeze(2).broadcast_to([P, NT, E])
        over_n = lambda a: a.unsqueeze(2).broadcast_to([P, E, NT])
        block = ctx.enter_context(nc.Block())
        LOOP = 7

        @block.gpsimd
        def _(pool):
            step = Chain(pool, start_steps)
            step(pool.memset(thr[:], 0))
            for k in range(3):
                step(pool.memset(bits[:, k:k + 1], float((k + 1) * 2 ** (BITS - 2))))
                step(pool.memset(cand[:, k:k + 1], (k + 1) * 2 ** (BITS - 2)))

        @block.sync
        def _(sp):
            sp.wait_ge(found, 1)
            sp.dma_start(limits_dram.rearrange("(p o) -> p o", o=1), thr[:]).then_inc(stored, 16)
            sp.wait_ge(stored, 16)
            sp.dma_start(limits[:], limits_dram.partition_broadcast(P)).then_inc(loaded, 16)

        @block.scalar
        def _(sc):
            sc.wait_ge(shifted, 1)
            sc.activation(score[:], score[:], ACT.Exp).then_inc(exp_ready, 1)

        @block.tensor
        def _(pe):
            pe.wait_ge(probs_ready, 1)
            segs = score[:].rearrange("p e (s i) -> p (e s) i", i=SEG)
            for i in range(SEG):
                ins = pe.transpose(ps[:, 3, i * P:(i + 1) * P], segs[:, :, i], t["ident"][:])
            ins.then_inc(seg_turned, 1)
            with pe.Fori(0, STEPS) as j:
                pe.wait_ge(counted, 3 * j + 3)
                pe.matmul(ps[:, 0, 0:3], t["blockones"][:], seg_count[:], start=True, stop=True).then_inc(summed, 1)
            pe.wait_ge(counted, 3 * STEPS + 1)
            pe.matmul(ps[:, 0, 0:E], t["ones"][:], count[:], start=True, stop=True).then_inc(summed, 1)
            flat = work[:].rearrange("p e n -> p (e n)")
            pe.wait_ge(counted, 3 * STEPS + 2)
            pe.matmul(ps[:, 1, :], tri[:], flat, start=True, stop=True).then_inc(summed, 1)
            pe.matmul(ps[:, 2, :], t["ones"][:], flat, start=True, stop=True).then_inc(summed, 1)

        @block.vector
        def _(v):
            step = Chain(v, steps)
            step(v.tensor_reduce(top[:], raw, X, ALU.max))
            v.tensor_tensor(by_tile(score), raw, over_e(top), ALU.subtract).then_inc(shifted, 1)
            v.wait_ge(exp_ready, 1)
            step(v.tensor_reduce(total[:], by_tile(score), X, ALU.add))
            step(v.reciprocal(total[:], total[:]))
            v.tensor_tensor(by_tile(score), by_tile(score), over_e(total), ALU.mult).then_inc(probs_ready, 1)
            v.wait_ge(seg_turned, 1)
            step(v.tensor_copy(seg_score[:], ps[:, 3, :].rearrange("p (i q) -> p i q", q=P)))
            v.wait_ge(start_steps, 7)
            with v.Fori(0, STEPS // UNROLL) as jj:
                for j in (jj * UNROLL + i for i in range(UNROLL)):
                    def did(ins, n):
                        ins.then_inc(loop_steps, 1)
                        v.wait_ge(loop_steps, j * LOOP + n)

                    for k in range(3):
                        v.tensor_scalar(junk[k][:], seg_score[:].rearrange("p i q -> p (i q)"), cand[:, k:k + 1].bitcast(F32), None,
                                        ALU.is_ge, ALU.add, accum_out=seg_count[:, k:k + 1]).then_inc(counted, 1)
                    did(v.tensor_scalar(nextbits[:], bits[:], 0.25, None, ALU.mult), 1)
                    did(v.tensor_copy(nexti[:], nextbits[:]), 2)
                    v.wait_ge(summed, j + 1)
                    did(v.tensor_scalar(reached[:, 0:3], ps[:, 0, 0:3], float(K) * E / P, None, ALU.is_ge, ALU.add, accum_out=reached[:, 3:4]), 3)
                    did(v.tensor_scalar(inc[:], reached[:, 3:4], bits[:, 0:1], None, ALU.mult), 4)
                    did(v.tensor_tensor(thr[:], thr[:], inc[:], ALU.bitwise_or), 5)
                    did(v.tensor_tensor(cand[:], thr[:].broadcast_to([P, 3]), nexti[:], ALU.bitwise_or), 6)
                    did(v.tensor_copy(bits[:], nextbits[:]), 7)
            v.tensor_copy(inc[:], thr[:]).then_inc(found, 1)
            v.wait_ge(loaded, 16)
            limit = over_n(limits[:].bitcast(F32).rearrange("p (e s) -> p e s", e=E)[:, :, 0])
            step(v.tensor_tensor(sel[:], score[:], limit, ALU.is_gt))
            v.tensor_reduce(count[:], sel[:], X, ALU.add).then_inc(counted, 1)
            v.wait_ge(counted, 3 * STEPS + 1)
            v.tensor_tensor(work[:], score[:], limit, ALU.is_equal).then_inc(counted, 1)
            v.wait_ge(summed, STEPS + 1)
            step(v.tensor_scalar(enough[:], ps[:, 0, 0:E], -1.0, float(K), ALU.mult, ALU.add))
            v.wait_ge(summed, STEPS + 3)
            flat = lambda a: a[:].rearrange("p e n -> p (e n)")
            step(v.tensor_tensor_scan(flat(before), flat(reset), ps[:, 2, :], 0.0, ALU.mult, ALU.add))
            step(v.tensor_tensor(flat(before), flat(before), ps[:, 2, :], ALU.subtract))
            step(v.tensor_tensor(flat(before), flat(before), ps[:, 1, :], ALU.add))
            step(v.tensor_tensor(before[:], before[:], over_n(enough[:]), ALU.is_lt))
            step(v.tensor_tensor(before[:], before[:], work[:], ALU.mult))
            step(v.tensor_tensor(sel[:], sel[:], before[:], ALU.add))
            step(v.tensor_tensor(score[:], sel[:], score[:], ALU.mult))
            step(v.tensor_scalar(t["comb"][:, 0:E, :], score[:], t["gate"][:, gate_at:gate_at + 1], None, ALU.mult))


def slot_lists(nc, u, stage, E, NG, two_choices):
    NHI = NG * TB if two_choices else TB
    CH = NT
    NC = 2 if two_choices else E
    with ExitStack() as ctx:
        s = Sems(nc, ctx, stage + "slots")
        steps, sums, iotas, lo_ready, hi_ready, hot_used, listed, hot_step, taken = (
            s.one("steps"), s.one("sums"), s.one("iotas"), s.two("lo_ready"), s.two("hi_ready"), s.two("hot_used"),
            s.two("listed"), s.two("hot_step"), s.two("taken"))
        table_ready = s.one("table_ready")
        rows_ready, stored = s.one("rows_ready"), s.one("stored")

        def sb(name, shape, dt=F32):
            return ctx.enter_context(nc.sbuf_tensor(f"{stage}_slots_{name}", shape, dt))

        rows, zero = sb("rows", [P, NT, D + E]), sb("zero", [P, D + E])
        rank = sb("rank", [P, E, NT])
        lo, hi, tile = sb("lo", [P, NC * CH]), sb("hi", [P, NC * CH]), sb("tile", [P, CH])
        iota_lo, iota_hi, iota_e, iota_g = sb("iota_lo", [P, P]), sb("iota_hi", [P, NHI]), sb("iota_e", [P, E]), sb("iota_g", [P, NG])
        token, spare_row = sb("token", [P, 1]), sb("spare_row", [P, NG * TB])
        lo_hot = [sb(f"lo_hot{p}", [P, P, CH], BF16) for p in range(2)]
        lo_table, lo_16 = sb("lo_table", [P, P, CH], BF16), sb("lo_16", [P, NC * CH], BF16)
        hi_hot = [sb(f"hi_hot{p}", [P, CH, NHI]) for p in range(2)]
        hi_num = [sb(f"hi_num{p}", [P, CH, 2, NHI], BF16) for p in range(2)]
        nums = sb("nums", [P, NG * TB, 2])
        slot, none = sb("slot", [P, NG * TB]), sb("none", [P, NG * TB])
        if two_choices:
            groups, first, ones_e = sb("groups", [P, E]), sb("first", [P, E]), sb("ones_e", [P, E])
            begun = sb("begun", [P, NG, E + 1])
            picked = sb("picked", [P, NT, E])
            eid = sb("eid", [P, NG])
        ps = u["ps"]
        sel = u["sel"]
        flat = lambda a: a[:].rearrange("p e n -> p (e n)")
        W = E * NT
        block = ctx.enter_context(nc.Block())
        wide = dict(channel_multiplier=0, allow_small_or_imprecise_dtypes=True)

        @block.gpsimd
        def _(pool):
            step = Chain(pool, iotas)
            step(pool.memset(zero[:], 0.0))
            step(pool.iota(iota_lo[:], pattern=[[1, P]], base=0, **wide))
            step(pool.iota(iota_hi[:], pattern=[[1, NHI]], base=0, **wide))
            step(pool.iota(iota_e[:], pattern=[[1, E]], base=0, **wide))
            step(pool.iota(iota_g[:], pattern=[[1, NG]], base=0, **wide))
            step(pool.iota(tile[:], pattern=[[1, CH]], base=0, **wide))
            step(pool.iota(token[:], pattern=[[0, 1]], base=1, channel_multiplier=1, allow_small_or_imprecise_dtypes=True))
            step(pool.iota(spare_row[:], pattern=[[0, NG], [P, TB]], base=NTOK + 1, channel_multiplier=1, allow_small_or_imprecise_dtypes=True))

        @block.sync
        def _(sp):
            by_tile = lambda a: a.rearrange("(n p) f -> p n f", p=P)
            sp.wait_ge(iotas, 1)
            sp.dma_start(by_tile(u["sum_rows"]), zero[:, 0:D].unsqueeze(1).broadcast_to([P, NT + TB, D])).then_inc(stored, 16)
            sp.dma_start(by_tile(u["rows"][NTOK:NTOK + BLK, :]), zero[:].unsqueeze(1).broadcast_to([P, TB, D + E])).then_inc(stored, 16)
            sp.wait_ge(rows_ready, 2)
            sp.dma_start(by_tile(u["rows"][0:NTOK, :]), rows[:]).then_inc(stored, 16)
            sp.wait_ge(stored, 48)

        @block.scalar
        def _(sc):
            sc.activation(rows[:, :, D:D + E], u["comb"][:].rearrange("p e n -> p n e"), ACT.Copy).then_inc(rows_ready, 1)
            sc.wait_ge(iotas, 2)
            sc.activation(lo_table[:], iota_lo[:].unsqueeze(2).broadcast_to([P, P, CH]), ACT.Copy).then_inc(table_ready, 1)

        @block.tensor
        def _(pe):
            pe.matmul(ps[:, 1, 0:W], u["tri"][:], flat(sel), start=True, stop=True).then_inc(sums, 1)
            pe.matmul(ps[:, 2, 0:W], u["ones"][:], flat(sel), start=True, stop=True).then_inc(sums, 1)

            def product(j, p, first, last):
                pe.wait_ge(lo_ready[p], j + 1)
                pe.wait_ge(hi_ready[p], 2 * j + 2)
                if not two_choices:
                    pe.wait_ge(taken[p], j)
                bank = 4 if two_choices else 4 + p
                for i in range(CH):
                    ins = pe.matmul(ps[:, bank, 0:2 * NHI], lo_hot[p][:, :, i], hi_num[p][:, i, :, :].rearrange("p k h -> p (k h)"),
                                    start=(first and i == 0), stop=(last and i == CH - 1))
                ins.then_inc(listed[p], 1)

            if two_choices:
                product(0, 0, True, False)
                product(0, 1, False, True)
            else:
                with pe.Fori(0, NC // 2) as j:
                    for p in range(2):
                        product(j, p, True, True)

        @block.vector
        def _(v):
            step = Chain(v, steps)
            rstd = u["small"][:, 2 * NT:3 * NT]
            v.tensor_tensor(rows[:, :, 0:D], u["xc"][:].rearrange("p (n d) -> p n d", d=D),
                            rstd.unsqueeze(2).broadcast_to([P, NT, D]), ALU.mult).then_inc(rows_ready, 1)
            v.wait_ge(sums, 2)
            step(v.tensor_tensor_scan(flat(rank), flat(u["reset"]), ps[:, 2, 0:W], 0.0, ALU.mult, ALU.add))
            if two_choices:
                v.wait_ge(iotas, 8)
                step(v.tensor_scalar(groups[:], rank[:, :, NT - 1], 1.0 / BLK, (BLK - 1.0) / BLK - 0.5 + 0.5 / BLK, ALU.mult, ALU.add))
                step(v.tensor_scalar(groups[:], groups[:], MAGIC, MAGIC, ALU.add, ALU.subtract))
                step(v.memset(ones_e[:], 1.0))
                step(v.tensor_tensor_scan(first[:], ones_e[:], groups[:], 0.0, ALU.mult, ALU.add))
                step(v.tensor_tensor(first[:], first[:], groups[:], ALU.subtract))
                step(v.memset(begun[:], 0.0))
                step(v.tensor_tensor(begun[:, :, 0:E], iota_g[:].unsqueeze(2).broadcast_to([P, NG, E]),
                                     first[:].unsqueeze(1).broadcast_to([P, NG, E]), ALU.is_ge))
                step(v.tensor_tensor(u["of_expert"][:], begun[:, :, 0:E], begun[:, :, 1:E + 1], ALU.subtract))
                step(v.tensor_tensor(begun[:, :, 0:E], u["of_expert"][:], iota_e[:].unsqueeze(1).broadcast_to([P, NG, E]), ALU.mult))
                step(v.tensor_reduce(eid[:], begun[:, :, 0:E], X, ALU.add))
                step(v.tensor_copy(u["expert_of"][:], eid[:]))
            step(v.tensor_tensor(flat(rank), flat(rank), ps[:, 2, 0:W], ALU.subtract))
            step(v.tensor_tensor(flat(rank), flat(rank), ps[:, 1, 0:W], ALU.add))
            if two_choices:
                step(v.scalar_tensor_tensor(rank[:], first[:].unsqueeze(2).broadcast_to([P, E, NT]), float(BLK), rank[:], ALU.mult, ALU.add))
                for c, hot in enumerate(u["hots"]):
                    step(v.tensor_tensor(picked[:], hot[:], rank[:].rearrange("p e n -> p n e"), ALU.mult))
                    step(v.tensor_reduce(lo[:, c * NT:(c + 1) * NT], picked[:], X, ALU.add))
            else:
                v.wait_ge(iotas, 8)
                step(v.tensor_tensor(u["of_expert"][:], iota_g[:].unsqueeze(2).broadcast_to([P, NG, E]),
                                     iota_e[:].unsqueeze(1).broadcast_to([P, NG, E]), ALU.is_equal))
                step(v.tensor_copy(lo[:], flat(rank)))
            step(v.tensor_scalar(hi[:], lo[:], 1.0 / P, -0.5 + 0.5 / P, ALU.mult, ALU.add))
            step(v.tensor_scalar(hi[:], hi[:], MAGIC, MAGIC, ALU.add, ALU.subtract))
            step(v.scalar_tensor_tensor(lo_16[:], hi[:], -float(P), lo[:], ALU.mult, ALU.add))
            if not two_choices:
                step(v.scalar_tensor_tensor(hi[:], hi[:], 1.0, flat(sel), ALU.add, ALU.mult))
                step(v.tensor_scalar(hi[:], hi[:], -1.0, None, ALU.add))

            v.wait_ge(table_ready, 1)

            def chunk(j, p):
                at = bass.ds((2 * j + p) * CH, CH)
                v.wait_ge(listed[p], j)
                v.tensor_tensor(lo_hot[p][:], lo_table[:], lo_16[:, at].unsqueeze(1).broadcast_to([P, P, CH]), ALU.is_equal).then_inc(lo_ready[p], 1)
                v.tensor_tensor(hi_hot[p][:], iota_hi[:].unsqueeze(1).broadcast_to([P, CH, NHI]),
                                hi[:, at].unsqueeze(2).broadcast_to([P, CH, NHI]), ALU.is_equal).then_inc(hot_step[p], 1)
                v.wait_ge(hot_step[p], j + 1)
                v.tensor_scalar(hi_num[p][:, :, 0, :], hi_hot[p][:], token[:], None, ALU.mult).then_inc(hi_ready[p], 1)
                v.tensor_tensor(hi_num[p][:, :, 1, :], hi_hot[p][:], tile[:].unsqueeze(2).broadcast_to([P, CH, NHI]), ALU.mult).then_inc(hi_ready[p], 1)

            def take(j, p):
                v.wait_ge(listed[p], j + 1)
                at = bass.ds((2 * j + p) * NHI, NHI) if not two_choices else slice(0, NHI)
                bank = 4 if two_choices else 4 + p
                v.tensor_copy(nums[:, at, :].rearrange("p h k -> p k h"), ps[:, bank, 0:2 * NHI].rearrange("p (k h) -> p k h", k=2)).then_inc(taken[p], 1)

            if two_choices:
                chunk(0, 0)
                chunk(0, 1)
                take(0, 1)
                v.wait_ge(taken[1], 1)
            else:
                chunk(0, 0)
                with v.Fori(0, NC // 2 - 1) as j:
                    chunk(j, 1)
                    take(j, 0)
                    chunk(j + 1, 0)
                    take(j, 1)
                chunk(NC // 2 - 1, 1)
                take(NC // 2 - 1, 0)
                take(NC // 2 - 1, 1)
                v.wait_ge(taken[0], NC // 2)
                v.wait_ge(taken[1], NC // 2)
            step(v.scalar_tensor_tensor(slot[:], nums[:, :, 1], float(P), nums[:, :, 0], ALU.mult, ALU.add))
            step(v.scalar_tensor_tensor(none[:], slot[:], 0.0, spare_row[:], ALU.is_equal, ALU.mult))
            step(v.scalar_tensor_tensor(slot[:], slot[:], -1.0, none[:], ALU.add, ALU.add))
            step(v.tensor_copy(u["slots"][:, 0:NG * TB], slot[:]))
            v.memset(u["slots"][:, NG * TB:], 0)


def gathered_experts(nc, u, d, stage, E, NG, C, kind, bias1=False, bias2=False):
    nin = 2 if kind == "glu" else 1
    width = (nin + 1) * C * P + (C if bias1 else 0) + (D if bias2 else 0)
    HB = C // 2
    RW = D + E
    chosen = "expert_of" in u
    with ExitStack() as ctx:
        s = Sems(nc, ctx, stage)
        w_came, x_came, x_turned, x_kept, weighed, w_step = (
            s.two("w_came"), s.two("x_came"), s.two("x_turned"), s.two("x_kept"), s.two("weighed"), s.two("w_step"))
        gi_ready, si_ready, spare_step = s.two("gi_ready"), s.two("si_ready"), s.one("spare_step")
        load_step, add_step = s.two("load_step"), s.two("add_step")
        made, acted, h_ready, down_made, y_ready, added = (
            s.two("made"), s.two("acted"), s.two("h_ready"), s.two("down_made"), s.two("y_ready"), s.two("added"))
        back = [s.one(f"back{q}") for q in range(4)]
        ps = u["ps"]

        def sb2(name, shape, dt=F32):
            return [ctx.enter_context(nc.sbuf_tensor(f"{stage}_g_{name}{p}", shape, dt)) for p in range(2)]

        wb, xg, xgT, h, ga = sb2("w", [P, width]), sb2("xg", [P, TB, RW]), sb2("xgT", [P, BLK]), sb2("h", [P, C, BLK]), sb2("ga", [P, BLK])
        wmul, wsel, y = sb2("wmul", [P, TB, E]), sb2("wsel", [P, TB]), sb2("y", [P, TB, D])
        gi, si, for_load, for_add, zero = sb2("gi", [P, TB], I32), sb2("si", [P, TB], I32), sb2("for_load", [P, 1]), sb2("for_add", [P, 1]), sb2("zero", [P, 1])[0]
        block = ctx.enter_context(nc.Block())

        def at(g):
            return g // 2, g % 2

        def run(eng, turn, up, down, start=None):
            turn(0, 0)
            with eng.Fori(0, (NG - 1) // 2) as j:
                for p in range(2):
                    up(j, p)
                    turn(j + p, 1 - p)
                    down(j, p)
            for g in range((NG - 1) // 2 * 2, NG):
                up(*at(g))
                if g + 1 < NG:
                    turn(*at(g + 1))
                down(*at(g))

        def chunk_free(eng, j, p, c):
            if c >= 2:
                eng.wait_ge(h_ready[p], j * C + c - 1)
            elif p == 1:
                eng.wait_ge(h_ready[0], j * C + C - 1 + c)
            else:
                eng.wait_ge(h_ready[1], j * C)

        def group(j, p):
            return bass.ds(2 * j + p, 1)

        @block.gpsimd
        def _(pool):
            def load_rows(j, p):
                pool.wait_ge(x_turned[p], j)
                pool.wait_ge(weighed[p], j)
                pool.wait_ge(gi_ready[p], j + 1)
                pool.wait_ge(load_step[p], j)
                pool.tensor_tensor(for_load[p][:], zero[:], zero[:], ALU.add).then_inc(load_step[p], 1)
                for i in range(TB):
                    pool.indirect_dma_start(out=xg[p][:, i, :], out_offset=None, in_=u["rows"],
                                            in_offset=bass.IndirectOffsetOnAxis(ap=gi[p][:, i:i + 1], axis=0)).then_inc(x_came[p], 16)

            def add_rows(j, p):
                pool.wait_ge(si_ready[p], j + 1)
                pool.wait_ge(y_ready[p], j + 1)
                pool.wait_ge(added[p], 16 * TB * j)
                pool.wait_ge(added[1 - p], 16 * TB * (j + p))
                pool.wait_ge(add_step[p], j)
                pool.tensor_tensor(for_add[p][:], zero[:], zero[:], ALU.add).then_inc(add_step[p], 1)
                for i in range(TB):
                    pool.indirect_dma_start(out=u["sum_rows"], out_offset=bass.IndirectOffsetOnAxis(ap=si[p][:, i:i + 1], axis=0),
                                            in_=y[p][:, i, :], in_offset=None, compute_op=ALU.add).then_inc(added[p], 16)

            pool.memset(zero[:], 0.0).then_inc(spare_step, 1)
            pool.wait_ge(spare_step, 1)
            for p in range(2):
                load_rows(0, p)
            with pool.Fori(0, NG // 2 - 1) as j:
                for p in range(2):
                    load_rows(j + 1, p)
                    add_rows(j, p)
            for g in range(NG // 2 * 2 - 2, NG):
                if g + 2 < NG:
                    load_rows(*at(g + 2))
                add_rows(*at(g))

        @block.sync
        def _(sp):
            def load_weights(j, p):
                e = sp.value_load(u["expert_of"][0:1, group(j, p)], min_val=0, max_val=E - 1) if chosen else 2 * j + p
                sp.wait_ge(down_made[p], j)
                sp.dma_start(wb[p][:], d[f"{stage}_W"][bass.ds(e, 1), :, :].rearrange("e p n -> (e p) n")).then_inc(w_came[p], 16)

            with sp.Fori(0, NG // 2) as j:
                for p in range(2):
                    load_weights(j, p)
            if NG % 2:
                load_weights(NG // 2, 0)
            sp.wait_ge(added[0], 16 * TB * ((NG + 1) // 2))
            sp.wait_ge(added[1], 16 * TB * (NG // 2))
            sums = u["sum_rows"][0:NTOK, :].rearrange("(n p) f -> p n f", p=P)
            for q in range(4):
                tiles = slice(q * NT // 4, (q + 1) * NT // 4)
                sp.dma_start(u["xc"][:].rearrange("p (n d) -> p n d", d=D)[:, tiles, :], sums[:, tiles, :]).then_inc(back[q], 16)

        @block.tensor
        def _(pe):
            def turn(j, p):
                pe.wait_ge(x_came[p], 16 * TB * (j + 1))
                pe.wait_ge(x_kept[p], j)
                for i in range(TB):
                    ins = pe.transpose(ps[:, 6 + p, i * P:(i + 1) * P], xg[p][:, i, 0:D], u["ident"][:])
                ins.then_inc(x_turned[p], 1)

            def up(j, p):
                pe.wait_ge(x_kept[p], j + 1)
                pe.wait_ge(w_came[p], 16 * (j + 1))
                for c in range(C):
                    b = c % 2
                    chunk_free(pe, j, p, c)
                    for i in range(nin):
                        ins = pe.matmul(ps[:, 2 * b + i, :], wb[p][:, (i * C + c) * P:(i * C + c + 1) * P], xgT[p][:], start=True, stop=True)
                    ins.then_inc(made[b], 1)

            def down(j, p):
                pe.wait_ge(h_ready[p], (j + 1) * C)
                pe.wait_ge(y_ready[p], j)
                for i in range(TB):
                    dst = ps[:, 4 + p, i * P:(i + 1) * P]
                    for c in range(C):
                        ins = pe.matmul(dst, h[p][:, c, i * P:(i + 1) * P], wb[p][:, (nin * C + c) * P:(nin * C + c + 1) * P],
                                        start=(c == 0), stop=(c == C - 1 and not bias2))
                    if bias2:
                        ins = pe.matmul(dst, u["ones"][0:1, 0:P], wb[p][0:1, width - D:width], start=False, stop=True)
                ins.then_inc(down_made[p], 1)

            run(pe, turn, up, down)

        @block.scalar
        def _(sc):
            def turn(j, p):
                sc.wait_ge(x_turned[p], j + 1)
                sc.activation(xgT[p][:], ps[:, 6 + p, :], ACT.Copy).then_inc(x_kept[p], 1)

            def up(j, p):
                n = (2 * j + p) * HB
                sc.wait_ge(w_came[p], 16 * (j + 1))
                for c in range(C):
                    b = c % 2
                    sc.wait_ge(made[b], n + c // 2 + 1)
                    if kind == "glu":
                        chunk_free(sc, j, p, c)
                        sc.activation(ga[b][:], ps[:, 2 * b, :], ACT.Gelu).then_inc(acted[b], 1)
                    else:
                        at_b1 = (nin + 1) * C * P + c
                        sc.wait_ge(down_made[p], j)
                        sc.activation(h[p][:, c, :], ps[:, 2 * b, :], ACT.Gelu, bias=wb[p][:, at_b1:at_b1 + 1]).then_inc(h_ready[p], 1)

            run(sc, turn, up, lambda j, p: None)

        @block.vector
        def _(v):
            def copy_rows(j, p):
                v.wait_ge(x_came[p], 16 * TB * j)
                v.tensor_copy(gi[p][:], u["slots"][:, bass.ds((2 * j + p) * TB, TB)]).then_inc(gi_ready[p], 1)

            def turn(j, p):
                v.wait_ge(x_came[p], 16 * TB * (j + 1))
                if not isinstance(j, int) or 2 * j + p + 2 < NG:
                    copy_rows(j + 1, p)
                v.wait_ge(w_step[p], j)
                v.tensor_tensor(wmul[p][:], xg[p][:, :, D:D + E], u["of_expert"][:, group(j, p), :].broadcast_to([P, TB, E]), ALU.mult).then_inc(w_step[p], 1)
                v.wait_ge(w_step[p], j + 1)
                v.wait_ge(y_ready[p], j)
                v.tensor_reduce(wsel[p][:], wmul[p][:], X, ALU.add).then_inc(weighed[p], 1)

            def up(j, p):
                n = (2 * j + p) * HB
                if kind == "glu":
                    for c in range(C):
                        b = c % 2
                        v.wait_ge(acted[b], n + c // 2 + 1)
                        v.wait_ge(down_made[p], j)
                        v.tensor_tensor(h[p][:, c, :], ga[b][:], ps[:, 2 * b + 1, :], ALU.mult).then_inc(h_ready[p], 1)

            def down(j, p):
                v.wait_ge(down_made[p], j + 1)
                v.wait_ge(weighed[p], j + 1)
                v.wait_ge(added[p], 16 * TB * j)
                v.tensor_copy(si[p][:], u["slots"][:, bass.ds((2 * j + p) * TB, TB)]).then_inc(si_ready[p], 1)
                v.tensor_tensor(y[p][:], ps[:, 4 + p, :].rearrange("p (i d) -> p i d", d=D),
                                wsel[p][:].unsqueeze(2).broadcast_to([P, TB, D]), ALU.mult).then_inc(y_ready[p], 1)

            for p in range(2):
                copy_rows(0, p)
            run(v, turn, up, down)
            for q in range(4):
                cols = slice(q * NT * D // 4, (q + 1) * NT * D // 4)
                v.wait_ge(back[q], 16)
                v.tensor_tensor(u["x"][:, cols], u["x"][:, cols], u["xc"][:, cols], ALU.add)


def sine_constants(nc, t, d, C=4):
    with ExitStack() as ctx:
        s = Sems(nc, ctx, "phase")
        loads, steps, angles, sines = s.one("loads"), s.one("steps"), s.one("angles"), s.one("sines")

        def sb(name, n):
            return ctx.enter_context(nc.sbuf_tensor("phase_" + name, [P, n], F32))

        inp, turns, whole, sc2, tmp = sb("inp", 4 * C), sb("turns", 2 * C), sb("whole", 2 * C), sb("sc2", 2 * C), sb("tmp", C)
        theta, wr, wi, b1 = (inp[:, k * C:(k + 1) * C] for k in range(4))
        block = ctx.enter_context(nc.Block())

        @block.sync
        def _(sp):
            sp.dma_start(inp[:], d["l2f_phase"]).then_inc(loads, 16)

        @block.vector
        def _(v):
            step = Chain(v, steps)
            v.wait_ge(loads, 16)
            step(v.tensor_scalar(turns[:, 0:C], theta, INV_2PI, None, ALU.mult))
            step(v.tensor_scalar(turns[:, C:2 * C], turns[:, 0:C], 0.25, None, ALU.add))
            step(v.tensor_scalar(whole[:], turns[:], MAGIC, MAGIC, ALU.add, ALU.subtract))
            k0 = whole[:, 0:C]
            step(v.scalar_tensor_tensor(tmp[:], k0, -6.28125, theta, ALU.mult, ALU.add))
            step(v.scalar_tensor_tensor(tmp[:], k0, -0.0019350051879882812, tmp[:], ALU.mult, ALU.add))
            step(v.scalar_tensor_tensor(tmp[:], k0, -3.019916050561733e-07, tmp[:], ALU.mult, ALU.add))
            step(v.tensor_scalar(turns[:, 0:C], tmp[:], INV_2PI, None, ALU.mult))
            step(v.tensor_scalar(turns[:, C:2 * C], turns[:, 0:C], 0.25, None, ALU.add))
            step(v.scalar_tensor_tensor(t["phase"][:], b1, 0.1 * INV_2PI, turns[:, 0:C], ALU.mult, ALU.add))
            step(v.tensor_scalar(whole[:], turns[:], MAGIC, MAGIC, ALU.add, ALU.subtract))
            v.tensor_tensor(turns[:], turns[:], whole[:], ALU.subtract).then_inc(angles, 1)
            v.wait_ge(sines, 1)
            step(v.tensor_tensor(tmp[:], sc2[:, 0:C], wi, ALU.mult))
            step(v.tensor_tensor(sc2[:, C:2 * C], sc2[:, C:2 * C], wr, ALU.mult))
            step(v.tensor_tensor(tmp[:], tmp[:], sc2[:, C:2 * C], ALU.add))
            step(v.scalar_tensor_tensor(t["amp"][:], tmp[:], 0.1, wi, ALU.mult, ALU.mult))

        @block.scalar
        def _(sc):
            sc.wait_ge(angles, 1)
            sc.activation(sc2[:], turns[:], ACT.Sin, scale=TWO_PI).then_inc(sines, 1)



def build(nc, d, out, stages=range(8)):
    with ExitStack() as ctx:
        t = {}

        def sb(name, shape, dt=F32):
            t[name] = ctx.enter_context(nc.sbuf_tensor(f"sb_{name}", shape, dt))

        def sb2(name, shape, dt=F32):
            t[name] = [ctx.enter_context(nc.sbuf_tensor(f"sb_{name}{p}", shape, dt)) for p in range(2)]

        sb("x", [P, NT * D])
        sb("xc", [P, NT * D])
        sb("xnT", [P, NTOK])
        sb("ctxT", [P, NT * KEYS])
        sb("graw", [P, 8])
        sb("gate", [P, 8])
        sb("ident", [P, P])
        sb("identb", [P, P], BF16)
        sb("ones", [P, P])
        sb("eps_ln", [P, 1])
        sb("tri", [P, P])
        sb("plus_half", [P, 32])
        sb("headmask", [P, HEADS])
        sb("blockones", [P, P])
        sb("onespad", [KEYS, HG, 32])
        sb("small", [P, 256])
        sb("eps", [P, 1])
        sb("phase", [P, 4])
        sb("amp", [P, 4])
        sb("row_any", [P, NT])
        sb("wstat", [P, 512])
        sb("cols", [P, 16])
        sb("row", [1, 2 * D])
        sb2("stage", [P, BLK])
        sb2("Vpad", [KEYS, HEADS, 32])
        sb2("maski", [P, 8 * KEYS], I32)
        sb("maskf", [P, 8 * KEYS])
        sb2("maskb", [P, KEYS], BF16)
        t["ps"] = ctx.enter_context(nc.psum_tensor("ps", [P, 8, 512], F32))

        def attention_stage(*a, **k):
            with ExitStack() as own:
                u = dict(t)
                for name, shape in (("qk", [P, P + KEYS]), ("kblk", [P, HEADS * KEYS]), ("prob", [P, HEADS, KEYS]),
                                    ("pt", [KEYS, HG, GROUPS, P]), ("oT", [P, P]), ("rden", [P, HEADS]), ("rowmax", [P, HEADS]),
                                    ("rowsum", [P, HEADS])):
                    u[name] = [own.enter_context(nc.sbuf_tensor(f"{a[0]}_{name}{p}", shape, F32)) for p in range(2)]
                attention(nc, u, d, *a, **k)

        def routed(stage, E, NG, gate_at, select, norm, *a, two_choices=False, **kw):
            with ExitStack() as own:
                u = dict(t)

                def sb(name, shape, dt=F32):
                    return own.enter_context(nc.sbuf_tensor(f"{stage}_route_{name}", shape, dt))

                u["scores"], u["comb"], u["sel"], u["reset"] = sb("scores", [P, NT, E]), sb("comb", [P, E, NT]), sb("sel", [P, E, NT]), sb("reset", [P, E, NT])
                u["slots"], u["of_expert"] = sb("slots", [P, (NG + 2) * TB], I32), sb("of_expert", [P, NG, E])
                if two_choices:
                    u["hots"] = [sb("one", [P, NT, E]), sb("two", [P, NT, E])]
                    u["expert_of"] = sb("expert_of", [P, NG], I32)
                u["rows"] = nc.dram_tensor(stage + "_rows", (NTOK + BLK, D + E), F32).ap()
                u["sum_rows"] = nc.dram_tensor(stage + "_sum_rows", (NTOK + BLK, D), F32).ap()
                route_scores(nc, u, d, stage, E, norm)
                select(u)
                slot_lists(nc, u, stage, E, NG, two_choices)
                gathered_experts(nc, u, d, stage, E, NG, *a, **kw)

        constants(nc, t, d)
        if 0 in stages:
            layernorm(nc, t, "ln0")
            concat_linear(nc, t, d)
        if 1 in stages:
            layernorm(nc, t, "ln1")
            quantised_ffn(nc, t, d, 4)
        if 2 in stages:
            layernorm(nc, t, "ln2")
            attention_stage("l1x", 1, bias_qk=True, bias_v=True, bias_out=True)
        if 3 in stages:
            layernorm(nc, t, "ln3")
            routed("l1f", 8, (2 * NTOK + 8 * (BLK - 1)) // BLK, 5, lambda u: top_two(nc, u, 8, 5), True, 4, "gelu", two_choices=True, bias1=True, bias2=True)
        if 4 in stages:
            layernorm(nc, t, "ln4")
            with ExitStack() as own:
                t["kT"] = own.enter_context(nc.sbuf_tensor("sb_kT", [P, NT * KEYS], F32))
                rms_qk(nc, t, d, "l2x")
                attention_stage("l2x", 2, ready_qk=True)
        if 5 in stages:
            layernorm(nc, t, "ln5")
            sine_constants(nc, t, d)
            dense_ffn(nc, t, d, "l2f", 4, "sine", 6)
        if 6 in stages:
            mask_rows(nc, t, d)
            layernorm(nc, t, "ln6", row_any=t["row_any"][:])
            attention_stage("l3x", 3, bias_out=True, masked=True)
        if 7 in stages:
            layernorm(nc, t, "ln7")
            routed("l3f", 16, 16, 7, lambda u: top_tokens(nc, u, 16, BLK, 7), False, 4, "glu")
            dense_ffn(nc, t, d, "l3s", 2, "glu", 7)
        with ExitStack() as c2:
            stored = c2.enter_context(nc.semaphore("stored"))
            block = c2.enter_context(nc.Block())

            @block.sync
            def _(sp):
                sp.dma_start(out, t["x"][:]).then_inc(stored, 16)
                sp.wait_ge(stored, 16)


def laid_out(i):
    import numpy as np
    a = {k: np.asarray(v) for k, v in i.items()}
    f = {}
    f["x"] = a["x"].transpose(1, 0, 2).reshape(P, NT * D)
    f["ctxT"] = a["ctx_1024"].transpose(2, 0, 1).reshape(D, NT * KEYS)
    f["mask"] = a["mask_BxSxS2_if1"].transpose(1, 0, 2).reshape(P, NT * KEYS)
    f["g_xattn"], f["g_ffn"] = a["g_xattn"], a["g_ffn"]
    f["l0_WT"] = a["L0_xattn_W"].T.reshape(2, D, D).transpose(1, 0, 2).reshape(D, 2 * D)
    f["l0_b"] = a["L0_xattn_b"][None]
    w, b = a["L1_xattn_in_proj_weight"], a["L1_xattn_in_proj_bias"]
    f["l1x_W"] = np.concatenate([w.T, a["L1_xattn_out_w"].T], 1)
    f["l1x_bqk"] = b[:2 * D].reshape(2, D).T
    f["l1x_bv"], f["l1x_bo"] = b[None, 2 * D:], a["L1_xattn_out_b"][None]
    f["l2x_W"] = np.concatenate([a["L2_xattn_Wq"], a["L2_xattn_Wkv"], a["L2_xattn_Wproj"]], 1)
    f["l2x_gamma"] = np.stack([np.tile(a["L2_xattn_q_gamma"], HEADS), np.tile(a["L2_xattn_k_gamma"], HEADS)], 1)
    f["l3x_W"] = np.concatenate([a[f"L3_xattn_W{c}"].T for c in "qkvo"], 1)
    f["l3x_bo"] = a["L3_xattn_bo"][None]
    def rows(w):
        E, F, _ = w.shape
        return w.reshape(E, F // P, P, D).transpose(0, 2, 1, 3).reshape(E, P, F // P * D)

    def column(b):
        E, F = b.shape
        return b.reshape(E, F // P, P).transpose(0, 2, 1)

    up, gate, down = a["L0_ffn_w_up"], a["L0_ffn_w_gate"], a["L0_ffn_w_down"]
    f["l0f_W"] = np.concatenate([rows(up[None])[0], rows(gate[None])[0], down], 1)
    f["l1f_proj"], f["l1f_vec"], f["l1f_temp"] = a["L1_ffn_Wp"].T, a["L1_ffn_sim_matrix"], a["L1_ffn_temperature"].reshape(1)
    b2 = np.broadcast_to(a["L1_ffn_b2"][:, None], (8, P, D))
    f["l1f_W"] = np.concatenate([a["L1_ffn_W1"], rows(a["L1_ffn_W2"]), column(a["L1_ffn_b1"]), b2], 2)
    f["l2f_W"] = np.concatenate([a["L2_ffn_W1"][None], rows(a["L2_ffn_W2"][None]), column(a["L2_ffn_b1"][None])], 2)
    f["l2f_b2"] = a["L2_ffn_b2"][None]
    f["l2f_phase"] = np.concatenate([column(a[f"L2_ffn_{n}"][None])[0] for n in ("quantum_phases", "quantum_weights_real", "quantum_weights_imag", "b1")], 1)
    f["l3f_G"] = a["L3_ffn_gate_w"].T
    turn = lambda w: w.transpose(0, 2, 1)
    f["l3f_W"] = np.concatenate([turn(a["L3_ffn_Wg"]), turn(a["L3_ffn_Wu"]), rows(turn(a["L3_ffn_Wd"]))], 2)
    f["l3s_W"] = np.concatenate([turn(a["L3_ffn_Sg"][None]), turn(a["L3_ffn_Su"][None]), rows(turn(a["L3_ffn_Sd"][None]))], 2)
    return {k: np.ascontiguousarray(v) for k, v in f.items()}


def kernel(**inputs):
    import concourse.bacc as bacc
    from concourse.bass_utils import run_bass_kernel_spmd

    nc = bacc.Bacc("TRN2", target_bir_lowering=False, num_devices=1)
    arrays = laid_out(inputs)
    d = {k: nc.dram_tensor(k, v.shape, mybir.dt.from_np(v.dtype), kind="ExternalInput").ap() for k, v in arrays.items()}
    out = nc.dram_tensor("out", (P, NT * D), F32, kind="ExternalOutput").ap()
    build(nc, d, out)
    r = run_bass_kernel_spmd(nc, [arrays], core_ids=[0]).results[0]["out"]
    return r.reshape(P, NT, D).transpose(1, 0, 2)
```
